# Optimizing a Trainium2 kernel written in Bass

```python
import numpy as np
import jax
import jax.numpy as jnp

def _softmax(x, axis=-1):
    return jax.nn.softmax(x, axis=axis)

def _gelu(x):
    return jax.nn.gelu(x, approximate=True)

def _silu(x):
    return jax.nn.silu(x)

def _sigmoid(x):
    return jax.nn.sigmoid(x)

def _layernorm(x, axis=-1, eps=1e-05):
    m = jnp.mean(x, axis=axis, keepdims=True)
    v = jnp.var(x, axis=axis, keepdims=True)
    return (x - m) / jnp.sqrt(v + eps)

def _scatter_add(tgt, idx, src, axis=0):
    return tgt.at[idx].add(src)

def _segment_sum(src, seg, n):
    return jax.ops.segment_sum(src, seg, n)
kernel_name = 'mk_vit_tower_cls_d1_tok_img512_r4_1a79b3'

def setup_inputs(seed: int=0):
    np.random.seed(seed)
    _w = jnp.asarray

    def _rec_inputs():
        import jax
        import jax.numpy as jnp
        _rk = jax.random.key(seed)
        x = -0.000178447 + 0.99995 * jax.random.normal(jax.random.fold_in(_rk, 1), (128, 3, 176, 208), jnp.float32)
        cls_tok = 0.02 * jax.random.normal(jax.random.fold_in(_rk, 5), (1, 1, 128), jnp.float32)
        return (x, cls_tok)
    x, cls_tok = _rec_inputs()

    def _L0_tok_setup():
        import jax, jax.numpy as jnp
        import numpy as np
        P1, P2, C = (16, 16, 3)
        PW, PH = (176 // P1, 208 // P2)
        key = jax.random.key(seed)
        k1, k2, k3, k4, k5 = jax.random.split(key, 5)
        B, D = (64, 128)
        patch_dim = P1 * P2 * C
        return {'x': jax.random.normal(k1, (B, C, PW * P1, PH * P2), dtype=jnp.float32), 'W': jax.random.normal(k2, (D, patch_dim), dtype=jnp.float32) * 0.02, 'b': jax.random.normal(k3, (D,), dtype=jnp.float32) * 0.02, 'cls_token': jax.random.uniform(k4, (1, 1, D), dtype=jnp.float32), 'pos_emb': jax.random.normal(k5, (1, PW * PH + 1, 1), dtype=jnp.float32)}
    _L0_tok_all = _L0_tok_setup()
    _L0_tok_in = {k: v for k, v in _L0_tok_all.items() if k in ('W', 'b', 'cls_token', 'pos_emb')}
    del _L0_tok_all

    def _L0_attn_setup():
        import jax, jax.numpy as jnp
        import numpy as np
        N_LAYERS = 2
        D = 128
        N = 16
        O = 128
        B = 4
        L = 512
        LN_EPS = 1e-05

        def _combine(e1, e2):
            a1, u1 = e1
            a2, u2 = e2
            return (a1 * a2, a2 * u1 + u2)
        key = jax.random.key(seed)
        ks = jax.random.split(key, 10)
        s = D ** (-0.5)
        inp = {'x': jax.random.normal(ks[0], (B, L, D), jnp.float32), 'A_log': jax.random.normal(ks[1], (N_LAYERS, D, N), jnp.float32) * 0.5, 'W_B': jax.random.normal(ks[2], (N_LAYERS, D, N), jnp.float32) * s, 'b_B': jnp.zeros((N_LAYERS, N), jnp.float32), 'W_C': jax.random.normal(ks[3], (N_LAYERS, D, N), jnp.float32) * s, 'b_C': jnp.zeros((N_LAYERS, N), jnp.float32), 'W_dt': jax.random.normal(ks[4], (N_LAYERS, D, D), jnp.float32) * s, 'b_dt': jnp.zeros((N_LAYERS, D), jnp.float32), 'D_skip': jnp.ones((N_LAYERS, D), jnp.float32), 'W_mix': jax.random.normal(ks[5], (N_LAYERS, D, D), jnp.float32) * s, 'b_mix': jnp.zeros((N_LAYERS, D), jnp.float32), 'ln_g': jnp.ones((N_LAYERS, D), jnp.float32), 'ln_b': jnp.zeros((N_LAYERS, D), jnp.float32), 'W_dec': jax.random.normal(ks[6], (D, O), jnp.float32) * s, 'b_dec': jnp.zeros((O,), jnp.float32)}
        return inp
    _L0_attn_all = _L0_attn_setup()
    _L0_attn_in = {k: v for k, v in _L0_attn_all.items() if k in ('A_log', 'W_B', 'b_B', 'W_C', 'b_C', 'W_dt', 'b_dt', 'D_skip', 'W_mix', 'b_mix', 'ln_g', 'ln_b', 'W_dec', 'b_dec')}
    del _L0_attn_all

    def _L0_ffn_setup():
        import jax, jax.numpy as jnp
        import numpy as np
        B, S, D, H, E = (4, 512, 128, 8, 8)
        FF = 4 * D
        HD = D // H
        EPS = 1e-05

        def _layernorm(x, g, b):
            mu = jnp.mean(x, axis=-1, keepdims=True)
            var = jnp.mean((x - mu) ** 2, axis=-1, keepdims=True)
            return (x - mu) * jax.lax.rsqrt(var + EPS) * g + b
        key = jax.random.key(seed)
        ks = jax.random.split(key, 16)
        s = 0.02
        return {'x': jax.random.normal(ks[0], (B, S, D), dtype=jnp.float32), 'ln1_g': jnp.ones((D,), jnp.float32), 'ln1_b': jnp.zeros((D,), jnp.float32), 'Wq': jax.random.normal(ks[1], (D, D), jnp.float32) * s, 'bq': jnp.zeros((D,), jnp.float32), 'Wk': jax.random.normal(ks[2], (D, D), jnp.float32) * s, 'bk': jnp.zeros((D,), jnp.float32), 'Wv': jax.random.normal(ks[3], (D, D), jnp.float32) * s, 'bv': jnp.zeros((D,), jnp.float32), 'Wo': jax.random.normal(ks[4], (D, D), jnp.float32) * s, 'bo': jnp.zeros((D,), jnp.float32), 'gate_W': jax.random.normal(ks[5], (D, E), jnp.float32) * s, 'gate_b': jnp.zeros((E,), jnp.float32), 'W1': jax.random.normal(ks[6], (E, D, FF), jnp.float32) * s, 'b1': jnp.zeros((E, FF), jnp.float32), 'W2': jax.random.normal(ks[7], (E, FF, D), jnp.float32) * s, 'b2': jnp.zeros((E, D), jnp.float32)}
    _L0_ffn_all = _L0_ffn_setup()
    _L0_ffn_in = {k: v for k, v in _L0_ffn_all.items() if k in ('ln1_g', 'ln1_b', 'Wq', 'bq', 'Wk', 'bk', 'Wv', 'bv', 'Wo', 'bo', 'gate_W', 'gate_b', 'W1', 'b1', 'W2', 'b2')}
    del _L0_ffn_all
    return {'x': x, 'cls_tok': cls_tok, 'L0_tok_W': _L0_tok_in['W'], 'L0_tok_b': _L0_tok_in['b'], 'L0_tok_cls_token': _L0_tok_in['cls_token'], 'L0_tok_pos_emb': _L0_tok_in['pos_emb'], 'L0_attn_A_log': _L0_attn_in['A_log'], 'L0_attn_W_B': _L0_attn_in['W_B'], 'L0_attn_b_B': _L0_attn_in['b_B'], 'L0_attn_W_C': _L0_attn_in['W_C'], 'L0_attn_b_C': _L0_attn_in['b_C'], 'L0_attn_W_dt': _L0_attn_in['W_dt'], 'L0_attn_b_dt': _L0_attn_in['b_dt'], 'L0_attn_D_skip': _L0_attn_in['D_skip'], 'L0_attn_W_mix': _L0_attn_in['W_mix'], 'L0_attn_b_mix': _L0_attn_in['b_mix'], 'L0_attn_ln_g': _L0_attn_in['ln_g'], 'L0_attn_ln_b': _L0_attn_in['ln_b'], 'L0_attn_W_dec': _L0_attn_in['W_dec'], 'L0_attn_b_dec': _L0_attn_in['b_dec'], 'L0_ffn_ln1_g': _L0_ffn_in['ln1_g'], 'L0_ffn_ln1_b': _L0_ffn_in['ln1_b'], 'L0_ffn_Wq': _L0_ffn_in['Wq'], 'L0_ffn_bq': _L0_ffn_in['bq'], 'L0_ffn_Wk': _L0_ffn_in['Wk'], 'L0_ffn_bk': _L0_ffn_in['bk'], 'L0_ffn_Wv': _L0_ffn_in['Wv'], 'L0_ffn_bv': _L0_ffn_in['bv'], 'L0_ffn_Wo': _L0_ffn_in['Wo'], 'L0_ffn_bo': _L0_ffn_in['bo'], 'L0_ffn_gate_W': _L0_ffn_in['gate_W'], 'L0_ffn_gate_b': _L0_ffn_in['gate_b'], 'L0_ffn_W1': _L0_ffn_in['W1'], 'L0_ffn_b1': _L0_ffn_in['b1'], 'L0_ffn_W2': _L0_ffn_in['W2'], 'L0_ffn_b2': _L0_ffn_in['b2']}

def reference(x, cls_tok, L0_tok_W, L0_tok_b, L0_tok_cls_token, L0_tok_pos_emb, L0_attn_A_log, L0_attn_W_B, L0_attn_b_B, L0_attn_W_C, L0_attn_b_C, L0_attn_W_dt, L0_attn_b_dt, L0_attn_D_skip, L0_attn_W_mix, L0_attn_b_mix, L0_attn_ln_g, L0_attn_ln_b, L0_attn_W_dec, L0_attn_b_dec, L0_ffn_ln1_g, L0_ffn_ln1_b, L0_ffn_Wq, L0_ffn_bq, L0_ffn_Wk, L0_ffn_bk, L0_ffn_Wv, L0_ffn_bv, L0_ffn_Wo, L0_ffn_bo, L0_ffn_gate_W, L0_ffn_gate_b, L0_ffn_W1, L0_ffn_b1, L0_ffn_W2, L0_ffn_b2):
    import jax
    import jax.numpy as jnp

    def _L0_tok_ref(x, W, b, cls_token, pos_emb):
        import jax, jax.numpy as jnp
        import numpy as np
        P1, P2, C = (16, 16, 3)
        PW, PH = (176 // P1, 208 // P2)
        B = x.shape[0]
        patches = x.reshape(B, C, PW, P1, PH, P2)
        patches = patches.transpose(0, 2, 4, 3, 5, 1).reshape(B, PW * PH, P1 * P2 * C)
        proj = jnp.einsum('bnp,dp->bnd', patches, W) + b
        cls = jnp.broadcast_to(cls_token, (B, 1, cls_token.shape[-1]))
        out = jnp.concatenate([cls, proj], axis=1) + pos_emb
        return out

    def _L0_attn_ref(x, A_log, W_B, b_B, W_C, b_C, W_dt, b_dt, D_skip, W_mix, b_mix, ln_g, ln_b, W_dec, b_dec):
        import jax, jax.numpy as jnp
        import numpy as np
        N_LAYERS = 2
        D = 128
        N = 16
        O = 128
        B = 4
        L = 512
        LN_EPS = 1e-05

        def _combine(e1, e2):
            a1, u1 = e1
            a2, u2 = e2
            return (a1 * a2, a2 * u1 + u2)
        h_in = x
        for i in range(N_LAYERS):
            A = -jnp.exp(A_log[i])
            Bm = h_in @ W_B[i] + b_B[i]
            Cm = h_in @ W_C[i] + b_C[i]
            dt = jax.nn.softplus(h_in @ W_dt[i] + b_dt[i])
            a = jnp.exp(dt[..., None] * A)
            u = (dt * h_in)[..., None] * Bm[:, :, None, :]
            _, h = jax.lax.associative_scan(_combine, (a, u), axis=1)
            y = jnp.einsum('bln,bldn->bld', Cm, h) + D_skip[i] * h_in
            y = jax.nn.gelu(y, approximate=False)
            y = y @ W_mix[i] + b_mix[i]
            mu = jnp.mean(y, axis=-1, keepdims=True)
            var = jnp.var(y, axis=-1, keepdims=True)
            y = (y - mu) / jnp.sqrt(var + LN_EPS) * ln_g[i] + ln_b[i]
            h_in = h_in + y
        return h_in @ W_dec + b_dec

    def _L0_ffn_ref(x, ln1_g, ln1_b, Wq, bq, Wk, bk, Wv, bv, Wo, bo, gate_W, gate_b, W1, b1, W2, b2):
        import jax, jax.numpy as jnp
        import numpy as np
        B, S, D, H, E = (4, 512, 128, 8, 8)
        FF = 4 * D
        HD = D // H
        EPS = 1e-05

        def _layernorm(x, g, b):
            mu = jnp.mean(x, axis=-1, keepdims=True)
            var = jnp.mean((x - mu) ** 2, axis=-1, keepdims=True)
            return (x - mu) * jax.lax.rsqrt(var + EPS) * g + b
        b, s, d = x.shape
        q = (x @ Wq + bq).reshape(b, s, H, HD)
        k = (x @ Wk + bk).reshape(b, s, H, HD)
        v = (x @ Wv + bv).reshape(b, s, H, HD)
        scores = jnp.einsum('bqhd,bkhd->bhqk', q, k) / jnp.sqrt(jnp.float32(HD))
        attn = jax.nn.softmax(scores, axis=-1)
        o = jnp.einsum('bhqk,bkhd->bqhd', attn, v).reshape(b, s, d) @ Wo + bo
        h = _layernorm(x + o, ln1_g, ln1_b)
        t = h.reshape(b * s, d)
        probs = jax.nn.softmax(t @ gate_W + gate_b, axis=-1)
        idx = jnp.argmax(probs, axis=-1)
        gw = jnp.max(probs, axis=-1)
        hid = jax.nn.gelu(jnp.einsum('nd,edf->enf', t, W1) + b1[:, None, :])
        out_all = jnp.einsum('enf,efd->end', hid, W2) + b2[:, None, :]
        onehot = jax.nn.one_hot(idx, E, dtype=t.dtype)
        out = jnp.einsum('ne,end->nd', onehot, out_all)
        out = out * gw[:, None]
        return out.reshape(b, s, d)
    h = _L0_tok_ref(x, L0_tok_W, L0_tok_b, L0_tok_cls_token, L0_tok_pos_emb)
    h = jnp.concatenate([jnp.broadcast_to(cls_tok, (h.shape[0], 1, h.shape[2])), h], axis=1)
    h = h + _L0_attn_ref(_layernorm(h, axis=-1), L0_attn_A_log, L0_attn_W_B, L0_attn_b_B, L0_attn_W_C, L0_attn_b_C, L0_attn_W_dt, L0_attn_b_dt, L0_attn_D_skip, L0_attn_W_mix, L0_attn_b_mix, L0_attn_ln_g, L0_attn_ln_b, L0_attn_W_dec, L0_attn_b_dec)
    h = h + _L0_ffn_ref(_layernorm(h, axis=-1), L0_ffn_ln1_g, L0_ffn_ln1_b, L0_ffn_Wq, L0_ffn_bq, L0_ffn_Wk, L0_ffn_bk, L0_ffn_Wv, L0_ffn_bv, L0_ffn_Wo, L0_ffn_bo, L0_ffn_gate_W, L0_ffn_gate_b, L0_ffn_W1, L0_ffn_b1, L0_ffn_W2, L0_ffn_b2)
    return h

_drawn_inputs = setup_inputs


def setup_inputs(seed=0):
    import zlib

    import numpy as np

    out = dict(_drawn_inputs(seed))
    spreads = {'L0_attn_b_B': (0.0, 0.1),
     'L0_attn_b_C': (0.0, 0.1),
     'L0_attn_b_dt': (0.0, 0.1),
     'L0_attn_D_skip': (1.0, 0.2),
     'L0_attn_b_mix': (0.0, 0.1),
     'L0_attn_ln_g': (1.0, 0.2),
     'L0_attn_ln_b': (0.0, 0.1),
     'L0_attn_b_dec': (0.0, 0.1),
     'L0_ffn_ln1_g': (1.0, 0.6),
     'L0_ffn_ln1_b': (0.0, 0.8),
     'L0_ffn_bq': (0.0, 0.8),
     'L0_ffn_bk': (0.0, 0.8),
     'L0_ffn_bv': (0.0, 0.8),
     'L0_ffn_bo': (0.0, 0.8),
     'L0_ffn_gate_b': (0.0, 0.8),
     'L0_ffn_b1': (0.0, 0.8),
     'L0_ffn_b2': (0.0, 0.8)}
    factors = {'L0_ffn_Wq': 8.0,
     'L0_ffn_Wk': 8.0,
     'L0_ffn_Wv': 8.0,
     'L0_ffn_Wo': 8.0,
     'L0_ffn_gate_W': 6.183,
     'L0_ffn_W1': 8.0,
     'L0_ffn_W2': 8.0}
    for name, (base, spread) in spreads.items():
        noise = np.random.default_rng([zlib.crc32(name.encode()), seed]).standard_normal(out[name].shape)
        drawn = base * np.exp(spread * noise) if base else spread * noise
        out[name] = jnp.asarray(drawn.astype(out[name].dtype))
    for name, factor in factors.items():
        out[name] = (out[name] * factor).astype(out[name].dtype)
    return out
```

```python
from contextlib import ExitStack

import concourse.bass as bass
from concourse import mybir

ALU = mybir.AluOpType
ACT = mybir.ActivationFunctionType
F32 = mybir.dt.float32
BF16 = mybir.dt.bfloat16
I32 = mybir.dt.int32
U32 = mybir.dt.uint32
AX = mybir.AxisListType.X

P = 128
D = 128
B = 128
CH, PSZ = 3, 16
PW, PH = 11, 13
NPATCH = PW * PH
L = NPATCH + 2
NST = 16
EPS = 1e-5


def at_least(eng, sem, value):
    if isinstance(value, int) and value <= 0:
        return
    eng.wait_ge(sem, value)


def clear(nc, semaphores):
    with nc.Block() as block:
        @block.gpsimd
        def _(pool):
            for s in semaphores:
                pool.sem_clear(s)


def wait_apart(eng, sem, value, met, met_value):
    if not isinstance(value, int):
        value = eng.snap(value)
    eng.wait_ge(met, met_value)
    eng.wait_ge(sem, value)


def embed_patches(nc, x, W, identity_ready, ident, proj_dram, stored):
    SLAB = PSZ * PH * PSZ
    KC = CH * 2
    PIX = CH * PSZ * PSZ
    NBLK = [4, 4, 4, 1]
    NB = len(NBLK)
    TURNS = NB * KC
    with ExitStack() as ctx:
        sb = lambda n, s, d=F32: ctx.enter_context(nc.sbuf_tensor(n, s, d))
        ps = lambda n, s, d=F32: ctx.enter_context(nc.psum_tensor(n, s, d))
        made = []

        def sem(name):
            made.append(ctx.enter_context(nc.semaphore(name)))
            return made[-1]

        slab = [sb(f"slab{i}", [B, CH, SLAB]) for i in range(2)]
        patches = sb("patches", [B, PH, PIX])
        w_rows = sb("w_rows", [D, KC * P])
        w_order = sb("w_order", [D, KC * P])
        w_t = sb("w_t", [P, KC, D])
        pix = [sb(f"pix{i}", [P, KC, 4 * P]) for i in range(2)]
        res = [sb(f"res{i}", [D, B, PH]) for i in range(2)]
        tp = ps("tp", [P, 4, 512])
        acc = ps("acc", [P, 2, 512])
        slab_in = [sem(f"slab_in{i}") for i in range(2)]
        w_in, w_ordered, w_turned, w_copied = sem("w_in"), sem("w_ordered"), sem("w_turned"), sem("w_copied")
        ordered, turned, pix_copied = sem("ordered"), sem("turned"), sem("pix_copied")
        acc_done, acc_copied = sem("acc_done"), sem("acc_copied")
        xs = x.rearrange("b c (w q) j -> w b c (q j)", q=PSZ)
        out = proj_dram.rearrange("d w b h -> w d (b h)")

        def steps(eng, body):
            body(0, 0, 0)
            with eng.Fori(0, PW // 2) as k:
                body(2 * k + 1, 1, k)
                body(2 * k + 2, 0, k + 1)

        ctx.callback(clear, nc, made)
        block = ctx.enter_context(nc.Block())

        @block.sync
        def _(sp):
            sp.dma_start(w_rows[:, :], W).then_inc(w_in, 16)
            sp.dma_start(slab[0][:, :, :], xs[0]).then_inc(slab_in[0], 16)
            sp.dma_start(slab[1][:, :, :], xs[1]).then_inc(slab_in[1], 16)
            with sp.Fori(0, PW // 2 - 1) as k:
                sp.wait_ge(ordered, (2 * k + 1) * NB)
                sp.dma_start(slab[0][:, :, :], xs[2 * k + 2]).then_inc(slab_in[0], 16)
                sp.wait_ge(ordered, (2 * k + 2) * NB)
                sp.dma_start(slab[1][:, :, :], xs[2 * k + 3]).then_inc(slab_in[1], 16)
            sp.wait_ge(ordered, (PW - 2) * NB)
            sp.dma_start(slab[0][:, :, :], xs[PW - 1]).then_inc(slab_in[0], 16)

        @block.tensor
        def _(pe):
            pe.wait_ge(w_ordered, 1)
            at_least(pe, identity_ready, 2)
            for k in range(KC):
                ins = pe.transpose(tp[:, k // 4, (k % 4) * P:(k % 4 + 1) * P], w_order[:, k * P:(k + 1) * P], ident[:, :])
            ins.then_inc(w_turned, 1)
            pe.wait_ge(w_copied, 1)

            def step(t, par, before):
                n, col = t * TURNS, 0
                for blk, nph in enumerate(NBLK):
                    pe.wait_ge(ordered, t * NB + blk + 1)
                    for k in range(KC):
                        at_least(pe, pix_copied, n + blk * KC + k - 3)
                        for j in range(nph):
                            ins = pe.transpose(tp[:, (blk * KC + k) % 4, j * P:(j + 1) * P],
                                               patches[:, col + j, k * P:(k + 1) * P], ident[:, :])
                        ins.then_inc(turned, 1)
                    pe.wait_ge(pix_copied, n + (blk + 1) * KC)
                    at_least(pe, acc_copied, t * NB + blk - 1)
                    for k in range(KC):
                        ins = pe.matmul(acc[:, blk % 2, 0:nph * P], w_t[:, k, :], pix[blk % 2][:, k, 0:nph * P],
                                        start=(k == 0), stop=(k == KC - 1))
                    ins.then_inc(acc_done, 1)
                    col += nph

            steps(pe, step)

        @block.vector
        def _(dve):
            dve.wait_ge(w_in, 16)
            nc.vector.tensor_copy(w_order[:, :].rearrange("d (c q) -> d c q", c=CH),
                                  w_rows[:, :].rearrange("d (q c) -> d c q", c=CH)).then_inc(w_ordered, 1)
            dve.wait_ge(w_turned, 1)
            nc.vector.tensor_copy(w_t[:, :, :].rearrange("p k d -> p (k d)"),
                                  tp[:, 0:2, :].rearrange("p a b -> p (a b)")[:, 0:KC * P]).then_inc(w_copied, 1)

            def step(t, par, before):
                dve.wait_ge(slab_in[par], 16 * (before + 1))
                for blk, nph in enumerate(NBLK):
                    at_least(dve, turned, (t - 1) * TURNS + (blk + 1) * KC)
                    c0 = 4 * blk
                    nc.vector.tensor_copy(
                        patches[:, c0:c0 + nph, :].rearrange("b j (q e) -> b j q e", e=PSZ),
                        slab[par][:, :, :].rearrange("b c (q j e) -> b j (c q) e", j=PH, e=PSZ)[:, c0:c0 + nph],
                    ).then_inc(ordered, 1)
                for blk, nph in enumerate(NBLK):
                    at_least(dve, acc_done, t * NB + blk - 1)
                    for k in range(0, KC, 2):
                        dve.wait_ge(turned, t * TURNS + blk * KC + k + 1)
                        at_least(dve, pix_copied, t * TURNS + blk * KC + k)
                        nc.vector.tensor_copy(pix[blk % 2][:, k, 0:nph * P],
                                              tp[:, (blk * KC + k) % 4, 0:nph * P]).then_inc(pix_copied, 1)

            steps(dve, step)

        @block.scalar
        def _(act):
            def step(t, par, before):
                col = 0
                for blk, nph in enumerate(NBLK):
                    at_least(act, acc_done, t * NB + blk - 1)
                    for k in range(1, KC, 2):
                        act.wait_ge(turned, t * TURNS + blk * KC + k + 1)
                        at_least(act, pix_copied, t * TURNS + blk * KC + k)
                        nc.scalar.activation(pix[blk % 2][:, k, 0:nph * P], tp[:, (blk * KC + k) % 4, 0:nph * P],
                                             ACT.Copy).then_inc(pix_copied, 1)
                    act.wait_ge(acc_done, t * NB + blk + 1)
                    if blk == 0:
                        at_least(act, stored[par], 16 * before)
                    nc.scalar.activation(res[par][:, :, col:col + nph].rearrange("p r c -> p c r"),
                                         acc[:, blk % 2, 0:nph * P].rearrange("p (c r) -> p c r", r=B),
                                         ACT.Copy).then_inc(acc_copied, 1)
                    col += nph

            steps(act, step)

        @block.gpsimd
        def _(pool):
            def step(t, par, before):
                pool.wait_ge(acc_copied, (t + 1) * NB)
                pool.dma_start(out[t], res[par][:, :, :].rearrange("p b h -> p (b h)")).then_inc(stored[par], 16)

            steps(pool, step)
            pool.wait_ge(stored[0], 16 * (PW // 2 + 1))
            pool.wait_ge(stored[1], 16 * (PW // 2))


G = 3
T = G * L
NGROUP = -(-B // G)
PAIRS = NST // 2
RING = 4
PARTS = 3
EXP_LN_SET = "natural_log_exp_and_others"
NBC = 2 * NST


def ssm_layers(nc, prm, ident, proj_dram, h1_dram, ngroup=NGROUP):
    with ExitStack() as ctx:
        sb = lambda n, s, d=F32: ctx.enter_context(nc.sbuf_tensor(n, s, d))
        ps = lambda n, s, d=F32: ctx.enter_context(nc.psum_tensor(n, s, d))
        made = []

        def sem(name):
            made.append(ctx.enter_context(nc.semaphore(name)))
            return made[-1]


        center = sb("center", [D, D])
        mean = sb("mean", [D, D])
        pick = sb("pick", [NBC * PARTS, NBC, P], BF16)
        eps = sb("eps", [D, 1])
        a_neg = sb("a_neg", [D, 2, NST])
        w_bc = sb("w_bc", [D, 2, PARTS, NBC])
        b_bc = sb("b_bc", [NBC * PARTS, 2])
        w_dt = sb("w_dt", [D, 2, D])
        w_mix = sb("w_mix", [D, 2, D])
        w_mix_t = sb("w_mix_t", [D, 2, D])
        w_mixc = sb("w_mixc", [D, 2, D])
        b_mixc = sb("b_mixc", [D, 2])
        w_dec = sb("w_dec", [D, D])
        cols = sb("cols", [D, 16])
        b_dt, b_mix, d_skip, ln_g, ln_b = (cols[:, 2 * i:2 * i + 2] for i in range(5))
        b_tok, b_dec, cls0, cls1 = (cols[:, 10 + i:11 + i] for i in range(4))
        pos = sb("pos", [D, L])
        pos_out = sb("pos_out", [D, L])

        proj = sb("patches_in", [D, PW, G, PH])
        proj_again = sb("proj_again", [D, PW, G, PH])
        h0 = sb("h0", [D, G, L])
        h0c = sb("h0c", [D, T])
        sq = sb("sq", [D, T])
        lnv0, lnv = sb("lnv0", [D, T]), sb("lnv", [D, T])
        rstd0 = sb("rstd0", [D, T])
        hin0 = sb("hin0", [D, T])
        hin1_next = sb("hin1_next", [D, T])
        hin1 = sb("hin1", [D, T])
        hin = [hin0, hin1]
        hin_pre = [hin0, hin1_next]
        dt = [sb(f"dt{i}", [D, T]) for i in range(2)]
        dtx = [sb(f"dtx{i}", [D, T]) for i in range(2)]
        bc = [sb(f"bc{i}", [NBC * PARTS, T], BF16) for i in range(2)]
        sp_abs, sp_relu = sb("sp_abs", [D, T]), sb("sp_relu", [D, T])
        left = sb("left", [NBC * (PARTS - 1), T])
        y = sb("y_sb", [D, T])
        gelu = sb("gelu", [D, T])
        yc = sb("yc", [D, T])
        rstd = sb("rstd", [D, T])
        yn = sb("yn", [D, T])
        zdec = sb("zdec", [D, T])
        res = sb("res_a", [D, G, L])
        outb = sb("outb", [D, G, L])
        a = [sb(f"a{i}", [D, 2, G, L]) for i in range(RING)]
        u = [sb(f"u{i}", [D, 2, T]) for i in range(RING)]
        h = [sb(f"h_ring{i}", [D, 2, T]) for i in range(RING)]
        cs = [sb(f"cs{i}", [D, 2, T]) for i in range(RING)]
        hc = [sb(f"hc{i}", [D, 2, T]) for i in range(RING)]

        b_ps = [ps(f"b_ps{i}", [P, 2, 512]) for i in range(2)]
        c_ps = ps("c_ps", [P, 2, 512])
        y_ps = ps("y_ps", [P, 512])
        mm_ps = ps("mm_ps", [P, 512])

        loaded, s_pool, s_act, s_pe, s_dve = (sem(n) for n in ("loaded", "s_pool", "s_act", "s_pe", "s_dve"))
        with nc.Block() as block:
            col = lambda v: v.rearrange("(d o) -> d o", o=1)
            loads = []
            for p in range(PARTS):
                for l in range(2):
                    loads += [(w_bc[:, l, p, 0:NST], prm["W_B"][l]), (w_bc[:, l, p, NST:NBC], prm["W_C"][l]),
                              (b_bc[NBC * p:NBC * p + NST, l:l + 1], col(prm["b_B"][l])),
                              (b_bc[NBC * p + NST:NBC * (p + 1), l:l + 1], col(prm["b_C"][l]))]
            loads += [(a_neg[:, :, :], prm["A_log"].rearrange("l d n -> d l n")),
                      (w_dt[:, :, :], prm["W_dt"].rearrange("l d n -> d l n")),
                      (w_mix[:, :, :], prm["W_mix"].rearrange("l d n -> d l n")), (w_dec[:, :], prm["W_dec"]),
                      (pos[:, 1:L], prm["pos"][0].rearrange("l o -> o l").broadcast_to([D, L - 1])),
                      (b_tok, col(prm["b_tok"])), (b_dec, col(prm["b_dec"])),
                      (cls0, col(prm["cls0"][0, 0])), (cls1, col(prm["cls1"][0, 0]))]
            for t, name in ((b_dt, "b_dt"), (b_mix, "b_mix"), (d_skip, "D_skip"), (ln_g, "ln_g"), (ln_b, "ln_b")):
                for l in range(2):
                    loads.append((t[:, l:l + 1], col(prm[name][l])))

            @block.sync
            def _(sp):
                for dst, src in loads:
                    sp.dma_start(dst, src).then_inc(loaded, 16)

            @block.gpsimd
            def _(pool):
                nc.gpsimd.memset(mean[:, :], 1.0 / D).then_inc(s_pool, 1)
                nc.gpsimd.memset(pick[:, :, :], 0.0).then_inc(s_pool, 1)
                for p in range(PARTS):
                    pool.wait_ge(s_pool, 2 + p)
                    pool.affine_select(out=pick[:, :, :], in_=pick[:, :, :], compare_op=ALU.not_equal, fill=1.0,
                                       base=-NBC * p, pattern=[[-1, NBC], [0, P]],
                                       channel_multiplier=1).then_inc(s_pool, 1)

            @block.scalar
            def _(act):
                act.wait_ge(loaded, 16 * len(loads))
                nc.scalar.activation(a_neg[:, :, :], a_neg[:, :, :], ACT.Exp).then_inc(s_act, 1)

            @block.tensor
            def _(pe):
                pe.wait_ge(loaded, 16 * len(loads))
                for l in range(2):
                    ins = pe.transpose(y_ps[:, l * D:(l + 1) * D], w_mix[:, l, :], ident[:, :])
                ins.then_inc(s_pe, 1)
                pe.wait_ge(s_dve, 6)
                for l in range(2):
                    pe.matmul(mm_ps[:, l * D:(l + 1) * D], w_mix_t[:, l, :], center[:, :], start=True, stop=True)
                    ins = pe.matmul(mm_ps[:, 2 * D + l:2 * D + l + 1], center[:, :], b_mix[:, l:l + 1],
                                    start=True, stop=True)
                ins.then_inc(s_pe, 1)

            @block.vector
            def _(dve):
                nc.vector.memset(eps[:, :], EPS).then_inc(s_dve, 1)
                for r in range(RING):
                    ins = nc.vector.memset(a[r][:, :, :, :], 0.0)
                ins.then_inc(s_dve, 1)
                dve.wait_ge(s_act, 1)
                nc.vector.tensor_scalar(a_neg[:, :, :], a_neg[:, :, :], -1.0, None, ALU.mult).then_inc(s_dve, 1)
                dve.wait_ge(s_pool, 1)
                nc.vector.tensor_tensor(center[:, :], ident[:, :], mean[:, :], ALU.subtract).then_inc(s_dve, 1)
                dve.wait_ge(s_pe, 1)
                nc.vector.tensor_copy(w_mix_t[:, :, :].rearrange("p a b -> p (a b)"), y_ps[:, 0:2 * D]).then_inc(s_dve, 1)
                nc.vector.tensor_scalar(pos[:, 2:L], pos[:, 2:L], b_tok, None, ALU.add).then_inc(s_dve, 1)
                nc.vector.tensor_scalar(pos[:, 1:2], pos[:, 1:2], cls1, None, ALU.add).then_inc(s_dve, 1)
                nc.vector.tensor_copy(pos[:, 0:1], cls0).then_inc(s_dve, 1)
                dve.wait_ge(s_dve, 8)
                nc.vector.tensor_scalar(pos_out[:, :], pos[:, :], b_dec, None, ALU.add).then_inc(s_dve, 1)
                for g in range(G):
                    ins = nc.vector.tensor_copy(h0[:, g, 0:2], pos[:, 0:2])
                    ins = nc.vector.memset(res[:, g, 0:2], 0.0)
                ins.then_inc(s_dve, 1)
                dve.wait_ge(s_dve, 10)
                for g in range(G):
                    ins = nc.vector.tensor_copy(res[:, g, 0:2], pos_out[:, 0:2])
                ins.then_inc(s_dve, 1)
                dve.wait_ge(s_pe, 2)
                nc.vector.tensor_copy(w_mixc[:, :, :].rearrange("p a b -> p (a b)"), mm_ps[:, 0:2 * D]).then_inc(s_dve, 1)
                nc.vector.tensor_copy(b_mixc[:, :], mm_ps[:, 2 * D:2 * D + 2]).then_inc(s_dve, 1)

        a_made, b_spread, c_spread, c_copied = sem("a_made"), sem("b_spread"), sem("c_spread"), sem("c_copied")
        u_made, scanned, hc_made, summed = (sem(n) for n in ("u_made", "scanned", "hc_made", "summed"))
        (dt_mm, sp_abs_made, sp_relu_made, sp_exp_made, sp_ln_made, dt_made, dtx_made, bc_mm, bc_part0, bc_left,
         bc_part1, bc_made) = (sem(n) for n in (
             "dt_mm", "sp_abs_made", "sp_relu_made", "sp_exp_made", "sp_ln_made", "dt_made", "dtx_made", "bc_mm",
             "bc_part0", "bc_left", "bc_part1", "bc_made"))
        y_made, gelu_made, mix_mm, yc_made, var_mm, rstd_made, yn_made, hin_next = (sem(n) for n in (
            "y_made", "gelu_made", "mix_mm", "yc_made", "var_mm", "rstd_made", "yn_made", "hin_next"))
        (proj_in, h0_made, h0c_mm, h0c_made, var0_mm, rstd0_made, hin0_made, again_in, res_made, hin1_moved,
         dec_mm, out_made, out_stored) = (sem(n) for n in (
             "proj_in", "h0_made", "h0c_mm", "h0c_made", "var0_mm", "rstd0_made", "hin0_made", "again_in", "res_made",
             "hin1_moved", "dec_mm", "out_made", "out_stored"))
        mm_free = sem("mm_free")
        flat = lambda t: t[:, :, :].rearrange("d g l -> d (g l)")
        grid = lambda t: t.rearrange("d (w h) -> d w h", w=PW)
        mm = mm_ps[:, 0:T]

        def pair_pe(pe, l, s, j):
            c = PAIRS * s + j
            if j == 0:
                pe.wait_ge(bc_made, s + 1)
            at_least(pe, u_made, c - 1)
            for k in range(2):
                ins = pe.matmul(b_ps[j % 2][:, k, 0:T], pick[:, 2 * j + k, :], bc[l][:, :], start=True, stop=True)
            ins.then_inc(b_spread, 1)
            at_least(pe, c_copied, c)
            for k in range(2):
                ins = pe.matmul(c_ps[:, k, 0:T], pick[:, NST + 2 * j + k, :], bc[l][:, :], start=True, stop=True)
            ins.then_inc(c_spread, 1)

        def pair_act(act, l, s, j):
            c, r = PAIRS * s + j, j % RING
            if j == 0:
                act.wait_ge(dt_made, s + 1)
            at_least(act, scanned, c - RING + 1)
            dtv = dt[l][:, :].rearrange("d (g l) -> d g l", g=G)[:, :, 1:L]
            for k in range(2):
                ins = nc.scalar.activation(a[r][:, k, :, 1:L], dtv, ACT.Exp, scale=a_neg[:, l, 2 * j + k:2 * j + k + 1])
            ins.then_inc(a_made, 1)
            act.wait_ge(c_spread, c + 1)
            at_least(act, hc_made, c - RING + 1)
            nc.scalar.activation(cs[r][:, :, :], c_ps[:, :, 0:T], ACT.Copy).then_inc(c_copied, 1)

        def pair_dve(dve, l, s, j):
            c, r = PAIRS * s + j, j % RING
            if j == 0:
                dve.wait_ge(dtx_made, s + 1)
            dve.wait_ge(b_spread, c + 1)
            at_least(dve, scanned, c - RING + 1)
            nc.vector.tensor_tensor(u[r][:, :, :], b_ps[j % 2][:, :, 0:T],
                                    dtx[l][:, :].rearrange("d (o t) -> d o t", o=1).broadcast_to([D, 2, T]),
                                    ALU.mult).then_inc(u_made, 1)
            dve.wait_ge(u_made, c + 1)
            dve.wait_ge(a_made, c + 1)
            at_least(dve, hc_made, c - RING + 1)
            nc.vector.tensor_tensor_scan(h[r][:, :, :].rearrange("d k t -> d (k t)"),
                                         a[r][:, :, :, :].rearrange("d k g l -> d (k g l)"),
                                         u[r][:, :, :].rearrange("d k t -> d (k t)"), 0.0,
                                         ALU.mult, ALU.add).then_inc(scanned, 1)

        def pair_pool(pool, l, s, j):
            c, r = PAIRS * s + j, j % RING
            pool.wait_ge(scanned, c + 1)
            pool.wait_ge(c_copied, c + 1)
            at_least(pool, summed, c - RING + 1)
            nc.gpsimd.tensor_tensor(hc[r][:, :, :], h[r][:, :, :], cs[r][:, :, :], ALU.mult).then_inc(hc_made, 1)

        def sum_pe(pe, s, j):
            pe.wait_ge(hc_made, PAIRS * s + j + 1)
            if j == 0:
                at_least(pe, y_made, s)
            for k in range(2):
                ins = pe.matmul(y_ps[:, 0:T], ident[:, :], hc[j % RING][:, k, :], start=(j == 0 and k == 0),
                                stop=(j == PAIRS - 1 and k == 1))
            ins.then_inc(summed, 1)

        def pre0_pool(pool, g):
            pool.wait_ge(proj_in, 16 * (g + 1))
            at_least(pool, h0c_mm, g)
            for k in range(G):
                ins = nc.gpsimd.tensor_tensor(grid(h0[:, k, 2:L]), proj[:, :, k, :], grid(pos[:, 2:L]), ALU.add)
            ins.then_inc(h0_made, 1)

        def pre0_pe_center(pe, g, taken):
            pe.wait_ge(h0_made, g + 1)
            at_least(pe, mm_free, taken)
            pe.matmul(mm, center[:, :], flat(h0), start=True, stop=True).then_inc(h0c_mm, 1)

        def pre0_act_center(act, g):
            act.wait_ge(h0c_mm, g + 1)
            at_least(act, hin0_made, g)
            nc.scalar.activation(h0c[:, :], mm, ACT.Copy).then_inc(h0c_made, 1)
            nc.scalar.activation(sq[:, :], mm, ACT.Square).then_inc(mm_free, 1)

        def pre0_pe_var(pe, g, taken):
            pe.wait_ge(mm_free, taken)
            pe.matmul(mm, mean[:, :], sq[:, :], start=True, stop=True).then_inc(var0_mm, 1)

        def pre0_act_rstd(act, g, taken):
            act.wait_ge(var0_mm, g + 1)
            at_least(act, rstd0_made, g)
            nc.scalar.activation(lnv0[:, :], mm, ACT.Ln, bias=eps[:, :]).then_inc(mm_free, 1)
            act.wait_ge(mm_free, taken + 1)
            at_least(act, hin0_made, g)
            nc.scalar.activation(rstd0[:, :], lnv0[:, :], ACT.Exp, scale=-0.5).then_inc(rstd0_made, 1)

        def pre0_dve(dve, g, post):
            dve.wait_ge(rstd0_made, g + 1)
            dve.wait_ge(h0c_made, g + 1)
            if post is not None:
                dve.wait_ge(hin_next, post + 1)
            nc.vector.tensor_tensor(hin0[:, :], h0c[:, :], rstd0[:, :], ALU.mult).then_inc(hin0_made, 1)

        def wait_hin(eng, l, g, posts):
            if l == 0:
                eng.wait_ge(hin0_made, g + 1)
            else:
                eng.wait_ge(hin_next, posts)

        def pre_pe_dt(pe, l, s, g, posts, taken):
            wait_hin(pe, l, g, posts)
            at_least(pe, mm_free, taken)
            pe.matmul(mm, w_dt[:, l, :], hin_pre[l][:, :], start=True, stop=True).then_inc(dt_mm, 1)

        def pre_act_dt(act, l, s):
            bias = b_dt[:, l:l + 1]
            act.wait_ge(dt_mm, s + 1)
            at_least(act, dt_made, s)
            nc.scalar.activation(sp_abs[:, :], mm, ACT.Abs, bias=bias).then_inc(sp_abs_made, 1)
            nc.scalar.activation(sp_relu[:, :], mm, ACT.Relu, bias=bias).then_inc(mm_free, 1)
            act.wait_ge(sp_abs_made, s + 1)
            nc.scalar.activation(sp_abs[:, :], sp_abs[:, :], ACT.Exp, scale=-1.0).then_inc(sp_exp_made, 1)
            act.wait_ge(sp_exp_made, s + 1)
            nc.scalar.activation(sp_abs[:, :], sp_abs[:, :], ACT.Ln, bias=1.0).then_inc(sp_ln_made, 1)

        def pre_pool_dt(pool, l, s, g, posts, pairs, taken):
            pool.wait_ge(sp_ln_made, s + 1)
            pool.wait_ge(mm_free, taken + 1)
            at_least(pool, a_made, pairs)
            at_least(pool, u_made, pairs)
            nc.gpsimd.tensor_tensor(dt[l][:, :], sp_abs[:, :], sp_relu[:, :], ALU.add).then_inc(dt_made, 1)
            pool.wait_ge(dt_made, s + 1)
            wait_hin(pool, l, g, posts)
            nc.gpsimd.tensor_tensor(dtx[l][:, :], dt[l][:, :], hin_pre[l][:, :], ALU.mult).then_inc(dtx_made, 1)

        def pre_pe_bc(pe, l, s, taken):
            pe.wait_ge(mm_free, taken)
            pe.matmul(mm_ps[0:NBC * PARTS, 0:T], w_bc[:, l, :, :].rearrange("d p n -> d (p n)"), hin_pre[l][:, :],
                      start=True, stop=True).then_inc(bc_mm, 1)

        def pre_dve_bc(dve, l, s, pairs, taken):
            dve.wait_ge(bc_mm, s + 1)
            at_least(dve, c_spread, pairs)
            x, bias = mm_ps[0:NBC * PARTS, 0:T], b_bc[:, l:l + 1]
            n2, n3 = NBC * 2, NBC
            nc.vector.tensor_scalar(bc[l][:, :], x, bias, None, ALU.add).then_inc(bc_part0, 1)
            dve.wait_ge(bc_part0, s + 1)
            at_least(dve, bc_made, s)
            nc.vector.scalar_tensor_tensor(out=left[:, :], in0=x[0:n2], scalar=bias[0:n2], in1=bc[l][0:n2, :],
                                           op0=ALU.add, op1=ALU.subtract).then_inc(mm_free, 1)
            dve.wait_ge(mm_free, taken + 1)
            nc.vector.tensor_copy(bc[l][0:n2, :], left[:, :]).then_inc(bc_part1, 1)
            dve.wait_ge(bc_part1, s + 1)
            nc.vector.tensor_tensor(bc[l][0:n3, :], left[0:n3, :], bc[l][0:n3, :], ALU.subtract).then_inc(bc_made, 1)

        def post_dve_y(dve, l, s, g):
            dve.wait_ge(summed, PAIRS * (s + 1))
            dve.wait_ge(hin1_moved if l else hin0_made, g + 1)
            at_least(dve, gelu_made, s)
            nc.vector.scalar_tensor_tensor(out=y[:, :], in0=hin[l][:, :], scalar=d_skip[:, l:l + 1], in1=y_ps[:, 0:T],
                                           op0=ALU.mult, op1=ALU.add).then_inc(y_made, 1)

        def post_act_gelu(act, s):
            act.wait_ge(y_made, s + 1)
            at_least(act, mix_mm, s)
            nc.scalar.activation(gelu[:, :], y[:, :], ACT.Gelu).then_inc(gelu_made, 1)
            act.preload_act_table_set(EXP_LN_SET)

        def post_pe_mix(pe, l, s, taken):
            pe.wait_ge(gelu_made, s + 1)
            at_least(pe, mm_free, taken)
            pe.matmul(mm, w_mixc[:, l, :], gelu[:, :], start=True, stop=True).then_inc(mix_mm, 1)

        def post_act_mix(act, l, s):
            act.wait_ge(mix_mm, s + 1)
            at_least(act, yn_made, s)
            nc.scalar.activation(yc[:, :], mm, ACT.Identity, bias=b_mixc[:, l:l + 1]).then_inc(yc_made, 1)
            nc.scalar.activation(sq[:, :], mm, ACT.Square, bias=b_mixc[:, l:l + 1]).then_inc(mm_free, 1)

        def post_pe_var(pe, s, taken):
            pe.wait_ge(mm_free, taken)
            pe.matmul(mm, mean[:, :], sq[:, :], start=True, stop=True).then_inc(var_mm, 1)

        def post_act_rstd(act, s, taken):
            act.wait_ge(var_mm, s + 1)
            at_least(act, rstd_made, s)
            nc.scalar.activation(lnv[:, :], mm, ACT.Ln, bias=eps[:, :]).then_inc(mm_free, 1)
            act.wait_ge(mm_free, taken + 1)
            at_least(act, yn_made, s)
            nc.scalar.activation(rstd[:, :], lnv[:, :], ACT.Exp, scale=-0.5).then_inc(rstd_made, 1)

        def post_dve_norm(dve, l, s, g):
            dve.wait_ge(rstd_made, s + 1)
            dve.wait_ge(yc_made, s + 1)
            at_least(dve, hin_next, s)
            nc.vector.scalar_tensor_tensor(out=yn[:, :], in0=yc[:, :], scalar=ln_g[:, l:l + 1], in1=rstd[:, :],
                                           op0=ALU.mult, op1=ALU.mult).then_inc(yn_made, 1)
            dve.wait_ge(yn_made, s + 1)
            at_least(dve, dec_mm if l else hin1_moved, g)
            nc.vector.scalar_tensor_tensor(out=(zdec if l else hin1_next)[:, :], in0=yn[:, :], scalar=ln_b[:, l:l + 1],
                                           in1=hin[l][:, :], op0=ALU.add, op1=ALU.add).then_inc(hin_next, 1)

        def post1_pool(pool, g):
            pool.wait_ge(again_in, 16 * (g + 1))
            at_least(pool, out_made, g)
            for k in range(G):
                ins = nc.gpsimd.tensor_tensor(grid(res[:, k, 2:L]), proj_again[:, :, k, :], grid(pos_out[:, 2:L]), ALU.add)
            ins.then_inc(res_made, 1)

        def pre1_dve_move(dve, s, g, post):
            dve.wait_ge(hin_next, s - 1 if post is None else post + 1)
            nc.vector.tensor_copy(hin1[:, :], hin1_next[:, :]).then_inc(hin1_moved, 1)

        def post1_pe_dec(pe, s, taken):
            pe.wait_ge(hin_next, s + 1)
            pe.wait_ge(mm_free, taken)
            pe.matmul(mm, w_dec[:, :], zdec[:, :], start=True, stop=True).then_inc(dec_mm, 1)

        def post1_dve(dve, g, taken):
            dve.wait_ge(dec_mm, g + 1)
            dve.wait_ge(res_made, g + 1)
            at_least(dve, out_stored, 16 * g)
            nc.vector.tensor_tensor(flat(outb), mm, flat(res), ALU.add).then_inc(mm_free, 1)
            dve.wait_ge(mm_free, taken + 1)
            dve.sem_inc(out_made, 1)

        MM_POST, MM_PRE = (2, 3), (4, 2)
        BEFORE_LOOP = MM_PRE[0] + MM_POST[0] + MM_PRE[0] + MM_PRE[1] + MM_POST[0] + MM_PRE[0]
        PER_ROUND = sum(MM_POST) + sum(MM_PRE)

        def rounds(eng, run):
            n = ngroup
            run(None, None, (0, 0, 0), 0)
            run((0, 0, 0), None, None, 4)
            run(None, (0, 0, 0), (0, 1, 1), 4)
            run((0, 1, 1), None, (1, 2, 0), 10)
            run((1, 2, 0), (0, 1, 1), (0, 3, 2), 12)

            def round_of(i, taken, ahead):
                run((0, 2 * i - 1, i), (1, 2 * i - 2, i - 2), (1, 2 * i, i - 1), taken)
                run((1, 2 * i, i - 1), (0, 2 * i - 1, i), (0, 2 * i + 1, i + 1) if ahead else None,
                    taken + MM_POST[1] + MM_PRE[1])

            with eng.Fori(2, n - 1) as i:
                round_of(i, (i - 2) * PER_ROUND + BEFORE_LOOP, True)
            taken = BEFORE_LOOP + (n - 3) * PER_ROUND
            round_of(n - 1, taken, False)
            taken += PER_ROUND - MM_PRE[0]
            run(None, (1, 2 * n - 2, n - 2), (1, 2 * n - 1, n - 1), taken)
            run((1, 2 * n - 1, n - 1), None, None, taken + 5)
            run(None, (1, 2 * n - 1, n - 1), None, taken + 5)

        def posts_before(pre, post):
            return post[1] if post is not None else pre[1] - 1

        def pairs_before(pre, pairs):
            return PAIRS * (pre[1] if pairs is None else pre[1] - 1)

        def taken_in(post, pre, taken):
            out = {}
            if pre is not None and pre[0] == 0:
                out["center"], out["var0"], taken = taken, taken + 1, taken + 2
            if pre is not None and pre[0] == 1:
                out["dt"], out["bc"], taken = taken, taken + 1, taken + 2
            if post is not None:
                out["mix"], out["var"], taken = taken, taken + 1, taken + 2
                if post[0] == 1:
                    out["dec"], taken = taken, taken + 1
            if pre is not None and pre[0] == 0:
                out["dt"], out["bc"] = taken, taken + 1
            return out

        ctx.callback(clear, nc, made)
        block = ctx.enter_context(nc.Block())

        @block.sync
        def _(sp):
            start = lambda g: min(G * g, B - G) if isinstance(g, int) else G * g

            def load(buf, done, last_read, g):
                at_least(sp, last_read, g)
                sp.dma_start(buf[:, :, :, :], proj_dram[:, :, bass.ds(start(g), G), :]).then_inc(done, 16)

            def store(g):
                sp.wait_ge(out_made, g + 1)
                sp.dma_start(h1_dram[:, bass.ds(start(g), G), :], outb[:, :, :]).then_inc(out_stored, 16)

            load(proj, proj_in, h0_made, 0)
            load(proj, proj_in, h0_made, 1)
            load(proj_again, again_in, res_made, 0)
            load(proj, proj_in, h0_made, 2)
            store(0)
            with sp.Fori(1, ngroup - 3) as g:
                load(proj_again, again_in, res_made, g)
                load(proj, proj_in, h0_made, g + 2)
                store(g)
            for g in range(ngroup - 3, ngroup):
                load(proj_again, again_in, res_made, g)
                if g + 2 < ngroup:
                    load(proj, proj_in, h0_made, g + 2)
                store(g)
            sp.wait_ge(out_stored, 16 * ngroup)

        @block.tensor
        def _(pe):
            def run(pairs, post, pre, taken):
                at = taken_in(post, pre, taken)
                if pairs is None and post is not None:
                    sum_pe(pe, post[1], PAIRS - 2)
                    sum_pe(pe, post[1], PAIRS - 1)
                for j in range(PAIRS):
                    if pairs is not None:
                        pair_pe(pe, pairs[0], pairs[1], j)
                        if j >= 2:
                            sum_pe(pe, pairs[1], j - 2)
                        elif post is not None:
                            sum_pe(pe, post[1], PAIRS - 2 + j)
                    if pre is not None and pre[0] == 0:
                        if j == 0:
                            pre0_pe_center(pe, pre[2], at["center"])
                        if j == 1:
                            pre0_pe_var(pe, pre[2], at["var0"])
                    if pre is not None and j == (5, 0)[pre[0]]:
                        pre_pe_dt(pe, *pre, posts_before(pre, post), at["dt"])
                    if pre is not None and j == (6, 1)[pre[0]]:
                        pre_pe_bc(pe, pre[0], pre[1], at["bc"])
                    if post is not None:
                        if j == 3:
                            post_pe_mix(pe, post[0], post[1], at["mix"])
                        if j == 4:
                            post_pe_var(pe, post[1], at["var"])
                        if j == 5 and post[0] == 1:
                            post1_pe_dec(pe, post[1], at["dec"])

            rounds(pe, run)

        @block.scalar
        def _(act):
            def run(pairs, post, pre, taken):
                at = taken_in(post, pre, taken)
                for j in range(PAIRS):
                    if pairs is not None:
                        pair_act(act, pairs[0], pairs[1], j)
                    if pre is not None and pre[0] == 0:
                        if j == 0:
                            pre0_act_center(act, pre[2])
                        if j == 1:
                            pre0_act_rstd(act, pre[2], at["var0"])
                    if pre is not None and j == (5, 0)[pre[0]]:
                        pre_act_dt(act, pre[0], pre[1])
                    if post is not None:
                        if j == 2:
                            post_act_gelu(act, post[1])
                        if j == 3:
                            post_act_mix(act, post[0], post[1])
                        if j == 4:
                            post_act_rstd(act, post[1], at["var"])

            act.preload_act_table_set(EXP_LN_SET)
            rounds(act, run)

        @block.vector
        def _(dve):
            def run(pairs, post, pre, taken):
                at = taken_in(post, pre, taken)
                for j in range(PAIRS):
                    if pairs is not None:
                        pair_dve(dve, pairs[0], pairs[1], j)
                    if post is not None:
                        if j == 1:
                            post_dve_y(dve, *post)
                        if j == 4:
                            post_dve_norm(dve, *post)
                        if j == 5 and post[0] == 1:
                            post1_dve(dve, post[2], at["dec"])
                    if pre is not None and pre[0] == 1 and j == 5:
                        pre1_dve_move(dve, pre[1], pre[2], post[1] if post is not None else None)
                    if pre is not None and pre[0] == 0 and j == 4:
                        pre0_dve(dve, pre[2], post[1] if post is not None else None)
                    if pre is not None and j == (6, 1)[pre[0]]:
                        pre_dve_bc(dve, pre[0], pre[1], pairs_before(pre, pairs), at["bc"])

            rounds(dve, run)

        @block.gpsimd
        def _(pool):
            def run(pairs, post, pre, taken):
                at = taken_in(post, pre, taken)
                for j in range(PAIRS):
                    if pre is not None and pre[0] == 0 and j == 0:
                        pre0_pool(pool, pre[2])
                    if pairs is not None:
                        pair_pool(pool, pairs[0], pairs[1], j)
                    if pre is not None and j == (5, 0)[pre[0]]:
                        pre_pool_dt(pool, *pre, posts_before(pre, post), pairs_before(pre, pairs), at["dt"])
                    if post is not None and post[0] == 1 and j == 3:
                        post1_pool(pool, post[2])

            rounds(pool, run)


H, HD = 8, 16
E = 8
Q = 4
NQUAD = B // Q
TAIL = L - P
TP = 32
SLOTS = Q + 1
W5 = SLOTS * P
HS = H + 2
LAG = 2
CAP = B * L
TILES = B * L // P + E - 1
TABLE = E * CAP + (TILES + 1) * P
NO_TOKEN = 1 << 20
ROW = 2 * D + 1


def attention_and_routing(nc, prm, ident, h1_dram, rows_dram, table_dram, tile_start, tile_expert, dma, nquad=NQUAD):
    with ExitStack() as ctx:
        sb = lambda n, s, d=F32: ctx.enter_context(nc.sbuf_tensor(n, s, d))
        ps = lambda n, s, d=F32: ctx.enter_context(nc.psum_tensor(n, s, d))
        made = []

        def sem(name):
            made.append(ctx.enter_context(nc.semaphore(name)))
            return made[-1]


        w_q, w_k, w_v = sb("w_q", [D, D]), sb("w_k", [D, D]), sb("w_v", [D, D])
        w_o = sb("w_o", [D, D])
        w_op = sb("w_op", [P, 2, D])
        b_q, b_k, b_v = sb("b_q", [D, 1]), sb("b_k", [D, 1]), sb("b_v", [D, 1])
        b_vrep = sb("b_vrep", [D, P])
        b_o, ln_g, ln_b = sb("b_o", [P, D]), sb("ln1_g", [P, D]), sb("ln1_b", [P, D])
        gate_w, gate_b = sb("gate_w", [D, E]), sb("gate_b", [P, E])
        head_mask = sb("head_mask", [D, H])
        eps = sb("eps_b", [P, 1])
        below, ones = sb("below", [P, P]), sb("ones", [P, P])
        rev = sb("rev", [P, E])
        p_int, p_low, p_high = sb("p_int", [P, 1], I32), sb("p_low", [P, 1], I32), sb("p_high", [P, 1], I32)
        p_f, low_f, high_f = sb("p_f", [P, 1]), sb("low_f", [P, 1]), sb("high_f", [P, 1])
        rev_int = sb("rev_int", [P, E], I32)
        valid = sb("valid", [P, SLOTS])
        skip = sb("skip", [P, SLOTS])
        token = sb("token", [P, SLOTS])
        region = sb("region", [P, E])
        base = sb("base", [1, E])
        count, upto, count_int = sb("count", [1, E]), sb("upto", [1, E]), sb("count_int", [1, E], I32)
        past = sb("past", [1, TILES, E])
        of_tile, tile_no, tile_int = sb("of_tile", [1, TILES]), sb("tile_no", [1, TILES]), sb("tile_int", [1, TILES], I32)
        blank = sb("blank", [P, TABLE // P], I32)

        hT = [sb(f"hT{i}", [D, W5]) for i in range(2)]
        h_tok = [sb(f"h_tok{i}", [P, SLOTS, D]) for i in range(2)]
        x_tok = [sb(f"x_tok{i}", [P, SLOTS, D]) for i in range(2)]
        x_bo = [sb(f"x_bo{i}", [P, SLOTS, D]) for i in range(2)]
        qT = [sb(f"qT{i}", [D, W5]) for i in range(2)]
        kT = [sb(f"kT{i}", [D, Q, L]) for i in range(2)]
        v_main = [sb(f"v_main{i}", [P, Q, H, TP]) for i in range(2)]
        v_tail = [sb(f"v_tail{i}", [P, Q, H, TP]) for i in range(2)]
        oT = [sb(f"oT{i}", [P, 2, W5]) for i in range(2)]
        xT = sb("xT", [D, W5])
        r_tok, n_tok, g_tok = sb("r_tok", [P, SLOTS, D]), sb("n_tok", [P, SLOTS, D]), sb("g_tok", [P, SLOTS, D])
        t_tok = sb("t_tok", [P, SLOTS, D + 1])
        tT = sb("tT", [D, W5])
        stats = [sb(f"stats{i}", [P, SLOTS, 6]) for i in range(2)]
        mv = [sb(f"mv{i}", [P, SLOTS, 2]) for i in range(2)]
        lnv = [sb(f"lnv_b{i}", [P, SLOTS]) for i in range(2)]
        rstd = [sb(f"rstd_b{i}", [P, SLOTS]) for i in range(2)]
        logit, lexp, eq, onehot, place = (sb(n, [P, SLOTS, E]) for n in ("logit", "lexp", "eq", "onehot", "place"))
        lmax, lsum, first, where = (sb(n, [P, SLOTS]) for n in ("lmax", "lsum", "first", "where"))
        where_int, token_int = sb("where_int", [P, SLOTS], I32), sb("token_int", [P, SLOTS], I32)
        k_heads = [sb(f"k_heads{i}", [D, H, L]) for i in range(2)]
        e = [sb(f"e{i}", [P, HS, L]) for i in range(4)]
        p_main = [sb(f"p_main{i}", [P, HS, P]) for i in range(2)]
        p_tail = [sb(f"p_tail{i}", [P, HS + 2, TP]) for i in range(2)]
        smax, ssum, srec = (sb(n, [P, 4, HS]) for n in ("smax", "ssum", "srec"))
        pT_main = sb("pT_main", [P, HS, P])
        pT_tail = sb("pT_tail", [P, 3, P])

        s_ps = ps("s_ps", [P, 4, 512])
        m_ps = ps("m_ps", [P, 4, 512])

        s_pool, s_pe, s_dve = (sem(n) for n in ("s_pool_b", "s_pe_b", "s_dve_b"))
        (loaded,), (table_in,), (t_stored,), (placed,) = dma["loaded"], dma["table_in"], dma["t_stored"], dma["placed"]
        h_in, h_stored = dma["h_in"], dma["h_stored"]
        with nc.Block() as block:
            col = lambda v: v.rearrange("(d o) -> d o", o=1)
            row = lambda v: v.rearrange("(o d) -> o d", o=1).broadcast_to([P, v.shape[0]])
            loads = [(w_q, prm["Wq"]), (w_k, prm["Wk"]), (w_v, prm["Wv"]), (w_o, prm["Wo"]), (b_q, col(prm["bq"])),
                     (b_k, col(prm["bk"])), (b_v, col(prm["bv"])), (b_o, row(prm["bo"])), (ln_g, row(prm["ln1_g"])),
                     (ln_b, row(prm["ln1_b"])), (gate_w, prm["gate_W"]), (gate_b, row(prm["gate_b"]))]

            @block.sync
            def _(sp):
                for dst, src in loads:
                    sp.dma_start(dst[:, :], src).then_inc(loaded, 16)
                sp.wait_ge(s_dve, 1)
                for h in range(H):
                    sp.dma_start(w_op[32 * (h % 4):32 * (h % 4) + HD, h // 4, :],
                                 prm["Wo"][HD * h:HD * (h + 1), :]).then_inc(loaded, 16)
                sp.wait_ge(s_pool, 1)
                sp.dma_start(table_dram.rearrange("(p n) o -> p (n o)", p=P), blank[:, :]).then_inc(table_in, 16)

            @block.gpsimd
            def _(pool):
                nc.gpsimd.memset(blank[:, :], NO_TOKEN).then_inc(s_pool, 1)
                nc.gpsimd.memset(head_mask[:, :], 1.0).then_inc(s_pool, 1)
                nc.gpsimd.memset(ones[:, :], 1.0).then_inc(s_pool, 1)
                nc.gpsimd.iota(p_int[:, :], pattern=[[0, 1]], base=0, channel_multiplier=1).then_inc(s_pool, 1)
                nc.gpsimd.iota(rev_int[:, :], pattern=[[-1, E]], base=E, channel_multiplier=0).then_inc(s_pool, 1)
                nc.gpsimd.iota(tile_int[:, :], pattern=[[1, TILES]], base=0, channel_multiplier=0).then_inc(s_pool, 1)
                pool.wait_ge(s_pool, 6)
                pool.affine_select(out=head_mask[:, :], in_=head_mask[:, :], compare_op=ALU.is_ge, fill=0.0, base=0,
                                   pattern=[[-HD, H]], channel_multiplier=1).then_inc(s_pool, 1)
                pool.wait_ge(s_pool, 7)
                pool.affine_select(out=head_mask[:, :], in_=head_mask[:, :], compare_op=ALU.is_ge, fill=0.0,
                                   base=HD - 1, pattern=[[HD, H]], channel_multiplier=-1).then_inc(s_pool, 1)
                pool.affine_select(out=below[:, :], in_=ones[:, :], compare_op=ALU.is_ge, fill=0.0, base=-1,
                                   pattern=[[1, P]], channel_multiplier=-1).then_inc(s_pool, 1)

            @block.vector
            def _(dve):
                nc.vector.memset(w_op[:, :, :], 0.0).then_inc(s_dve, 1)
                nc.vector.memset(eps[:, :], EPS)
                for t in hT + [x for x in v_main + v_tail + p_tail]:
                    flat = t[:, :] if len(t.shape) == 2 else (t[:, :, :] if len(t.shape) == 3 else t[:, :, :, :])
                    nc.vector.memset(flat, 0.0)
                nc.vector.memset(valid[:, :], 1.0)
                nc.vector.memset(skip[:, :], 0.0)
                for k in range(E):
                    nc.vector.memset(region[:, k:k + 1], float(k * CAP))
                    nc.vector.memset(base[:, k:k + 1], float(k * CAP))
                nc.vector.memset(b_vrep[:, :], 0.0).then_inc(s_dve, 1)
                dve.wait_ge(s_pool, 9)
                nc.vector.tensor_scalar(p_low[:, :], p_int[:, :], TP - 1, None, ALU.bitwise_and).then_inc(s_dve, 1)
                nc.vector.tensor_scalar(p_high[:, :], p_int[:, :], 5, None, ALU.logical_shift_right).then_inc(s_dve, 1)
                nc.vector.tensor_copy(p_f[:, :], p_int[:, :]).then_inc(s_dve, 1)
                nc.vector.tensor_copy(tile_no[:, :], tile_int[:, :])
                nc.vector.tensor_copy(rev[:, :], rev_int[:, :]).then_inc(s_dve, 1)
                dve.wait_ge(s_dve, 6)
                nc.vector.tensor_copy(low_f[:, :], p_low[:, :]).then_inc(s_dve, 1)
                nc.vector.tensor_copy(high_f[:, :], p_high[:, :]).then_inc(s_dve, 1)
                dve.wait_ge(s_dve, 8)
                nc.vector.tensor_scalar(valid[:, Q:SLOTS], low_f[:, :], float(TAIL), None, ALU.is_lt).then_inc(s_dve, 1)
                nc.vector.tensor_scalar(skip[:, Q:SLOTS], low_f[:, :], float(TAIL), float(1 << 20), ALU.is_ge,
                                        ALU.mult).then_inc(s_dve, 1)
                for k in range(Q):
                    nc.vector.tensor_scalar(token[:, k:k + 1], p_f[:, :], float(L * k), None, ALU.add)
                nc.vector.tensor_scalar(token[:, Q:SLOTS], high_f[:, :], float(L - TP), float(P), ALU.mult,
                                        ALU.add).then_inc(s_dve, 1)
                dve.wait_ge(s_dve, 11)
                nc.vector.tensor_tensor(token[:, Q:SLOTS], token[:, Q:SLOTS], p_f[:, :], ALU.add).then_inc(s_dve, 1)
                dve.wait_ge(loaded, 16 * (len(loads) + H))
                nc.vector.tensor_scalar(b_vrep[:, :], b_vrep[:, :], b_v[:, :], None, ALU.add).then_inc(s_dve, 1)
                nc.vector.tensor_scalar(b_q[:, :], b_q[:, :], HD ** -0.5, None, ALU.mult).then_inc(s_dve, 1)
                dve.wait_ge(s_pe, 1)
                nc.vector.tensor_tensor(b_o[:, :], b_o[:, :], m_ps[:, 0, 0:D], ALU.add).then_inc(s_dve, 1)

            @block.tensor
            def _(pe):
                pe.wait_ge(s_dve, 13)
                pe.matmul(m_ps[:, 0, 0:D], b_vrep[:, :], w_o[:, :], start=True, stop=True).then_inc(s_pe, 1)

        sems = lambda names: [sem("b_" + n) for n in names.split()]
        k_ready, s_mm, s_max, s_sub, e_exp, s_sum, s_rec, p_made, pv_half, pv_mm, oT_made = sems(
            "k_ready s_mm s_max s_sub e_exp s_sum s_rec p_made pv_half pv_mm oT_made")
        pt_mm, pT_copied = sems("pt_mm pT_copied")
        h_mm, h_tok_made, st0, agg0, lnv0, rstd0, x_made, x_bo_made, x_mm, xT_made = sems(
            "h_mm h_tok_made st0 agg0 lnv0 rstd0 x_made x_bo_made x_mm xT_made")
        q_mm, qT_made, k_mm, kT_made, v_mm, v_made = sems("q_mm qT_made k_mm kT_made v_mm v_made")
        wo_mm, r_made, st1, agg1, lnv1, rstd1, n_made, g_made, t_made, t_mm, tT_made = sems(
            "wo_mm r_made st1 agg1 lnv1 rstd1 n_made g_made t_made t_mm tT_made")
        logit_mm, logit_made, lmax_made, lsub_made, lexp_made, lsum_made, gw_made = sems(
            "logit_mm logit_made lmax_made lsub_made lexp_made lsum_made gw_made")
        eq_made, eqv_made, first_made, one_made, onehot_made, rank_mm, place_made, placed_one, region_made = sems(
            "eq_made eqv_made first_made one_made onehot_made rank_mm place_made placed_one region_made")
        where_made, where_skip, where_ready, token_ready, token_next = sems(
            "where_made where_skip where_ready token_ready token_next")
        token_seen, tiles_step = sems("token_seen tiles_step")

        AHEAD = {"h": 2, "x": 1, "q": 1, "k": 1, "v": 1, "wo": -1, "t": -1, "logit": -2, "rank": -2}
        ORDER = []
        for i in range(Q):
            ORDER += [("pt", i, k) for k in range(4)] + [("pv", i, 0)]
            ORDER += {0: [("logit", 0, 0)],
                      1: [("rank", 0, 0), ("wo", 0, 0), ("wo", 0, 1), ("x", 0, 0), ("x", 0, 1)],
                      2: [("q", 0, 0), ("q", 0, 1), ("k", 0, 0), ("k", 0, 1), ("v", 0, 0), ("v", 0, 1)],
                      3: [("t", 0, 0), ("t", 0, 1), ("h", 0, 0), ("h", 0, 1)]}[i]
        assert len(ORDER) % 4 == 0
        TAKEN = {"pt": pT_copied, "pv": oT_made, "wo": r_made, "h": h_tok_made, "x": xT_made, "q": qT_made,
                 "k": kT_made, "v": v_made, "t": tT_made, "logit": logit_made, "rank": region_made}

        def runs(q, kind, i):
            if not isinstance(q, int):
                return True
            if kind in ("pt", "pv"):
                return 0 <= Q * q + i - LAG < Q * nquad
            return 0 <= q + AHEAD[kind] < nquad

        def count_of(q, kind, i, k):
            if kind == "pt":
                return 4 * (Q * q + i - LAG) + k + 1
            if kind == "pv":
                return Q * q + i - LAG + 1
            quad = q + AHEAD[kind]
            return 2 * quad + k + 1 if kind not in ("logit", "rank") else quad + 1

        def bank(kind, i, k=0):
            return ORDER.index((kind, i, k)) % 4

        def wait_bank(pe, q, kind, i, k=0):
            n = ORDER.index((kind, i, k)) - 4
            while True:
                quad = q if n >= 0 else q - 1
                before = ORDER[n]
                if runs(quad, before[0], before[1]):
                    pe.wait_ge(TAKEN[before[0]], count_of(quad, *before))
                    return
                n -= 4
                if n < -len(ORDER):
                    return

        def load_h(sp, r, par):
            at_least(sp, h_mm, 2 * (r - 1))
            sp.dma_start(hT[par][:, 0:Q * P].rearrange("d (i t) -> d i t", i=Q),
                         h1_dram[:, bass.ds(Q * r, Q), 0:P]).then_inc(h_in[par], 16)
            sp.dma_start(hT[par][:, Q * P:W5].rearrange("d (i t) -> d i t", i=Q)[:, :, 0:TAIL],
                         h1_dram[:, bass.ds(Q * r, Q), P:L]).then_inc(h_in[par], 16)

        def turn_h(pe, q, r, par):
            pe.wait_ge(h_in[par], 16 * (r - par) + 32)
            wait_bank(pe, q, "h", 0, 0)
            for s in range(Q):
                ins = pe.transpose(m_ps[:, bank("h", 0, 0), s * P:(s + 1) * P], hT[par][:, s * P:(s + 1) * P], ident[:, :])
            ins.then_inc(h_mm, 1)
            wait_bank(pe, q, "h", 0, 1)
            pe.transpose(m_ps[:, bank("h", 0, 1), 0:P], hT[par][:, Q * P:W5], ident[:, :]).then_inc(h_mm, 1)

        def copy_h(act, r, par):
            at_least(act, h_stored[par], 40 * (r - par))
            act.wait_ge(h_mm, 2 * r + 1)
            nc.scalar.activation(h_tok[par][:, 0:Q, :], m_ps[:, bank("h", 0, 0), :].rearrange("p (s d) -> p s d", s=Q),
                                 ACT.Copy).then_inc(h_tok_made, 1)
            act.wait_ge(h_mm, 2 * r + 2)
            nc.scalar.activation(h_tok[par][:, Q, :], m_ps[:, bank("h", 0, 1), 0:P], ACT.Copy).then_inc(h_tok_made, 1)

        def norm_stats(dve, src, par, n, made, st, agg):
            at_least(dve, agg, n)
            for s in range(SLOTS):
                ins = nc.vector.bn_stats(stats[par][:, s, :], src[:, s, :])
            ins.then_inc(st, 1)
            wait_apart(dve, st, n + 1, s_dve, 13)
            for s in range(SLOTS):
                ins = nc.vector.bn_aggr(mv[par][:, s, :], stats[par][:, s, :])
            ins.then_inc(agg, 1)

        def norm_rstd(act, par, n, agg, lnv_made, rstd_made, applied):
            act.wait_ge(agg, n + 1)
            at_least(act, rstd_made, n)
            nc.scalar.activation(lnv[par][:, :], mv[par][:, :, 1], ACT.Ln, bias=eps[:, :]).then_inc(lnv_made, 1)
            act.wait_ge(lnv_made, n + 1)
            at_least(act, applied, n)
            nc.scalar.activation(rstd[par][:, :], lnv[par][:, :], ACT.Exp, scale=-0.5).then_inc(rstd_made, 1)

        def norm_apply(dve, dst, src, par, n, rstd_made, applied):
            dve.wait_ge(rstd_made, n + 1)
            for s in range(SLOTS):
                ins = nc.vector.tensor_scalar(dst[:, s, :], src[:, s, :], mv[par][:, s, 0:1], rstd[par][:, s:s + 1],
                                              ALU.subtract, ALU.mult)
            ins.then_inc(applied, 1)

        def stats_x(dve, r, par):
            dve.wait_ge(h_tok_made, 2 * (r + 1))
            at_least(dve, x_made, r)
            norm_stats(dve, h_tok[par], 0, r, None, st0, agg0)

        def apply_x(dve, r, par):
            at_least(dve, x_mm, 2 * (r - 1))
            at_least(dve, x_bo_made, r - 1)
            norm_apply(dve, x_tok[par], h_tok[par], 0, r, rstd0, x_made)

        def add_bo(pool, r, par):
            pool.wait_ge(x_made, r + 1)
            at_least(pool, r_made, 2 * (r - 1))
            nc.gpsimd.tensor_tensor(x_bo[par][:, :, :], x_tok[par][:, :, :],
                                    b_o[:, :].rearrange("p (o d) -> p o d", o=1).broadcast_to([P, SLOTS, D]),
                                    ALU.add).then_inc(x_bo_made, 1)

        def turn(pe, q, kind, src, mm):
            wait_bank(pe, q, kind, 0, 0)
            for s in range(Q):
                ins = pe.transpose(m_ps[:, bank(kind, 0, 0), s * P:(s + 1) * P], src[:, s, 0:D], ident[:, :])
            ins.then_inc(mm, 1)
            wait_bank(pe, q, kind, 0, 1)
            pe.transpose(m_ps[:, bank(kind, 0, 1), 0:P], src[:, Q, 0:D], ident[:, :]).then_inc(mm, 1)

        def turn_x(pe, q, r, par):
            pe.wait_ge(x_made, r + 1)
            turn(pe, q, "x", x_tok[par], x_mm)

        def copy_turned(act, kind, dst, n, mm, copied):
            act.wait_ge(mm, 2 * n + 1)
            nc.scalar.activation(dst[:, 0:Q * P], m_ps[:, bank(kind, 0, 0), :], ACT.Copy).then_inc(copied, 1)
            act.wait_ge(mm, 2 * n + 2)
            nc.scalar.activation(dst[:, Q * P:W5], m_ps[:, bank(kind, 0, 1), 0:P], ACT.Copy).then_inc(copied, 1)

        def copy_x(act, r):
            at_least(act, v_mm, 2 * r)
            copy_turned(act, "x", xT, r, x_mm, xT_made)

        def project(pe, q, r):
            pe.wait_ge(xT_made, 2 * (r + 1))
            for kind, w, mm in (("q", w_q, q_mm), ("k", w_k, k_mm)):
                wait_bank(pe, q, kind, 0, 0)
                pe.matmul(m_ps[:, bank(kind, 0, 0), :], w[:, :], xT[:, 0:Q * P], start=True, stop=True).then_inc(mm, 1)
                wait_bank(pe, q, kind, 0, 1)
                pe.matmul(m_ps[:, bank(kind, 0, 1), 0:P], w[:, :], xT[:, Q * P:W5], start=True, stop=True).then_inc(mm, 1)
            wait_bank(pe, q, "v", 0, 0)
            for i in range(Q):
                ins = pe.matmul(m_ps[:, bank("v", 0, 0), i * P:(i + 1) * P], xT[:, i * P:(i + 1) * P], w_v[:, :],
                                start=True, stop=True)
            ins.then_inc(v_mm, 1)
            wait_bank(pe, q, "v", 0, 1)
            for i in range(Q):
                for j in range(4):
                    ins = pe.matmul(m_ps[TP * j:TP * (j + 1), bank("v", 0, 1), i * P:(i + 1) * P],
                                    xT[:, Q * P + TP * i:Q * P + TP * (i + 1)], w_v[:, :], start=True, stop=True)
            ins.then_inc(v_mm, 1)

        def copy_qk(act, r, par):
            at_least(act, s_mm, Q * (r - 1))
            for k, (dst, src) in enumerate(((qT[par][:, 0:Q * P], m_ps[:, bank("q", 0, 0), :]),
                                            (qT[par][:, Q * P:W5], m_ps[:, bank("q", 0, 1), 0:P]))):
                act.wait_ge(q_mm, 2 * r + k + 1)
                nc.scalar.activation(dst, src, ACT.Identity, scale=HD ** -0.5, bias=b_q[:, :]).then_inc(qT_made, 1)
            at_least(act, k_ready, Q * (r - 1))
            act.wait_ge(k_mm, 2 * r + 1)
            nc.scalar.activation(kT[par][:, :, 0:P], m_ps[:, bank("k", 0, 0), :].rearrange("d (i t) -> d i t", i=Q),
                                 ACT.Identity, bias=b_k[:, :]).then_inc(kT_made, 1)
            act.wait_ge(k_mm, 2 * r + 2)
            nc.scalar.activation(kT[par][:, :, P:L],
                                 m_ps[:, bank("k", 0, 1), 0:P].rearrange("d (i t) -> d i t", i=Q)[:, :, 0:TAIL],
                                 ACT.Identity, bias=b_k[:, :]).then_inc(kT_made, 1)

        def copy_v(dve, r, par):
            at_least(dve, pv_mm, Q * (r - 1))
            for k, dst in enumerate((v_main[par], v_tail[par])):
                dve.wait_ge(v_mm, 2 * r + k + 1)
                nc.vector.tensor_copy(dst[:, :, :, 0:HD],
                                      m_ps[:, bank("v", 0, k), :].rearrange("p (i h c) -> p i h c", i=Q, c=HD)
                                      ).then_inc(v_made, 1)

        def heads_of_k(pool, m, i, par, r):
            pool.wait_ge(kT_made, 2 * (r + 1))
            at_least(pool, s_mm, m - 1)
            nc.gpsimd.tensor_tensor(k_heads[i % 2][:, :, :],
                                    kT[par][:, i:i + 1, :].broadcast_to([D, H, L]),
                                    head_mask[:, :].rearrange("d (h o) -> d h o", o=1).broadcast_to([D, H, L]),
                                    ALU.mult).then_inc(k_ready, 1)

        def scores(pe, m, i, par, r):
            pe.wait_ge(k_ready, m + 1)
            if i == 0:
                pe.wait_ge(qT_made, 2 * (r + 1))
            at_least(pe, s_sub, m)
            kh = k_heads[i % 2]
            for b, (h0, h1) in enumerate(((0, 3), (3, 6), (6, 8))):
                pe.matmul(s_ps[:, b, 0:(h1 - h0) * L], qT[par][:, i * P:(i + 1) * P],
                          kh[:, h0:h1, :].rearrange("d h k -> d (h k)"), start=True, stop=True)
            for j in range(4):
                ins = pe.matmul(s_ps[TP * j:TP * (j + 1), 3, 0:2 * L], qT[par][:, Q * P + TP * i:Q * P + TP * (i + 1)],
                                kh[:, 2 * j:2 * j + 2, :].rearrange("d h k -> d (h k)"), start=True, stop=True)
            ins.then_inc(s_mm, 1)

        S_PARTS = ((0, 2, 3), (2, 4, 2))

        def softmax(dve, m, i):
            dve.wait_ge(s_mm, m + 1)
            at_least(dve, s_rec, m - 3)
            c = 0
            for b0, b1, n in S_PARTS:
                w = (b1 - b0) * n
                ins = nc.vector.tensor_reduce(smax[:, i, c:c + w].rearrange("p (b h) -> p b h", b=b1 - b0),
                                              s_ps[:, b0:b1, 0:n * L].rearrange("p b (h k) -> p b h k", h=n), AX, ALU.max)
                c += w
            ins.then_inc(s_max, 1)
            dve.wait_ge(s_max, m + 1)
            at_least(dve, p_made, m - 3)
            c = 0
            for b0, b1, n in S_PARTS:
                w = (b1 - b0) * n
                ins = nc.vector.tensor_tensor(
                    e[i][:, c:c + w, :].rearrange("p (b h) k -> p b h k", b=b1 - b0),
                    s_ps[:, b0:b1, 0:n * L].rearrange("p b (h k) -> p b h k", h=n),
                    smax[:, i, c:c + w].rearrange("p (b h o) -> p b h o", b=b1 - b0, o=1).broadcast_to([P, b1 - b0, n, L]),
                    ALU.subtract)
                c += w
            ins.then_inc(s_sub, 1)

        def exponentials(act, m, i):
            act.wait_ge(s_sub, m + 1)
            nc.scalar.activation(e[i][:, :, :], e[i][:, :, :], ACT.Exp).then_inc(e_exp, 1)

        def denominators(dve, m, i):
            dve.wait_ge(e_exp, m + 1)
            nc.vector.tensor_reduce(ssum[:, i, :], e[i][:, :, :], AX, ALU.add).then_inc(s_sum, 1)
            dve.wait_ge(s_sum, m + 1)
            at_least(dve, p_made, m - 3)
            nc.vector.reciprocal(srec[:, i, :], ssum[:, i, :]).then_inc(s_rec, 1)

        def weights(pool, m, i):
            pool.wait_ge(s_rec, m + 1)
            at_least(pool, pt_mm, 4 * (m - 1))
            for dst, k0, k1 in ((p_main[i % 2], 0, P), (p_tail[i % 2], P, L)):
                ins = nc.gpsimd.tensor_tensor(dst[:, 0:HS, 0:k1 - k0], e[i][:, :, k0:k1],
                                              srec[:, i, :].rearrange("p (h o) -> p h o", o=1).broadcast_to([P, HS, k1 - k0]),
                                              ALU.mult)
            ins.then_inc(p_made, 1)

        def turn_p(pe, q, m, slot):
            i = (slot - LAG) % Q
            pe.wait_ge(p_made, m + 1)
            main, tail = p_main[i % 2], p_tail[i % 2]
            for k in range(4):
                wait_bank(pe, q, "pt", slot, k)
                out = m_ps[:, bank("pt", slot, k), :]
                if k < 2:
                    for s in range(4):
                        ins = pe.transpose(out[:, s * P:(s + 1) * P], main[:, 4 * k + s, :], ident[:, :])
                elif k == 2:
                    for s in range(2):
                        pe.transpose(out[:, s * P:(s + 1) * P], main[:, H + s, :], ident[:, :])
                    for s in range(2):
                        ins = pe.transpose(out[:, (2 + s) * P:(3 + s) * P],
                                           tail[:, 4 * s:4 * s + 4, :].rearrange("p h k -> p (h k)"), ident[:, :])
                else:
                    ins = pe.transpose(out[:, 0:P], tail[:, H:HS + 2, :].rearrange("p h k -> p (h k)"), ident[:, :])
                ins.then_inc(pt_mm, 1)

        def copy_pT(act, m, slot):
            at_least(act, pv_mm, m)
            for k in range(4):
                act.wait_ge(pt_mm, 4 * m + k + 1)
                src = m_ps[:, bank("pt", slot, k), :]
                if k < 2:
                    nc.scalar.activation(pT_main[:, 4 * k:4 * k + 4, :], src.rearrange("p (s q) -> p s q", s=4),
                                         ACT.Copy).then_inc(pT_copied, 1)
                elif k == 2:
                    nc.scalar.activation(pT_main[:, H:HS, :], src[:, 0:2 * P].rearrange("p (s q) -> p s q", s=2), ACT.Copy)
                    nc.scalar.activation(pT_tail[:, 0:2, :], src[:, 2 * P:4 * P].rearrange("p (s q) -> p s q", s=2),
                                         ACT.Copy).then_inc(pT_copied, 1)
                else:
                    nc.scalar.activation(pT_tail[:, 2, :], src[:, 0:P], ACT.Copy).then_inc(pT_copied, 1)

        def with_v(pe, q, m, slot, par, r):
            i = (slot - LAG) % Q
            pe.wait_ge(pT_copied, 4 * (m + 1))
            if i == 0:
                pe.wait_ge(v_made, 2 * (r + 1))
            wait_bank(pe, q, "pv", slot)
            out = m_ps[:, bank("pv", slot), 0:2 * (P + TP)].rearrange("p (a t) -> p a t", a=2)
            vm, vt = v_main[par], v_tail[par]
            for h in range(H):
                j, a = h % 4, h // 4
                pe.matmul(out[TP * j:TP * (j + 1), a, 0:P], vm[:, i, h, :], pT_main[:, h, :], start=(a == 0), stop=False,
                          skip_group_check=True)
            for h in range(H):
                j, a = h % 4, h // 4
                pe.matmul(out[TP * j:TP * (j + 1), a, P:P + TP], vm[:, i, h, :],
                          pT_main[:, H + h % 2, TP * (h // 2):TP * (h // 2 + 1)], start=False, stop=False,
                          skip_group_check=True)
            for h in range(H):
                j, a = h % 4, h // 4
                ins = pe.matmul(out[TP * j:TP * (j + 1), a, 0:P], vt[TP * j:TP * (j + 1), i, h, :],
                                pT_tail[TP * j:TP * (j + 1), a, :], start=False, stop=False, skip_group_check=True)
            ins.then_inc(pv_half, 1)
            wait_apart(pe, pv_half, m + 1, s_dve, 13)
            for h in range(H):
                j, a, g = h % 4, h // 4, h % 2
                ins = pe.matmul(out[TP * j:TP * (j + 1), a, P:P + TP], vt[TP * g:TP * (g + 1), i, h, :],
                                pT_tail[TP * g:TP * (g + 1), 2, TP * (h // 2):TP * (h // 2 + 1)], start=False,
                                stop=True, skip_group_check=True)
            ins.then_inc(pv_mm, 1)

        def copy_o(act, m, slot, par, r):
            i = (slot - LAG) % Q
            act.wait_ge(pv_mm, m + 1)
            if i == 0:
                at_least(act, wo_mm, 2 * (r - 1))
            src = m_ps[:, bank("pv", slot), 0:2 * (P + TP)].rearrange("p (a t) -> p a t", a=2)
            nc.scalar.activation(oT[par][:, :, i * P:(i + 1) * P], src[:, :, 0:P], ACT.Copy)
            nc.scalar.activation(oT[par][:, :, Q * P + TP * i:Q * P + TP * (i + 1)], src[:, :, P:P + TP],
                                 ACT.Copy).then_inc(oT_made, 1)

        def output_of_heads(pe, q, r, par):
            pe.wait_ge(oT_made, Q * (r + 1))
            for k, slots in enumerate((range(Q), [Q])):
                wait_bank(pe, q, "wo", 0, k)
                for s in slots:
                    for a in range(2):
                        ins = pe.matmul(m_ps[:, bank("wo", 0, k), (s % Q) * P:(s % Q + 1) * P],
                                        oT[par][:, a, s * P:(s + 1) * P], w_op[:, a, :], start=(a == 0), stop=(a == 1))
                ins.then_inc(wo_mm, 1)

        def add_x(dve, r, par):
            dve.wait_ge(x_bo_made, r + 1)
            at_least(dve, n_made, r)
            for k, (s0, s1) in enumerate(((0, Q), (Q, SLOTS))):
                dve.wait_ge(wo_mm, 2 * r + k + 1)
                src = m_ps[:, bank("wo", 0, k), 0:(s1 - s0) * P].rearrange("p (s d) -> p s d", d=D)
                nc.vector.tensor_tensor(r_tok[:, s0:s1, :], src, x_bo[par][:, s0:s1, :], ALU.add).then_inc(r_made, 1)
            dve.wait_ge(r_made, 2 * (r + 1))
            norm_stats(dve, r_tok, 1, r, None, st1, agg1)

        def apply_r(dve, r):
            at_least(dve, g_made, r)
            norm_apply(dve, n_tok, r_tok, 1, r, rstd1, n_made)

        def gain_and_bias(pool, r):
            pool.wait_ge(n_made, r + 1)
            at_least(pool, t_made, r)
            bc = lambda v: v[:, :].rearrange("p (o d) -> p o d", o=1).broadcast_to([P, SLOTS, D])
            nc.gpsimd.tensor_tensor(g_tok[:, :, :], n_tok[:, :, :], bc(ln_g), ALU.mult).then_inc(g_made, 1)
            pool.wait_ge(g_made, r + 1)
            at_least(pool, t_mm, 2 * r)
            at_least(pool, t_stored, 80 * r)
            nc.gpsimd.tensor_tensor(t_tok[:, :, 0:D], g_tok[:, :, :], bc(ln_b), ALU.add).then_inc(t_made, 1)

        def turn_t(pe, q, r):
            pe.wait_ge(t_made, r + 1)
            turn(pe, q, "t", t_tok, t_mm)

        def copy_t(act, r):
            at_least(act, logit_mm, r)
            copy_turned(act, "t", tT, r, t_mm, tT_made)

        def gate(pe, q, r):
            pe.wait_ge(tT_made, 2 * (r + 1))
            wait_bank(pe, q, "logit", 0)
            for s in range(SLOTS):
                ins = pe.matmul(m_ps[:, bank("logit", 0), E * s:E * (s + 1)], tT[:, s * P:(s + 1) * P], gate_w[:, :],
                                start=True, stop=True)
            ins.then_inc(logit_mm, 1)

        bc_slot = lambda v: v.rearrange("p (s o) -> p s o", o=1).broadcast_to([P, SLOTS, E])
        bc_row = lambda v: v.rearrange("p (o x) -> p o x", o=1).broadcast_to([P, SLOTS, E])

        def choose(dve, r):
            dve.wait_ge(logit_mm, r + 1)
            at_least(dve, eq_made, r)
            nc.vector.tensor_tensor(logit[:, :, :], m_ps[:, bank("logit", 0), 0:SLOTS * E].rearrange("p (s x) -> p s x", x=E),
                                    bc_row(gate_b[:, :]), ALU.add).then_inc(logit_made, 1)
            dve.wait_ge(logit_made, r + 1)
            nc.vector.tensor_reduce(lmax[:, :], logit[:, :, :], AX, ALU.max).then_inc(lmax_made, 1)
            dve.wait_ge(lmax_made, r + 1)
            at_least(dve, lsum_made, r)
            nc.vector.tensor_tensor(lexp[:, :, :], logit[:, :, :], bc_slot(lmax[:, :]), ALU.subtract).then_inc(lsub_made, 1)
            at_least(dve, eqv_made, r)
            nc.vector.tensor_tensor(eq[:, :, :], logit[:, :, :], bc_slot(lmax[:, :]), ALU.is_equal).then_inc(eq_made, 1)
            dve.wait_ge(eq_made, r + 1)
            nc.vector.tensor_tensor(eq[:, :, :], eq[:, :, :], bc_row(rev[:, :]), ALU.mult).then_inc(eqv_made, 1)
            dve.wait_ge(eqv_made, r + 1)
            nc.vector.tensor_reduce(first[:, :], eq[:, :, :], AX, ALU.max).then_inc(first_made, 1)
            dve.wait_ge(first_made, r + 1)
            at_least(dve, rank_mm, r)
            at_least(dve, placed_one, r)
            nc.vector.tensor_tensor(onehot[:, :, :], bc_row(rev[:, :]), bc_slot(first[:, :]), ALU.is_equal).then_inc(one_made, 1)
            dve.wait_ge(one_made, r + 1)
            nc.vector.tensor_tensor(onehot[:, :, :], onehot[:, :, :], bc_slot(valid[:, :]), ALU.mult).then_inc(onehot_made, 1)

        def choice_exp(act, r):
            act.wait_ge(lsub_made, r + 1)
            nc.scalar.activation(lexp[:, :, :], lexp[:, :, :], ACT.Exp).then_inc(lexp_made, 1)

        def ranks(pe, q, r):
            pe.wait_ge(onehot_made, r + 1)
            wait_bank(pe, q, "rank", 0)
            out = m_ps[:, bank("rank", 0), :]
            flat = onehot[:, :, :].rearrange("p s x -> p (s x)")
            pe.matmul(out[:, 0:SLOTS * E], below[:, :], flat, start=True, stop=False, skip_group_check=True)
            for s in range(1, SLOTS):
                pe.matmul(out[:, E * s:E * SLOTS], ones[:, :], flat[:, 0:E * (SLOTS - s)], start=False, stop=True,
                          skip_group_check=True)
            for s in range(SLOTS):
                ins = pe.matmul(out[:, 64:64 + E], ones[:, :], flat[:, E * s:E * (s + 1)], start=False,
                                stop=(s == SLOTS - 1), skip_group_check=True)
            ins.then_inc(rank_mm, 1)

        def places(dve, r):
            dve.wait_ge(lexp_made, r + 1)
            nc.vector.tensor_reduce(lsum[:, :], lexp[:, :, :], AX, ALU.add).then_inc(lsum_made, 1)
            dve.wait_ge(lsum_made, r + 1)
            at_least(dve, t_stored, 80 * r)
            nc.vector.reciprocal(t_tok[:, :, D], lsum[:, :]).then_inc(gw_made, 1)
            dve.wait_ge(rank_mm, r + 1)
            out = m_ps[:, bank("rank", 0), :]
            at_least(dve, where_made, r)
            nc.vector.tensor_tensor(place[:, :, :], out[:, 0:SLOTS * E].rearrange("p (s x) -> p s x", x=E),
                                    bc_row(region[:, :]), ALU.add).then_inc(place_made, 1)
            dve.wait_ge(place_made, r + 1)
            nc.vector.tensor_tensor(region[:, :], region[:, :], out[:, 64:64 + E], ALU.add).then_inc(region_made, 1)
            nc.vector.tensor_tensor(place[:, :, :], place[:, :, :], onehot[:, :, :], ALU.mult).then_inc(placed_one, 1)
            dve.wait_ge(placed_one, r + 1)
            at_least(dve, where_skip, r)
            nc.vector.tensor_reduce(where[:, :], place[:, :, :], AX, ALU.add).then_inc(where_made, 1)
            dve.wait_ge(where_made, r + 1)
            at_least(dve, placed, 16 * SLOTS * r)
            nc.vector.tensor_tensor(where_int[:, :], where[:, :], skip[:, :], ALU.add).then_inc(where_skip, 1)
            at_least(dve, token_next, r)
            nc.vector.tensor_copy(token_int[:, :], token[:, :]).then_inc(token_ready, 1)
            dve.wait_ge(token_ready, r + 1)
            nc.vector.tensor_scalar(token[:, :], token[:, :], float(Q * L), None, ALU.add).then_inc(token_next, 1)

        def store_h(sp, r, par):
            rows = rows_dram.rearrange("(i t) c -> t i c", t=L)
            sp.wait_ge(h_tok_made, 2 * (r + 1))
            sp.dma_start(rows[0:P, bass.ds(Q * r, Q), D + 1:ROW], h_tok[par][:, 0:Q, :]).then_inc(h_stored[par], 16)
            for i in range(Q):
                sp.dma_start(rows[P:L, bass.ds(Q * r + i, 1), D + 1:ROW],
                             h_tok[par][TP * i:TP * i + TAIL, Q:SLOTS, :]).then_inc(h_stored[par], 16)

        def store_t(sp, r):
            rows = rows_dram.rearrange("(i t) c -> t i c", t=L)
            sp.wait_ge(t_made, r + 1)
            sp.wait_ge(gw_made, r + 1)
            sp.dma_start(rows[0:P, bass.ds(Q * r, Q), 0:D + 1], t_tok[:, 0:Q, :]).then_inc(t_stored, 16)
            for i in range(Q):
                sp.dma_start(rows[P:L, bass.ds(Q * r + i, 1), 0:D + 1],
                             t_tok[TP * i:TP * i + TAIL, Q:SLOTS, :]).then_inc(t_stored, 16)

        def put_tokens(pool, r):
            last = pool.to_reg(E * CAP - 1)
            pool.wait_ge(token_ready, r + 1)
            pool.sem_inc(token_seen, 1)
            for s in range(SLOTS):
                pool.indirect_dma_start(table_dram, bass.IndirectOffsetOnAxis(where_int[:, s:s + 1], 0),
                                        token_int[:, s:s + 1], None, bounds_check=last,
                                        oob_is_err=False).then_inc(placed, 16)

        def quads(eng, body):
            for q in range(-2, 4):
                body(q, q % 2)
            with eng.Fori(2, nquad // 2 - 2) as k:
                body(2 * k, 0)
                body(2 * k + 1, 1)
            for q in range(nquad - 4, nquad + 2):
                body(q, q % 2)

        def within(v, lo, hi):
            return not isinstance(v, int) or lo <= v < hi

        def tiles_of_experts(dve):
            num = [0]

            def step(ins):
                ins.then_inc(tiles_step, 1)
                num[0] += 1
                dve.wait_ge(tiles_step, num[0])

            over_e = lambda v: v.rearrange("p (o x) -> p o x", o=1).broadcast_to([1, TILES, E])
            over_j = lambda v: v.rearrange("p (j o) -> p j o", o=1).broadcast_to([1, TILES, E])
            dve.wait_ge(region_made, nquad)
            step(nc.vector.tensor_tensor(count[:, :], region[0:1, :], base[:, :], ALU.subtract))
            step(nc.vector.tensor_scalar(count[:, :], count[:, :], float(P - 1), None, ALU.add))
            step(nc.vector.tensor_copy(count_int[:, :], count[:, :]))
            step(nc.vector.tensor_scalar(count_int[:, :], count_int[:, :], 7, None, ALU.logical_shift_right))
            step(nc.vector.tensor_copy(count[:, :], count_int[:, :]))
            step(nc.vector.tensor_tensor_scan(upto[:, :], ones[0:1, 0:E], count[:, :], 0.0, ALU.mult, ALU.add))
            step(nc.vector.tensor_scalar(count[:, :], count[:, :], -float(P), float(CAP), ALU.mult, ALU.add))
            step(nc.vector.tensor_tensor(past[:, :, :], over_j(tile_no[:, :]), over_e(upto[:, :]), ALU.is_ge))
            step(nc.vector.tensor_reduce(of_tile[:, :], past[:, :, :], AX, ALU.add))
            step(nc.vector.tensor_scalar(of_tile[:, :], of_tile[:, :], float(E - 1), None, ALU.min))
            step(nc.vector.tensor_copy(tile_expert[:, :], of_tile[:, :]))
            step(nc.vector.tensor_tensor(past[:, :, :], past[:, :, :], over_e(count[:, :]), ALU.mult))
            step(nc.vector.tensor_reduce(of_tile[:, :], past[:, :, :], AX, ALU.add))
            step(nc.vector.tensor_scalar(tile_no[:, :], tile_no[:, :], float(P), None, ALU.mult))
            step(nc.vector.tensor_tensor(of_tile[:, :], of_tile[:, :], tile_no[:, :], ALU.add))
            step(nc.vector.tensor_copy(tile_start[:, :], of_tile[:, :]))

        ctx.callback(clear, nc, made)
        block = ctx.enter_context(nc.Block())

        @block.sync
        def _(sp):
            def body(q, par):
                if within(q + 3, 0, nquad):
                    load_h(sp, q + 3, 1 - par)
                if within(q - 2, 0, nquad):
                    store_t(sp, q - 2)
                if within(q + 2, 0, nquad):
                    store_h(sp, q + 2, par)

            sp.wait_ge(table_in, 16)
            load_h(sp, 0, 0)
            quads(sp, body)
            sp.wait_ge(h_stored[0], 40 * nquad)
            sp.wait_ge(h_stored[1], 40 * nquad)
            sp.wait_ge(t_stored, 80 * nquad)

        def images(q, par):
            inside = lambda m: m if within(m, 0, Q * nquad) else None
            for slot in range(Q):
                m = Q * q + slot
                yield (slot, inside(m), inside(m - 1), inside(m + 1), inside(m - LAG),
                       1 - par if slot < LAG else par, q - 1 if slot < LAG else q)

        def near(q):
            return (within(q + d, 0, nquad) for d in (2, 1, -1, -2))

        @block.tensor
        def _(pe):
            def body(q, par):
                next2, next1, last1, last2 = near(q)
                for slot, m, _, _, back, bpar, br in images(q, par):
                    if m is not None:
                        scores(pe, m, slot, par, q)
                    if back is not None:
                        turn_p(pe, q, back, slot)
                        with_v(pe, q, back, slot, bpar, br)
                    if slot == 0 and last2:
                        gate(pe, q, q - 2)
                    if slot == 1 and last2:
                        ranks(pe, q, q - 2)
                    if slot == 1 and last1:
                        output_of_heads(pe, q, q - 1, 1 - par)
                    if slot == 1 and next1:
                        turn_x(pe, q, q + 1, 1 - par)
                    if slot == 2 and next1:
                        project(pe, q, q + 1)
                    if slot == 3 and last1:
                        turn_t(pe, q, q - 1)
                    if slot == 3 and next2:
                        turn_h(pe, q, q + 2, par)

            quads(pe, body)

        @block.scalar
        def _(act):
            def body(q, par):
                next2, next1, last1, last2 = near(q)
                for slot, m, _, _, back, bpar, br in images(q, par):
                    if back is not None:
                        copy_pT(act, back, slot)
                    if slot == 1 and last2:
                        choice_exp(act, q - 2)
                    if m is not None:
                        exponentials(act, m, slot)
                    if back is not None:
                        copy_o(act, back, slot, bpar, br)
                    if slot == 0 and next1:
                        norm_rstd(act, 0, q + 1, agg0, lnv0, rstd0, x_made)
                    if slot == 1 and next1:
                        copy_x(act, q + 1)
                    if slot == 2 and last1:
                        norm_rstd(act, 1, q - 1, agg1, lnv1, rstd1, n_made)
                    if slot == 2 and next1:
                        copy_qk(act, q + 1, 1 - par)
                    if slot == 3 and last1:
                        copy_t(act, q - 1)
                    if slot == 3 and next2:
                        copy_h(act, q + 2, par)

            act.preload_act_table_set(EXP_LN_SET)
            quads(act, body)

        @block.vector
        def _(dve):
            def body(q, par):
                next2, next1, last1, last2 = near(q)
                for slot, m, before, _, _, _, _ in images(q, par):
                    if m is not None:
                        softmax(dve, m, slot)
                    if slot == 0 and next1:
                        stats_x(dve, q + 1, 1 - par)
                    if slot == 2 and last1:
                        add_x(dve, q - 1, 1 - par)
                    if slot == 3 and next1:
                        copy_v(dve, q + 1, 1 - par)
                    if before is not None:
                        denominators(dve, before, (slot - 1) % Q)
                    if slot == 0 and next1:
                        apply_x(dve, q + 1, 1 - par)
                    if slot == 0 and last2:
                        choose(dve, q - 2)
                    if slot == 1 and last2:
                        places(dve, q - 2)
                    if slot == 2 and last1:
                        apply_r(dve, q - 1)

            quads(dve, body)
            tiles_of_experts(dve)

        @block.gpsimd
        def _(pool):
            def body(q, par):
                next2, next1, last1, last2 = near(q)
                for slot, _, before, after, _, _, _ in images(q, par):
                    if after is not None:
                        heads_of_k(pool, after, (slot + 1) % Q, 1 - par if slot == Q - 1 else par,
                                   q + 1 if slot == Q - 1 else q)
                    if slot == 3 and last1:
                        gain_and_bias(pool, q - 1)
                    if before is not None:
                        weights(pool, before, (slot - 1) % Q)
                    if slot == 2 and last2:
                        put_tokens(pool, q - 2)
                    if slot == 3 and next1:
                        add_bo(pool, q + 1, 1 - par)

            pool.wait_ge(table_in, 16)
            quads(pool, body)
            pool.wait_ge(placed, 16 * SLOTS * nquad)


FF = 4 * D
FC = FF // P
RINGT = 8


def dma_semaphores(nc, ctx):
    counts = dict(proj_stored=2, loaded=1, table_in=1, t_stored=1, placed=1, h_in=2, h_stored=2, weights_in=1,
                  place_in=RINGT, row_in=RINGT, out_put=2)
    return {name: [ctx.enter_context(nc.semaphore(f"{name}_{i}")) for i in range(n)] for name, n in counts.items()}


def chosen_experts(nc, prm, ident, rows_dram, table_dram, tile_start, tile_expert, out, dma, tiles=TILES):
    with ExitStack() as ctx:
        sb = lambda n, s, d=F32: ctx.enter_context(nc.sbuf_tensor(n, s, d))
        ps = lambda n, s, d=F32: ctx.enter_context(nc.psum_tensor(n, s, d))
        sems = lambda names: [ctx.enter_context(nc.semaphore("c_" + n)) for n in names.split()]

        w1, b1 = sb("w1", [D, E * FF]), sb("b1", [P, E * FF])
        w2, b2 = sb("w2", [P, E * FC * D]), sb("b2", [P, E * D])
        place = [sb(f"place_c{i}", [P, 1], I32) for i in range(RINGT)]
        rows = [sb(f"rows_c{i}", [P, ROW]) for i in range(RINGT)]
        tT = [sb(f"tT_c{i}", [D, P]) for i in range(2)]
        pre = [sb(f"pre{i}", [P, FF]) for i in range(2)]
        hid = [sb(f"hid{i}", [P, FF]) for i in range(2)]
        hidT = [sb(f"hidT{i}", [P, FF]) for i in range(2)]
        ffn = [sb(f"ffn{i}", [P, D]) for i in range(2)]
        res = [sb(f"res_c{i}", [P, D]) for i in range(2)]
        t_ps = [ps(f"t_ps{i}", [P, 512]) for i in range(2)]
        h_ps = [ps(f"h_ps{i}", [P, FF]) for i in range(2)]
        hT_ps = [ps(f"hT_ps{i}", [P, FF]) for i in range(2)]
        o_ps = [ps(f"o_ps{i}", [P, 512]) for i in range(2)]

        weights_in = dma["weights_in"][0]
        cleared, t_turned, tT_made, h_mm, pre_made, hid_made, h_turned, hidT_made, o_mm, ffn_made, res_made, place_seen, res_seen = sems(
            "cleared t_turned tT_made h_mm pre_made hid_made h_turned hidT_made o_mm ffn_made res_made place_seen res_seen")
        place_in, row_in, out_put = dma["place_in"], dma["row_in"], dma["out_put"]

        def steps(eng, parts):
            def body(s, r):
                for part, delay in parts:
                    j = s - delay
                    if not isinstance(j, int) or 0 <= j < tiles:
                        part(eng, j, (r - delay) % RINGT)
            for s in range(RINGT):
                body(s, s)
            with eng.Fori(1, tiles // RINGT - 1) as k:
                for r in range(RINGT):
                    body(RINGT * k + r, r)
            for s in range(tiles - RINGT, tiles + parts[-1][1]):
                body(s, s % RINGT)

        turns = 16 // RINGT

        def load_place(sp, j, r):
            if not isinstance(j, int) or j >= RINGT:
                sp.wait_ge(out_put[r % 2], 8 * (j - RINGT - r % 2) + 16)
            start = sp.value_load(tile_start[0:1, bass.ds(j, 1)], min_val=0, max_val=TABLE - P)
            sp.dma_start(place[r][:, :], table_dram[bass.ds(start, P), :]).then_inc(place_in[r], 16)

        def gather(pool, j, r):
            last = pool.to_reg(B * L - 1)
            pool.wait_ge(place_in[r], turns * (j - r) + 16)
            pool.sem_inc(place_seen, 1)
            pool.indirect_dma_start(rows[r][:, :], None, rows_dram, bass.IndirectOffsetOnAxis(place[r][:, 0:1], 0),
                                    bounds_check=last, oob_is_err=False).then_inc(row_in[r], 16)

        def put(pool, j, r):
            last = pool.to_reg(B * L - 1)
            pool.wait_ge(res_made, j + 1)
            pool.sem_inc(res_seen, 1)
            pool.indirect_dma_start(out, bass.IndirectOffsetOnAxis(place[r][:, 0:1], 0), res[r % 2][:, :], None,
                                    bounds_check=last, oob_is_err=False).then_inc(out_put[r % 2], 16)

        def turn_t(pe, j, r):
            pe.wait_ge(row_in[r], turns * (j - r) + 16)
            at_least(pe, tT_made, j - 1)
            pe.transpose(t_ps[r % 2][:, 0:P], rows[r][:, 0:D], ident[:, :]).then_inc(t_turned, 1)

        def copy_t(act, j, r):
            act.wait_ge(t_turned, j + 1)
            at_least(act, h_mm, j - 1)
            nc.scalar.activation(tT[r % 2][:, :], t_ps[r % 2][:, 0:P], ACT.Copy).then_inc(tT_made, 1)

        def hidden(pe, j, r):
            e = pe.value_load(tile_expert[0:1, bass.ds(j, 1)], min_val=0, max_val=E - 1)
            pe.wait_ge(tT_made, j + 1)
            at_least(pe, pre_made, j - 1)
            pe.matmul(h_ps[r % 2][:, :], tT[r % 2][:, :], w1[:, bass.ds(e * FF, FF)], start=True, stop=True).then_inc(h_mm, 1)

        def add_b1(dve, j, r):
            e = dve.value_load(tile_expert[0:1, bass.ds(j, 1)], min_val=0, max_val=E - 1)
            dve.wait_ge(h_mm, j + 1)
            at_least(dve, hid_made, j - 1)
            nc.vector.tensor_tensor(pre[r % 2][:, :], h_ps[r % 2][:, :], b1[:, bass.ds(e * FF, FF)], ALU.add).then_inc(pre_made, 1)

        def gelu(act, j, r):
            act.wait_ge(pre_made, j + 1)
            at_least(act, h_turned, j - 1)
            nc.scalar.activation(hid[r % 2][:, :], pre[r % 2][:, :], ACT.Gelu_apprx_tanh).then_inc(hid_made, 1)

        def turn_hidden(pe, j, r):
            pe.wait_ge(hid_made, j + 1)
            at_least(pe, hidT_made, j - 1)
            for c in range(FC):
                ins = pe.transpose(hT_ps[r % 2][:, c * P:(c + 1) * P], hid[r % 2][:, c * P:(c + 1) * P], ident[:, :])
            ins.then_inc(h_turned, 1)

        def copy_hidden(act, j, r):
            act.wait_ge(h_turned, j + 1)
            at_least(act, o_mm, j - 1)
            nc.scalar.activation(hidT[r % 2][:, :], hT_ps[r % 2][:, :], ACT.Copy).then_inc(hidT_made, 1)

        def output(pe, j, r):
            e = pe.value_load(tile_expert[0:1, bass.ds(j, 1)], min_val=0, max_val=E - 1)
            pe.wait_ge(hidT_made, j + 1)
            at_least(pe, ffn_made, j - 1)
            for c in range(FC):
                ins = pe.matmul(o_ps[r % 2][:, 0:D], hidT[r % 2][:, c * P:(c + 1) * P],
                                w2[:, bass.ds(e * (FC * D) + c * D, D)], start=(c == 0), stop=(c == FC - 1))
            ins.then_inc(o_mm, 1)

        def add_b2(dve, j, r):
            e = dve.value_load(tile_expert[0:1, bass.ds(j, 1)], min_val=0, max_val=E - 1)
            dve.wait_ge(o_mm, j + 1)
            at_least(dve, res_made, j - 1)
            nc.vector.tensor_tensor(ffn[r % 2][:, :], o_ps[r % 2][:, 0:D], b2[:, bass.ds(e * D, D)], ALU.add).then_inc(ffn_made, 1)
            dve.wait_ge(ffn_made, j + 1)
            if not isinstance(j, int) or j >= 2:
                dve.wait_ge(out_put[r % 2], 8 * (j - r % 2))
            nc.vector.scalar_tensor_tensor(out=res[r % 2][:, :], in0=ffn[r % 2][:, :], scalar=rows[r][:, D:D + 1],
                                           in1=rows[r][:, D + 1:ROW], op0=ALU.mult, op1=ALU.add).then_inc(res_made, 1)

        block = ctx.enter_context(nc.Block())

        @block.sync
        def _(sp):
            sp.dma_start(w1[:, :].rearrange("d (e f) -> d e f", e=E), prm["W1"].rearrange("e d f -> d e f")).then_inc(weights_in, 16)
            steps(sp, [(load_place, 0)])

        @block.scalar
        def _(act):
            bc = lambda v, n: v.rearrange("e f -> (e f)").rearrange("(o n) -> o n", o=1).broadcast_to([P, n])
            act.dma_start(b1[:, :], bc(prm["b1"], E * FF)).then_inc(weights_in, 16)
            act.dma_start(b2[:, :], bc(prm["b2"], E * D)).then_inc(weights_in, 16)
            act.dma_start(w2[:, :].rearrange("p (e c d) -> p e c d", e=E, c=FC),
                          prm["W2"].rearrange("e (c p) d -> p e c d", p=P)).then_inc(weights_in, 16)
            steps(act, [(copy_t, 3), (gelu, 4), (copy_hidden, 5)])

        @block.gpsimd
        def _(pool):
            pool.wait_ge(cleared, 1)
            steps(pool, [(gather, 1), (put, 7)])
            for i in range(2):
                pool.wait_ge(out_put[i], 8 * tiles)

        @block.tensor
        def _(pe):
            pe.wait_ge(weights_in, 64)
            steps(pe, [(turn_t, 3), (hidden, 4), (turn_hidden, 5), (output, 6)])

        @block.vector
        def _(dve):
            for r in rows:
                ins = nc.vector.memset(r[:, :], 0.0)
            ins.then_inc(cleared, 1)
            dve.wait_ge(weights_in, 64)
            steps(dve, [(add_b1, 4), (add_b2, 6)])


def vit_tower(nc, x, cls_tok, tok_W, tok_b, tok_cls_token, tok_pos_emb, A_log, W_B, b_B, W_C, b_C, W_dt, b_dt, D_skip,
              W_mix, b_mix, ln_g, ln_b, W_dec, b_dec, ln1_g, ln1_b, Wq, bq, Wk, bk, Wv, bv, Wo, bo, gate_W, gate_b,
              W1, b1, W2, b2, out):
    proj_dram = nc.dram_tensor("proj", [D, PW, B, PH], F32).ap()
    h1_dram = nc.dram_tensor("h1", [D, B, L], F32).ap()
    rows_dram = nc.dram_tensor("rows", [B * L, ROW], F32).ap()
    table_dram = nc.dram_tensor("table", [TABLE, 1], I32).ap()
    with ExitStack() as ctx:
        ident = ctx.enter_context(nc.sbuf_tensor("ident", [P, P], F32))
        tile_start = ctx.enter_context(nc.sbuf_tensor("tile_start", [1, TILES], I32))
        tile_expert = ctx.enter_context(nc.sbuf_tensor("tile_expert", [1, TILES], I32))
        identity_ready = ctx.enter_context(nc.semaphore("identity_ready"))
        dma = dma_semaphores(nc, ctx)

        with nc.Block() as block:
            @block.gpsimd
            def _(pool):
                nc.gpsimd.memset(ident[:, :], 0.0).then_inc(identity_ready, 1)
                pool.wait_ge(identity_ready, 1)
                pool.affine_select(out=ident[:, :], in_=ident[:, :], compare_op=ALU.not_equal, fill=1.0, base=0,
                                   pattern=[[-1, P]], channel_multiplier=1).then_inc(identity_ready, 1)

        embed_patches(nc, x, tok_W, identity_ready, ident, proj_dram, dma["proj_stored"])
        ssm_layers(nc, dict(W_B=W_B, W_C=W_C, b_B=b_B, b_C=b_C, A_log=A_log, W_dt=W_dt, W_mix=W_mix, W_dec=W_dec,
                            pos=tok_pos_emb, b_tok=tok_b, b_dec=b_dec, cls0=cls_tok, cls1=tok_cls_token, b_dt=b_dt,
                            b_mix=b_mix, D_skip=D_skip, ln_g=ln_g, ln_b=ln_b), ident, proj_dram, h1_dram)
        attention_and_routing(nc, dict(ln1_g=ln1_g, ln1_b=ln1_b, Wq=Wq, bq=bq, Wk=Wk, bk=bk, Wv=Wv, bv=bv, Wo=Wo, bo=bo,
                                       gate_W=gate_W, gate_b=gate_b), ident, h1_dram, rows_dram, table_dram,
                              tile_start, tile_expert, dma)
        chosen_experts(nc, dict(W1=W1, b1=b1, W2=W2, b2=b2), ident, rows_dram, table_dram, tile_start, tile_expert,
                       out.rearrange("b t d -> (b t) d"), dma)


_INS = ['x', 'cls_tok', 'L0_tok_W', 'L0_tok_b', 'L0_tok_cls_token', 'L0_tok_pos_emb', 'L0_attn_A_log', 'L0_attn_W_B',
        'L0_attn_b_B', 'L0_attn_W_C', 'L0_attn_b_C', 'L0_attn_W_dt', 'L0_attn_b_dt', 'L0_attn_D_skip', 'L0_attn_W_mix',
        'L0_attn_b_mix', 'L0_attn_ln_g', 'L0_attn_ln_b', 'L0_attn_W_dec', 'L0_attn_b_dec', 'L0_ffn_ln1_g', 'L0_ffn_ln1_b',
        'L0_ffn_Wq', 'L0_ffn_bq', 'L0_ffn_Wk', 'L0_ffn_bk', 'L0_ffn_Wv', 'L0_ffn_bv', 'L0_ffn_Wo', 'L0_ffn_bo',
        'L0_ffn_gate_W', 'L0_ffn_gate_b', 'L0_ffn_W1', 'L0_ffn_b1', 'L0_ffn_W2', 'L0_ffn_b2']
_OUTS = [((128, 145, 128), 'float32')]


def kernel(**inputs):
    import numpy as _np
    import concourse.bacc as _bacc
    from concourse import mybir as _mybir
    from concourse.bass_utils import run_bass_kernel_spmd as _run

    nc = _bacc.Bacc("TRN2", target_bir_lowering=False, num_devices=1)
    arrays, args = {}, []
    for name in _INS:
        a = _np.ascontiguousarray(inputs[name])
        arrays[f"in_{name}_dram"] = a
        args.append(nc.dram_tensor(f"in_{name}_dram", a.shape, _mybir.dt.from_np(a.dtype), kind="ExternalInput").ap())
    for i, (shape, dtype) in enumerate(_OUTS):
        dt = _mybir.dt.from_np(_np.dtype(dtype))
        args.append(nc.dram_tensor(f"out_{i}_dram", shape, dt, kind="ExternalOutput").ap())
    vit_tower(nc, *args)
    r = _run(nc, [arrays], core_ids=[0])
    got = tuple(r.results[0][f"out_{i}_dram"] for i in range(len(_OUTS)))
    return got[0]
```

```python
from contextlib import ExitStack

import concourse.bass as bass
from concourse import mybir

ALU = mybir.AluOpType
ACT = mybir.ActivationFunctionType
F32 = mybir.dt.float32
BF16 = mybir.dt.bfloat16
I32 = mybir.dt.int32
U32 = mybir.dt.uint32
AX = mybir.AxisListType.X

P = 128
D = 128
B = 128
CH, PSZ = 3, 16
PW, PH = 11, 13
NPATCH = PW * PH
L = NPATCH + 2
NST = 16
EPS = 1e-5


def at_least(eng, sem, value):
    if isinstance(value, int) and value <= 0:
        return
    eng.wait_ge(sem, value)


def clear(nc, semaphores):
    with nc.Block() as block:
        @block.gpsimd
        def _(pool):
            for s in semaphores:
                pool.sem_clear(s)


def wait_apart(eng, sem, value, met, met_value):
    if not isinstance(value, int):
        value = eng.snap(value)
    eng.wait_ge(met, met_value)
    eng.wait_ge(sem, value)


def embed_patches(nc, x, W, identity_ready, ident, proj_dram, stored):
    SLAB = PSZ * PH * PSZ
    KC = CH * 2
    PIX = CH * PSZ * PSZ
    NBLK = [4, 4, 4, 1]
    NB = len(NBLK)
    TURNS = NB * KC
    HALF = KC // 2
    with ExitStack() as ctx:
        sb = lambda n, s, d=F32: ctx.enter_context(nc.sbuf_tensor(n, s, d))
        ps = lambda n, s, d=F32: ctx.enter_context(nc.psum_tensor(n, s, d))
        made = []

        def sem(name):
            made.append(ctx.enter_context(nc.semaphore(name)))
            return made[-1]

        slab = [sb(f"slab{i}", [B, CH, SLAB]) for i in range(2)]
        patches = sb("patches", [B, PH, PIX])
        w_rows = sb("w_rows", [D, KC * P])
        w_order = sb("w_order", [D, KC * P])
        w_t = sb("w_t", [P, KC, D])
        pix = [sb(f"pix{i}", [P, KC, 4 * P]) for i in range(2)]
        res = [sb(f"res{i}", [D, B, PH]) for i in range(2)]
        tp = ps("tp", [P, 4, 512])
        acc = ps("acc", [P, 2, 512])
        slab_in = [sem(f"slab_in{i}") for i in range(2)]
        w_in, w_ordered, w_turned, w_copied = sem("w_in"), sem("w_ordered"), sem("w_turned"), sem("w_copied")
        ordered, turned = sem("ordered"), sem("turned")
        pix_even, pix_odd = sem("pix_even"), sem("pix_odd")
        acc_done, acc_copied = sem("acc_done"), sem("acc_copied")
        xs = x.rearrange("b c (w q) j -> w b c (q j)", q=PSZ)
        out = proj_dram.rearrange("d w b h -> w d (b h)")

        def steps(eng, body):
            for t in (0, 1, 2):
                body(t, t % 2, t // 2)
            with eng.Fori(1, PW // 2 - 1) as k:
                body(2 * k + 1, 1, k)
                body(2 * k + 2, 0, k + 1)
            for t in (PW - 2, PW - 1):
                body(t, t % 2, t // 2)

        ctx.callback(clear, nc, made)
        block = ctx.enter_context(nc.Block())

        @block.sync
        def _(sp):
            sp.dma_start(w_rows[:, :], W).then_inc(w_in, 16)
            sp.dma_start(slab[0][:, :, :], xs[0]).then_inc(slab_in[0], 16)
            sp.dma_start(slab[1][:, :, :], xs[1]).then_inc(slab_in[1], 16)
            with sp.Fori(0, PW // 2 - 1) as k:
                sp.wait_ge(ordered, (2 * k + 1) * NB)
                sp.dma_start(slab[0][:, :, :], xs[2 * k + 2]).then_inc(slab_in[0], 16)
                sp.wait_ge(ordered, (2 * k + 2) * NB)
                sp.dma_start(slab[1][:, :, :], xs[2 * k + 3]).then_inc(slab_in[1], 16)
            sp.wait_ge(ordered, (PW - 2) * NB)
            sp.dma_start(slab[0][:, :, :], xs[PW - 1]).then_inc(slab_in[0], 16)

        @block.tensor
        def _(pe):
            pe.wait_ge(w_ordered, 1)
            at_least(pe, identity_ready, 2)
            for k in range(KC):
                ins = pe.transpose(tp[:, k // 4, (k % 4) * P:(k % 4 + 1) * P], w_order[:, k * P:(k + 1) * P], ident[:, :])
            ins.then_inc(w_turned, 1)
            pe.wait_ge(w_copied, 1)

            def product(n, blk, k):
                nph = NBLK[blk]
                pe.wait_ge(pix_odd if k % 2 else pix_even, HALF * n + k // 2 + 1)
                if k == 0:
                    at_least(pe, acc_copied, n - 1)
                ins = pe.matmul(acc[:, blk % 2, 0:nph * P], w_t[:, k, :], pix[blk % 2][:, k, 0:nph * P],
                                start=(k == 0), stop=(k == KC - 1))
                if k == KC - 1:
                    ins.then_inc(acc_done, 1)

            def step(t, par, before):
                col = 0
                for blk, nph in enumerate(NBLK):
                    n = t * NB + blk
                    pe.wait_ge(ordered, n + 1)
                    for k in range(KC):
                        at_least(pe, pix_odd if k % 2 else pix_even, HALF * n + k // 2 - 1)
                        for j in range(nph):
                            ins = pe.transpose(tp[:, (blk * KC + k) % 4, j * P:(j + 1) * P],
                                               patches[:, col + j, k * P:(k + 1) * P], ident[:, :])
                        ins.then_inc(turned, 1)
                        if blk or not isinstance(t, int) or t:
                            product(n - 1, (blk - 1) % NB, k)
                    col += nph

            steps(pe, step)
            for k in range(KC):
                product(PW * NB - 1, NB - 1, k)

        @block.vector
        def _(dve):
            dve.wait_ge(w_in, 16)
            nc.vector.tensor_copy(w_order[:, :].rearrange("d (c q) -> d c q", c=CH),
                                  w_rows[:, :].rearrange("d (q c) -> d c q", c=CH)).then_inc(w_ordered, 1)
            dve.wait_ge(w_turned, 1)
            nc.vector.tensor_copy(w_t[:, :, :].rearrange("p k d -> p (k d)"),
                                  tp[:, 0:2, :].rearrange("p a b -> p (a b)")[:, 0:KC * P]).then_inc(w_copied, 1)

            def order(t, par, before, blk):
                c0, nph = 4 * blk, NBLK[blk]
                if blk == 0:
                    dve.wait_ge(slab_in[par], 16 * (before + 1))
                at_least(dve, turned, (t - 1) * TURNS + (blk + 1) * KC)
                nc.vector.tensor_copy(
                    patches[:, c0:c0 + nph, :].rearrange("b j (q e) -> b j q e", e=PSZ),
                    slab[par][:, :, :].rearrange("b c (q j e) -> b j (c q) e", j=PH, e=PSZ)[:, c0:c0 + nph],
                ).then_inc(ordered, 1)

            def step(t, par, before):
                for blk, nph in enumerate(NBLK):
                    n = t * NB + blk
                    at_least(dve, acc_done, n - 1)
                    for k in range(0, KC, 2):
                        dve.wait_ge(turned, n * KC + k + 1)
                        nc.vector.tensor_copy(pix[blk % 2][:, k, 0:nph * P],
                                              tp[:, (blk * KC + k) % 4, 0:nph * P]).then_inc(pix_even, 1)
                    if not isinstance(t, int) or t + 1 < PW:
                        order(t + 1, 1 - par, before + par, blk)

            for blk in range(NB):
                order(0, 0, 0, blk)
            steps(dve, step)

        @block.scalar
        def _(act):
            def take_product(n, blk, par, before):
                nph, col = NBLK[blk], 4 * blk
                act.wait_ge(acc_done, n + 1)
                if blk == 0:
                    at_least(act, stored[par], 16 * before)
                nc.scalar.activation(res[par][:, :, col:col + nph].rearrange("p r c -> p c r"),
                                     acc[:, blk % 2, 0:nph * P].rearrange("p (c r) -> p c r", r=B),
                                     ACT.Copy).then_inc(acc_copied, 1)

            def step(t, par, before):
                for blk, nph in enumerate(NBLK):
                    n = t * NB + blk
                    at_least(act, acc_done, n - 1)
                    for k in range(1, KC, 2):
                        act.wait_ge(turned, n * KC + k + 1)
                        nc.scalar.activation(pix[blk % 2][:, k, 0:nph * P], tp[:, (blk * KC + k) % 4, 0:nph * P],
                                             ACT.Copy).then_inc(pix_odd, 1)
                    if blk:
                        take_product(n - 1, blk - 1, par, before)
                    elif not isinstance(t, int) or t:
                        take_product(n - 1, NB - 1, 1 - par, None)

            steps(act, step)
            take_product(PW * NB - 1, NB - 1, (PW - 1) % 2, None)

        @block.gpsimd
        def _(pool):
            def step(t, par, before):
                pool.wait_ge(acc_copied, (t + 1) * NB)
                pool.dma_start(out[t], res[par][:, :, :].rearrange("p b h -> p (b h)")).then_inc(stored[par], 16)

            steps(pool, step)
            pool.wait_ge(stored[0], 16 * (PW // 2 + 1))
            pool.wait_ge(stored[1], 16 * (PW // 2))


G = 3
T = G * L
NGROUP = -(-B // G)
PAIRS = NST // 2
RING = 4
DVE_PAIRS = (3,)
AT = dict(center=1, var0=2, y=1, gelu=2, mix=3, res=3, var=4, norm=4, hin0=4, dec=5, out=5, move=5,
          dt=(5, 0), bc=(6, 1))
PARTS = 3
EXP_LN_SET = "natural_log_exp_and_others"
NBC = 2 * NST


def ssm_layers(nc, prm, ident, proj_dram, h1_dram, ngroup=NGROUP):
    with ExitStack() as ctx:
        sb = lambda n, s, d=F32: ctx.enter_context(nc.sbuf_tensor(n, s, d))
        ps = lambda n, s, d=F32: ctx.enter_context(nc.psum_tensor(n, s, d))
        made = []

        def sem(name):
            made.append(ctx.enter_context(nc.semaphore(name)))
            return made[-1]


        center = sb("center", [D, D])
        mean = sb("mean", [D, D])
        pick = sb("pick", [NBC * PARTS, NBC, P], BF16)
        eps = sb("eps", [D, 1])
        a_neg = sb("a_neg", [D, 2, NST])
        w_bc = sb("w_bc", [D, 2, PARTS, NBC])
        b_bc = sb("b_bc", [NBC * PARTS, 2])
        w_dt = sb("w_dt", [D, 2, D])
        w_mix = sb("w_mix", [D, 2, D])
        w_mix_t = sb("w_mix_t", [D, 2, D])
        w_mixc = sb("w_mixc", [D, 2, D])
        b_mixc = sb("b_mixc", [D, 2])
        w_dec = sb("w_dec", [D, D])
        cols = sb("cols", [D, 16])
        b_dt, b_mix, d_skip, ln_g, ln_b = (cols[:, 2 * i:2 * i + 2] for i in range(5))
        b_tok, b_dec, cls0, cls1 = (cols[:, 10 + i:11 + i] for i in range(4))
        pos = sb("pos", [D, L])
        pos_out = sb("pos_out", [D, L])

        proj = sb("patches_in", [D, PW, G, PH])
        proj_again = sb("proj_again", [D, PW, G, PH])
        h0 = sb("h0", [D, G, L])
        h0c = sb("h0c", [D, T])
        sq = sb("sq", [D, T])
        lnv0, lnv = sb("lnv0", [D, T]), sb("lnv", [D, T])
        rstd0 = sb("rstd0", [D, T])
        hin0 = sb("hin0", [D, T])
        hin1_next = sb("hin1_next", [D, T])
        hin1 = sb("hin1", [D, T])
        hin = [hin0, hin1]
        hin_pre = [hin0, hin1_next]
        dt = [sb(f"dt{i}", [D, T]) for i in range(2)]
        dtx = [sb(f"dtx{i}", [D, T]) for i in range(2)]
        bc = [sb(f"bc{i}", [NBC * PARTS, T], BF16) for i in range(2)]
        sp_abs, sp_relu = sb("sp_abs", [D, T]), sb("sp_relu", [D, T])
        left = sb("left", [NBC * (PARTS - 1), T])
        y = sb("y_sb", [D, T])
        gelu = sb("gelu", [D, T])
        yc = sb("yc", [D, T])
        rstd = sb("rstd", [D, T])
        yn = sb("yn", [D, T])
        zdec = sb("zdec", [D, T])
        res = sb("res_a", [D, G, L])
        outb = sb("outb", [D, G, L])
        a = [sb(f"a{i}", [D, 2, G, L]) for i in range(RING)]
        u = [sb(f"u{i}", [D, 2, T]) for i in range(RING)]
        h = [sb(f"h_ring{i}", [D, 2, T]) for i in range(RING)]
        cs = [sb(f"cs{i}", [D, 2, T]) for i in range(RING)]
        hc = [sb(f"hc{i}", [D, 2, T]) for i in range(RING)]

        b_ps = [ps(f"b_ps{i}", [P, 2, 512]) for i in range(2)]
        c_ps = ps("c_ps", [P, 2, 512])
        y_ps = ps("y_ps", [P, 512])
        mm_ps = ps("mm_ps", [P, 512])

        loaded, s_pool, s_act, s_pe, s_dve = (sem(n) for n in ("loaded", "s_pool", "s_act", "s_pe", "s_dve"))
        with nc.Block() as block:
            col = lambda v: v.rearrange("(d o) -> d o", o=1)
            loads = []
            for p in range(PARTS):
                for l in range(2):
                    loads += [(w_bc[:, l, p, 0:NST], prm["W_B"][l]), (w_bc[:, l, p, NST:NBC], prm["W_C"][l]),
                              (b_bc[NBC * p:NBC * p + NST, l:l + 1], col(prm["b_B"][l])),
                              (b_bc[NBC * p + NST:NBC * (p + 1), l:l + 1], col(prm["b_C"][l]))]
            loads += [(a_neg[:, :, :], prm["A_log"].rearrange("l d n -> d l n")),
                      (w_dt[:, :, :], prm["W_dt"].rearrange("l d n -> d l n")),
                      (w_mix[:, :, :], prm["W_mix"].rearrange("l d n -> d l n")), (w_dec[:, :], prm["W_dec"]),
                      (pos[:, 1:L], prm["pos"][0].rearrange("l o -> o l").broadcast_to([D, L - 1])),
                      (b_tok, col(prm["b_tok"])), (b_dec, col(prm["b_dec"])),
                      (cls0, col(prm["cls0"][0, 0])), (cls1, col(prm["cls1"][0, 0]))]
            for t, name in ((b_dt, "b_dt"), (b_mix, "b_mix"), (d_skip, "D_skip"), (ln_g, "ln_g"), (ln_b, "ln_b")):
                for l in range(2):
                    loads.append((t[:, l:l + 1], col(prm[name][l])))

            @block.sync
            def _(sp):
                for dst, src in loads:
                    sp.dma_start(dst, src).then_inc(loaded, 16)

            @block.gpsimd
            def _(pool):
                nc.gpsimd.memset(mean[:, :], 1.0 / D).then_inc(s_pool, 1)
                nc.gpsimd.memset(pick[:, :, :], 0.0).then_inc(s_pool, 1)
                for p in range(PARTS):
                    pool.wait_ge(s_pool, 2 + p)
                    pool.affine_select(out=pick[:, :, :], in_=pick[:, :, :], compare_op=ALU.not_equal, fill=1.0,
                                       base=-NBC * p, pattern=[[-1, NBC], [0, P]],
                                       channel_multiplier=1).then_inc(s_pool, 1)

            @block.scalar
            def _(act):
                act.wait_ge(loaded, 16 * len(loads))
                nc.scalar.activation(a_neg[:, :, :], a_neg[:, :, :], ACT.Exp).then_inc(s_act, 1)

            @block.tensor
            def _(pe):
                pe.wait_ge(loaded, 16 * len(loads))
                for l in range(2):
                    ins = pe.transpose(y_ps[:, l * D:(l + 1) * D], w_mix[:, l, :], ident[:, :])
                ins.then_inc(s_pe, 1)
                pe.wait_ge(s_dve, 6)
                for l in range(2):
                    pe.matmul(mm_ps[:, l * D:(l + 1) * D], w_mix_t[:, l, :], center[:, :], start=True, stop=True)
                    ins = pe.matmul(mm_ps[:, 2 * D + l:2 * D + l + 1], center[:, :], b_mix[:, l:l + 1],
                                    start=True, stop=True)
                ins.then_inc(s_pe, 1)

            @block.vector
            def _(dve):
                nc.vector.memset(eps[:, :], EPS).then_inc(s_dve, 1)
                for r in range(RING):
                    ins = nc.vector.memset(a[r][:, :, :, :], 0.0)
                ins.then_inc(s_dve, 1)
                dve.wait_ge(s_act, 1)
                nc.vector.tensor_scalar(a_neg[:, :, :], a_neg[:, :, :], -1.0, None, ALU.mult).then_inc(s_dve, 1)
                dve.wait_ge(s_pool, 1)
                nc.vector.tensor_tensor(center[:, :], ident[:, :], mean[:, :], ALU.subtract).then_inc(s_dve, 1)
                dve.wait_ge(s_pe, 1)
                nc.vector.tensor_copy(w_mix_t[:, :, :].rearrange("p a b -> p (a b)"), y_ps[:, 0:2 * D]).then_inc(s_dve, 1)
                nc.vector.tensor_scalar(pos[:, 2:L], pos[:, 2:L], b_tok, None, ALU.add).then_inc(s_dve, 1)
                nc.vector.tensor_scalar(pos[:, 1:2], pos[:, 1:2], cls1, None, ALU.add).then_inc(s_dve, 1)
                nc.vector.tensor_copy(pos[:, 0:1], cls0).then_inc(s_dve, 1)
                dve.wait_ge(s_dve, 8)
                nc.vector.tensor_scalar(pos_out[:, :], pos[:, :], b_dec, None, ALU.add).then_inc(s_dve, 1)
                for g in range(G):
                    ins = nc.vector.tensor_copy(h0[:, g, 0:2], pos[:, 0:2])
                    ins = nc.vector.memset(res[:, g, 0:2], 0.0)
                ins.then_inc(s_dve, 1)
                dve.wait_ge(s_dve, 10)
                for g in range(G):
                    ins = nc.vector.tensor_copy(res[:, g, 0:2], pos_out[:, 0:2])
                ins.then_inc(s_dve, 1)
                dve.wait_ge(s_pe, 2)
                nc.vector.tensor_copy(w_mixc[:, :, :].rearrange("p a b -> p (a b)"), mm_ps[:, 0:2 * D]).then_inc(s_dve, 1)
                nc.vector.tensor_copy(b_mixc[:, :], mm_ps[:, 2 * D:2 * D + 2]).then_inc(s_dve, 1)

        a_made, b_spread, c_spread, c_copied = sem("a_made"), sem("b_spread"), sem("c_spread"), sem("c_copied")
        c_by_dve = sem("c_by_dve")
        u_made, scanned, hc_made, summed = (sem(n) for n in ("u_made", "scanned", "hc_made", "summed"))
        (dt_mm, sp_abs_made, sp_relu_made, sp_exp_made, sp_ln_made, dt_made, dtx_made, bc_mm, bc_part0, bc_left,
         bc_part1, bc_made) = (sem(n) for n in (
             "dt_mm", "sp_abs_made", "sp_relu_made", "sp_exp_made", "sp_ln_made", "dt_made", "dtx_made", "bc_mm",
             "bc_part0", "bc_left", "bc_part1", "bc_made"))
        y_made, gelu_made, mix_mm, yc_made, var_mm, rstd_made, yn_made, hin_next = (sem(n) for n in (
            "y_made", "gelu_made", "mix_mm", "yc_made", "var_mm", "rstd_made", "yn_made", "hin_next"))
        (proj_in, h0_made, h0c_mm, h0c_made, var0_mm, rstd0_made, hin0_made, again_in, res_made, hin1_moved,
         dec_mm, out_made, out_stored) = (sem(n) for n in (
             "proj_in", "h0_made", "h0c_mm", "h0c_made", "var0_mm", "rstd0_made", "hin0_made", "again_in", "res_made",
             "hin1_moved", "dec_mm", "out_made", "out_stored"))
        mm_free = sem("mm_free")
        flat = lambda t: t[:, :, :].rearrange("d g l -> d (g l)")
        grid = lambda t: t.rearrange("d (w h) -> d w h", w=PW)
        mm = mm_ps[:, 0:T]

        def by_dve(j):
            return j in DVE_PAIRS

        def wait_c(eng, s, j):
            if j < 0:
                s, j = s - 1, j + PAIRS
            kind = by_dve(j)
            count = s * sum(by_dve(i) == kind for i in range(PAIRS)) + sum(by_dve(i) == kind for i in range(j + 1))
            at_least(eng, c_by_dve if kind else c_copied, count)

        def copy_c(eng, s, j):
            eng.wait_ge(c_spread, PAIRS * s + j + 1)
            at_least(eng, hc_made, PAIRS * s + j - RING + 1)
            if by_dve(j):
                nc.vector.tensor_copy(cs[j % RING][:, :, :], c_ps[:, :, 0:T]).then_inc(c_by_dve, 1)
            else:
                nc.scalar.activation(cs[j % RING][:, :, :], c_ps[:, :, 0:T], ACT.Copy).then_inc(c_copied, 1)

        def pair_pe(pe, l, s, j):
            c = PAIRS * s + j
            if j == 0:
                pe.wait_ge(bc_made, s + 1)
            at_least(pe, u_made, c - 1)
            for k in range(2):
                ins = pe.matmul(b_ps[j % 2][:, k, 0:T], pick[:, 2 * j + k, :], bc[l][:, :], start=True, stop=True)
            ins.then_inc(b_spread, 1)
            wait_c(pe, s, j - 1)
            for k in range(2):
                ins = pe.matmul(c_ps[:, k, 0:T], pick[:, NST + 2 * j + k, :], bc[l][:, :], start=True, stop=True)
            ins.then_inc(c_spread, 1)

        def pair_act(act, l, s, j):
            c, r = PAIRS * s + j, j % RING
            if j == 0:
                act.wait_ge(dt_made, s + 1)
            at_least(act, scanned, c - RING + 1)
            dtv = dt[l][:, :].rearrange("d (g l) -> d g l", g=G)[:, :, 1:L]
            for k in range(2):
                ins = nc.scalar.activation(a[r][:, k, :, 1:L], dtv, ACT.Exp, scale=a_neg[:, l, 2 * j + k:2 * j + k + 1])
            ins.then_inc(a_made, 1)
            if not by_dve(j):
                copy_c(act, s, j)

        def pair_dve(dve, l, s, j):
            c, r = PAIRS * s + j, j % RING
            if j == 0:
                dve.wait_ge(dtx_made, s + 1)
            dve.wait_ge(b_spread, c + 1)
            at_least(dve, scanned, c - RING + 1)
            nc.vector.tensor_tensor(u[r][:, :, :], b_ps[j % 2][:, :, 0:T],
                                    dtx[l][:, :].rearrange("d (o t) -> d o t", o=1).broadcast_to([D, 2, T]),
                                    ALU.mult).then_inc(u_made, 1)
            if by_dve(j):
                copy_c(dve, s, j)
            dve.wait_ge(u_made, c + 1)
            dve.wait_ge(a_made, c + 1)
            at_least(dve, hc_made, c - RING + 1)
            nc.vector.tensor_tensor_scan(h[r][:, :, :].rearrange("d k t -> d (k t)"),
                                         a[r][:, :, :, :].rearrange("d k g l -> d (k g l)"),
                                         u[r][:, :, :].rearrange("d k t -> d (k t)"), 0.0,
                                         ALU.mult, ALU.add).then_inc(scanned, 1)

        def pair_pool(pool, l, s, j):
            c, r = PAIRS * s + j, j % RING
            pool.wait_ge(scanned, c + 1)
            wait_c(pool, s, j)
            at_least(pool, summed, c - RING + 1)
            nc.gpsimd.tensor_tensor(hc[r][:, :, :], h[r][:, :, :], cs[r][:, :, :], ALU.mult).then_inc(hc_made, 1)

        def sum_pe(pe, s, j):
            pe.wait_ge(hc_made, PAIRS * s + j + 1)
            if j == 0:
                at_least(pe, y_made, s)
            for k in range(2):
                ins = pe.matmul(y_ps[:, 0:T], ident[:, :], hc[j % RING][:, k, :], start=(j == 0 and k == 0),
                                stop=(j == PAIRS - 1 and k == 1))
            ins.then_inc(summed, 1)

        def pre0_pool(pool, g):
            pool.wait_ge(proj_in, 16 * (g + 1))
            at_least(pool, h0c_mm, g)
            for k in range(G):
                ins = nc.gpsimd.tensor_tensor(grid(h0[:, k, 2:L]), proj[:, :, k, :], grid(pos[:, 2:L]), ALU.add)
            ins.then_inc(h0_made, 1)

        def pre0_pe_center(pe, g, taken):
            pe.wait_ge(h0_made, g + 1)
            at_least(pe, mm_free, taken)
            pe.matmul(mm, center[:, :], flat(h0), start=True, stop=True).then_inc(h0c_mm, 1)

        def pre0_act_center(act, g):
            act.wait_ge(h0c_mm, g + 1)
            at_least(act, hin0_made, g)
            nc.scalar.activation(h0c[:, :], mm, ACT.Copy).then_inc(h0c_made, 1)
            nc.scalar.activation(sq[:, :], mm, ACT.Square).then_inc(mm_free, 1)

        def pre0_pe_var(pe, g, taken):
            pe.wait_ge(mm_free, taken)
            pe.matmul(mm, mean[:, :], sq[:, :], start=True, stop=True).then_inc(var0_mm, 1)

        def pre0_act_rstd(act, g, taken):
            act.wait_ge(var0_mm, g + 1)
            at_least(act, rstd0_made, g)
            nc.scalar.activation(lnv0[:, :], mm, ACT.Ln, bias=eps[:, :]).then_inc(mm_free, 1)
            act.wait_ge(mm_free, taken + 1)
            at_least(act, hin0_made, g)
            nc.scalar.activation(rstd0[:, :], lnv0[:, :], ACT.Exp, scale=-0.5).then_inc(rstd0_made, 1)

        def pre0_dve(dve, g, post):
            dve.wait_ge(rstd0_made, g + 1)
            dve.wait_ge(h0c_made, g + 1)
            if post is not None:
                dve.wait_ge(hin_next, post + 1)
            nc.vector.tensor_tensor(hin0[:, :], h0c[:, :], rstd0[:, :], ALU.mult).then_inc(hin0_made, 1)

        def wait_hin(eng, l, g, posts):
            if l == 0:
                eng.wait_ge(hin0_made, g + 1)
            else:
                eng.wait_ge(hin_next, posts)

        def pre_pe_dt(pe, l, s, g, posts, taken):
            wait_hin(pe, l, g, posts)
            at_least(pe, mm_free, taken)
            pe.matmul(mm, w_dt[:, l, :], hin_pre[l][:, :], start=True, stop=True).then_inc(dt_mm, 1)

        def pre_act_dt(act, l, s):
            bias = b_dt[:, l:l + 1]
            act.wait_ge(dt_mm, s + 1)
            at_least(act, dt_made, s)
            nc.scalar.activation(sp_abs[:, :], mm, ACT.Abs, bias=bias).then_inc(sp_abs_made, 1)
            act.wait_ge(sp_abs_made, s + 1)
            nc.scalar.activation(sp_abs[:, :], sp_abs[:, :], ACT.Exp, scale=-1.0).then_inc(sp_exp_made, 1)
            act.wait_ge(sp_exp_made, s + 1)
            nc.scalar.activation(sp_abs[:, :], sp_abs[:, :], ACT.Ln, bias=1.0).then_inc(sp_ln_made, 1)

        def pre_dve_relu(dve, l, s):
            dve.wait_ge(sp_abs_made, s + 1)
            at_least(dve, dt_made, s)
            nc.vector.tensor_scalar(sp_relu[:, :], mm, b_dt[:, l:l + 1], 0.0, ALU.add, ALU.max).then_inc(mm_free, 1)

        def pre_pool_dt(pool, l, s, g, posts, pairs, taken):
            pool.wait_ge(sp_ln_made, s + 1)
            pool.wait_ge(mm_free, taken + 1)
            at_least(pool, a_made, pairs)
            at_least(pool, u_made, pairs)
            nc.gpsimd.tensor_tensor(dt[l][:, :], sp_abs[:, :], sp_relu[:, :], ALU.add).then_inc(dt_made, 1)
            pool.wait_ge(dt_made, s + 1)
            wait_hin(pool, l, g, posts)
            nc.gpsimd.tensor_tensor(dtx[l][:, :], dt[l][:, :], hin_pre[l][:, :], ALU.mult).then_inc(dtx_made, 1)

        def pre_pe_bc(pe, l, s, taken):
            pe.wait_ge(mm_free, taken)
            pe.matmul(mm_ps[0:NBC * PARTS, 0:T], w_bc[:, l, :, :].rearrange("d p n -> d (p n)"), hin_pre[l][:, :],
                      start=True, stop=True).then_inc(bc_mm, 1)

        def pre_dve_bc(dve, l, s, pairs, taken):
            dve.wait_ge(bc_mm, s + 1)
            at_least(dve, c_spread, pairs)
            x, bias = mm_ps[0:NBC * PARTS, 0:T], b_bc[:, l:l + 1]
            n2, n3 = NBC * 2, NBC
            nc.vector.tensor_scalar(bc[l][:, :], x, bias, None, ALU.add).then_inc(bc_part0, 1)
            dve.wait_ge(bc_part0, s + 1)
            at_least(dve, bc_made, s)
            nc.vector.scalar_tensor_tensor(out=left[:, :], in0=x[0:n2], scalar=bias[0:n2], in1=bc[l][0:n2, :],
                                           op0=ALU.add, op1=ALU.subtract).then_inc(mm_free, 1)
            dve.wait_ge(mm_free, taken + 1)
            nc.vector.tensor_copy(bc[l][0:n2, :], left[:, :]).then_inc(bc_part1, 1)
            dve.wait_ge(bc_part1, s + 1)
            nc.vector.tensor_tensor(bc[l][0:n3, :], left[0:n3, :], bc[l][0:n3, :], ALU.subtract).then_inc(bc_made, 1)

        def post_dve_y(dve, l, s, g):
            dve.wait_ge(summed, PAIRS * (s + 1))
            dve.wait_ge(hin1_moved if l else hin0_made, g + 1)
            at_least(dve, gelu_made, s)
            nc.vector.scalar_tensor_tensor(out=y[:, :], in0=hin[l][:, :], scalar=d_skip[:, l:l + 1], in1=y_ps[:, 0:T],
                                           op0=ALU.mult, op1=ALU.add).then_inc(y_made, 1)

        def post_act_gelu(act, s):
            act.wait_ge(y_made, s + 1)
            at_least(act, mix_mm, s)
            nc.scalar.activation(gelu[:, :], y[:, :], ACT.Gelu).then_inc(gelu_made, 1)
            act.preload_act_table_set(EXP_LN_SET)

        def post_pe_mix(pe, l, s, taken):
            pe.wait_ge(gelu_made, s + 1)
            at_least(pe, mm_free, taken)
            pe.matmul(mm, w_mixc[:, l, :], gelu[:, :], start=True, stop=True).then_inc(mix_mm, 1)

        def post_act_mix(act, l, s):
            act.wait_ge(mix_mm, s + 1)
            at_least(act, yn_made, s)
            nc.scalar.activation(yc[:, :], mm, ACT.Identity, bias=b_mixc[:, l:l + 1]).then_inc(yc_made, 1)
            nc.scalar.activation(sq[:, :], mm, ACT.Square, bias=b_mixc[:, l:l + 1]).then_inc(mm_free, 1)

        def post_pe_var(pe, s, taken):
            pe.wait_ge(mm_free, taken)
            pe.matmul(mm, mean[:, :], sq[:, :], start=True, stop=True).then_inc(var_mm, 1)

        def post_act_rstd(act, s, taken):
            act.wait_ge(var_mm, s + 1)
            at_least(act, rstd_made, s)
            nc.scalar.activation(lnv[:, :], mm, ACT.Ln, bias=eps[:, :]).then_inc(mm_free, 1)
            act.wait_ge(mm_free, taken + 1)
            at_least(act, yn_made, s)
            nc.scalar.activation(rstd[:, :], lnv[:, :], ACT.Exp, scale=-0.5).then_inc(rstd_made, 1)

        def post_dve_norm(dve, l, s, g):
            dve.wait_ge(rstd_made, s + 1)
            dve.wait_ge(yc_made, s + 1)
            at_least(dve, hin_next, s)
            nc.vector.scalar_tensor_tensor(out=yn[:, :], in0=yc[:, :], scalar=ln_g[:, l:l + 1], in1=rstd[:, :],
                                           op0=ALU.mult, op1=ALU.mult).then_inc(yn_made, 1)
            dve.wait_ge(yn_made, s + 1)
            at_least(dve, dec_mm if l else hin1_moved, g)
            nc.vector.scalar_tensor_tensor(out=(zdec if l else hin1_next)[:, :], in0=yn[:, :], scalar=ln_b[:, l:l + 1],
                                           in1=hin[l][:, :], op0=ALU.add, op1=ALU.add).then_inc(hin_next, 1)

        def post1_pool(pool, g):
            pool.wait_ge(again_in, 16 * (g + 1))
            at_least(pool, out_made, g)
            for k in range(G):
                ins = nc.gpsimd.tensor_tensor(grid(res[:, k, 2:L]), proj_again[:, :, k, :], grid(pos_out[:, 2:L]), ALU.add)
            ins.then_inc(res_made, 1)

        def pre1_dve_move(dve, s, g, post):
            dve.wait_ge(hin_next, s - 1 if post is None else post + 1)
            nc.vector.tensor_copy(hin1[:, :], hin1_next[:, :]).then_inc(hin1_moved, 1)

        def post1_pe_dec(pe, s, taken):
            pe.wait_ge(hin_next, s + 1)
            pe.wait_ge(mm_free, taken)
            pe.matmul(mm, w_dec[:, :], zdec[:, :], start=True, stop=True).then_inc(dec_mm, 1)

        def post1_dve(dve, g, taken):
            dve.wait_ge(dec_mm, g + 1)
            dve.wait_ge(res_made, g + 1)
            at_least(dve, out_stored, 16 * g)
            nc.vector.tensor_tensor(flat(outb), mm, flat(res), ALU.add).then_inc(mm_free, 1)
            dve.wait_ge(mm_free, taken + 1)
            dve.sem_inc(out_made, 1)

        MM_POST, MM_PRE = (2, 3), (4, 2)
        BEFORE_LOOP = MM_PRE[0] + MM_POST[0] + MM_PRE[0] + MM_PRE[1] + MM_POST[0] + MM_PRE[0]
        PER_ROUND = sum(MM_POST) + sum(MM_PRE)

        def rounds(eng, run):
            n = ngroup
            run(None, None, (0, 0, 0), 0)
            run((0, 0, 0), None, None, 4)
            run(None, (0, 0, 0), (0, 1, 1), 4)
            run((0, 1, 1), None, (1, 2, 0), 10)
            run((1, 2, 0), (0, 1, 1), (0, 3, 2), 12)

            def round_of(i, taken, ahead):
                run((0, 2 * i - 1, i), (1, 2 * i - 2, i - 2), (1, 2 * i, i - 1), taken)
                run((1, 2 * i, i - 1), (0, 2 * i - 1, i), (0, 2 * i + 1, i + 1) if ahead else None,
                    taken + MM_POST[1] + MM_PRE[1])

            round_of(2, BEFORE_LOOP, True)
            with eng.Fori(3, n - 1) as i:
                round_of(i, (i - 2) * PER_ROUND + BEFORE_LOOP, True)
            taken = BEFORE_LOOP + (n - 3) * PER_ROUND
            round_of(n - 1, taken, False)
            taken += PER_ROUND - MM_PRE[0]
            run(None, (1, 2 * n - 2, n - 2), (1, 2 * n - 1, n - 1), taken)
            run((1, 2 * n - 1, n - 1), None, None, taken + 5)
            run(None, (1, 2 * n - 1, n - 1), None, taken + 5)

        def posts_before(pre, post):
            return post[1] if post is not None else pre[1] - 1

        def pairs_before(pre, pairs):
            return PAIRS * (pre[1] if pairs is None else pre[1] - 1)

        def taken_in(post, pre, taken):
            out = {}
            if pre is not None and pre[0] == 0:
                out["center"], out["var0"], taken = taken, taken + 1, taken + 2
            if pre is not None and pre[0] == 1:
                out["dt"], out["bc"], taken = taken, taken + 1, taken + 2
            if post is not None:
                out["mix"], out["var"], taken = taken, taken + 1, taken + 2
                if post[0] == 1:
                    out["dec"], taken = taken, taken + 1
            if pre is not None and pre[0] == 0:
                out["dt"], out["bc"] = taken, taken + 1
            return out

        ctx.callback(clear, nc, made)
        block = ctx.enter_context(nc.Block())

        @block.sync
        def _(sp):
            start = lambda g: min(G * g, B - G) if isinstance(g, int) else G * g

            def load(buf, done, last_read, g):
                at_least(sp, last_read, g)
                sp.dma_start(buf[:, :, :, :], proj_dram[:, :, bass.ds(start(g), G), :]).then_inc(done, 16)

            def store(g):
                sp.wait_ge(out_made, g + 1)
                sp.dma_start(h1_dram[:, bass.ds(start(g), G), :], outb[:, :, :]).then_inc(out_stored, 16)

            load(proj, proj_in, h0_made, 0)
            load(proj, proj_in, h0_made, 1)
            load(proj_again, again_in, res_made, 0)
            load(proj, proj_in, h0_made, 2)
            store(0)
            with sp.Fori(1, ngroup - 3) as g:
                load(proj_again, again_in, res_made, g)
                load(proj, proj_in, h0_made, g + 2)
                store(g)
            for g in range(ngroup - 3, ngroup):
                load(proj_again, again_in, res_made, g)
                if g + 2 < ngroup:
                    load(proj, proj_in, h0_made, g + 2)
                store(g)
            sp.wait_ge(out_stored, 16 * ngroup)

        @block.tensor
        def _(pe):
            def run(pairs, post, pre, taken):
                at = taken_in(post, pre, taken)
                if pairs is None and post is not None:
                    sum_pe(pe, post[1], PAIRS - 2)
                    sum_pe(pe, post[1], PAIRS - 1)
                for j in range(PAIRS):
                    if pairs is not None:
                        pair_pe(pe, pairs[0], pairs[1], j)
                        if j >= 2:
                            sum_pe(pe, pairs[1], j - 2)
                        elif post is not None:
                            sum_pe(pe, post[1], PAIRS - 2 + j)
                    if pre is not None and pre[0] == 0:
                        if j == AT['center']:
                            pre0_pe_center(pe, pre[2], at["center"])
                        if j == AT['var0']:
                            pre0_pe_var(pe, pre[2], at["var0"])
                    if pre is not None and j == AT['dt'][pre[0]]:
                        pre_pe_dt(pe, *pre, posts_before(pre, post), at["dt"])
                    if pre is not None and j == AT['bc'][pre[0]]:
                        pre_pe_bc(pe, pre[0], pre[1], at["bc"])
                    if post is not None:
                        if j == AT['mix']:
                            post_pe_mix(pe, post[0], post[1], at["mix"])
                        if j == AT['var']:
                            post_pe_var(pe, post[1], at["var"])
                        if j == AT['dec'] and post[0] == 1:
                            post1_pe_dec(pe, post[1], at["dec"])

            rounds(pe, run)

        @block.scalar
        def _(act):
            def run(pairs, post, pre, taken):
                at = taken_in(post, pre, taken)
                for j in range(PAIRS):
                    if pairs is not None:
                        pair_act(act, pairs[0], pairs[1], j)
                    if pre is not None and pre[0] == 0:
                        if j == AT['center']:
                            pre0_act_center(act, pre[2])
                        if j == AT['var0']:
                            pre0_act_rstd(act, pre[2], at["var0"])
                    if pre is not None and j == AT['dt'][pre[0]]:
                        pre_act_dt(act, pre[0], pre[1])
                    if post is not None:
                        if j == AT['gelu']:
                            post_act_gelu(act, post[1])
                        if j == AT['mix']:
                            post_act_mix(act, post[0], post[1])
                        if j == AT['var']:
                            post_act_rstd(act, post[1], at["var"])

            act.preload_act_table_set(EXP_LN_SET)
            rounds(act, run)

        @block.vector
        def _(dve):
            def run(pairs, post, pre, taken):
                at = taken_in(post, pre, taken)
                for j in range(PAIRS):
                    if pairs is not None:
                        pair_dve(dve, pairs[0], pairs[1], j)
                    if post is not None:
                        if j == AT['y']:
                            post_dve_y(dve, *post)
                        if j == AT['norm']:
                            post_dve_norm(dve, *post)
                        if j == AT['out'] and post[0] == 1:
                            post1_dve(dve, post[2], at["dec"])
                    if pre is not None and pre[0] == 1 and j == AT['move']:
                        pre1_dve_move(dve, pre[1], pre[2], post[1] if post is not None else None)
                    if pre is not None and pre[0] == 0 and j == AT['hin0']:
                        pre0_dve(dve, pre[2], post[1] if post is not None else None)
                    if pre is not None and j == AT['dt'][pre[0]]:
                        pre_dve_relu(dve, pre[0], pre[1])
                    if pre is not None and j == AT['bc'][pre[0]]:
                        pre_dve_bc(dve, pre[0], pre[1], pairs_before(pre, pairs), at["bc"])

            rounds(dve, run)

        @block.gpsimd
        def _(pool):
            def run(pairs, post, pre, taken):
                at = taken_in(post, pre, taken)
                for j in range(PAIRS):
                    if pre is not None and pre[0] == 0 and j == 0:
                        pre0_pool(pool, pre[2])
                    if pairs is not None:
                        pair_pool(pool, pairs[0], pairs[1], j)
                    if pre is not None and j == AT['dt'][pre[0]]:
                        pre_pool_dt(pool, *pre, posts_before(pre, post), pairs_before(pre, pairs), at["dt"])
                    if post is not None and post[0] == 1 and j == AT['res']:
                        post1_pool(pool, post[2])

            rounds(pool, run)


H, HD = 8, 16
E = 8
Q = 4
NQUAD = B // Q
TAIL = L - P
TP = 32
SLOTS = Q + 1
W5 = SLOTS * P
HS = H + 2
LAG = {"pt": 2, "pv": 3}
CAP = B * L
TILES = B * L // P + E - 1
TABLE = E * CAP + (TILES + 1) * P
NO_TOKEN = 1 << 20
ROW = 2 * D + 1


def attention_and_routing(nc, prm, ident, h1_dram, rows_dram, table_dram, tile_start, tile_expert, dma, nquad=NQUAD):
    with ExitStack() as ctx:
        sb = lambda n, s, d=F32: ctx.enter_context(nc.sbuf_tensor(n, s, d))
        ps = lambda n, s, d=F32: ctx.enter_context(nc.psum_tensor(n, s, d))
        made = []

        def sem(name):
            made.append(ctx.enter_context(nc.semaphore(name)))
            return made[-1]


        w_q, w_k, w_v = sb("w_q", [D, D]), sb("w_k", [D, D]), sb("w_v", [D, D])
        w_o = sb("w_o", [D, D])
        w_op = sb("w_op", [P, 2, D])
        b_q, b_k, b_v = sb("b_q", [D, 1]), sb("b_k", [D, 1]), sb("b_v", [D, 1])
        b_vrep = sb("b_vrep", [D, P])
        b_o, ln_g, ln_b = sb("b_o", [P, D]), sb("ln1_g", [P, D]), sb("ln1_b", [P, D])
        gate_w, gate_b = sb("gate_w", [D, E]), sb("gate_b", [P, E])
        head_mask = sb("head_mask", [D, H])
        eps = sb("eps_b", [P, 1])
        below, ones = sb("below", [P, P]), sb("ones", [P, P])
        rev = sb("rev", [P, E])
        p_int, p_low, p_high = sb("p_int", [P, 1], I32), sb("p_low", [P, 1], I32), sb("p_high", [P, 1], I32)
        p_f, low_f, high_f = sb("p_f", [P, 1]), sb("low_f", [P, 1]), sb("high_f", [P, 1])
        rev_int = sb("rev_int", [P, E], I32)
        valid = sb("valid", [P, SLOTS])
        skip = sb("skip", [P, SLOTS])
        token = sb("token", [P, SLOTS])
        region = sb("region", [P, E])
        base = sb("base", [1, E])
        count, upto, count_int = sb("count", [1, E]), sb("upto", [1, E]), sb("count_int", [1, E], I32)
        past = sb("past", [1, TILES, E])
        of_tile, tile_no, tile_int = sb("of_tile", [1, TILES]), sb("tile_no", [1, TILES]), sb("tile_int", [1, TILES], I32)
        blank = sb("blank", [P, TABLE // P], I32)

        hT = [sb(f"hT{i}", [D, W5]) for i in range(2)]
        h_tok = [sb(f"h_tok{i}", [P, SLOTS, D]) for i in range(2)]
        x_tok = [sb(f"x_tok{i}", [P, SLOTS, D]) for i in range(2)]
        x_bo = [sb(f"x_bo{i}", [P, SLOTS, D]) for i in range(2)]
        qT = [sb(f"qT{i}", [D, W5]) for i in range(2)]
        kT = [sb(f"kT{i}", [D, Q, L]) for i in range(2)]
        v_main = [sb(f"v_main{i}", [P, Q, H, TP]) for i in range(2)]
        v_tail = [sb(f"v_tail{i}", [P, Q, H, TP]) for i in range(2)]
        oT = [sb(f"oT{i}", [P, 2, W5]) for i in range(2)]
        xT = sb("xT", [D, W5])
        r_tok, n_tok, g_tok = sb("r_tok", [P, SLOTS, D]), sb("n_tok", [P, SLOTS, D]), sb("g_tok", [P, SLOTS, D])
        t_tok = [sb(f"t_tok{i}", [P, SLOTS, D + 1]) for i in range(2)]
        tT = sb("tT", [D, W5])
        stats = [sb(f"stats{i}", [P, SLOTS, 6]) for i in range(2)]
        mv = [sb(f"mv{i}", [P, SLOTS, 2]) for i in range(2)]
        lnv = [sb(f"lnv_b{i}", [P, SLOTS]) for i in range(2)]
        rstd = [sb(f"rstd_b{i}", [P, SLOTS]) for i in range(2)]
        logit, lexp, eq, onehot, place = (sb(n, [P, SLOTS, E]) for n in ("logit", "lexp", "eq", "onehot", "place"))
        lmax, lsum, first, where = (sb(n, [P, SLOTS]) for n in ("lmax", "lsum", "first", "where"))
        where_int, token_int = sb("where_int", [P, SLOTS], I32), sb("token_int", [P, SLOTS], I32)
        k_heads = [sb(f"k_heads{i}", [D, H, L]) for i in range(2)]
        e = [sb(f"e{i}", [P, HS, L]) for i in range(4)]
        p_main = [sb(f"p_main{i}", [P, HS, P]) for i in range(2)]
        p_tail = [sb(f"p_tail{i}", [P, HS + 2, TP]) for i in range(2)]
        smax, ssum, srec = (sb(n, [P, 4, HS]) for n in ("smax", "ssum", "srec"))
        pT_main = sb("pT_main", [P, HS, P])
        pT_tail = sb("pT_tail", [P, 3, P])

        s_ps = ps("s_ps", [P, 4, 512])
        m_ps = ps("m_ps", [P, 4, 512])

        s_pool, s_pe, s_dve = (sem(n) for n in ("s_pool_b", "s_pe_b", "s_dve_b"))
        (loaded,), (table_in,), (placed,) = dma["loaded"], dma["table_in"], dma["placed"]
        h_in, h_stored, t_stored = dma["h_in"], dma["h_stored"], dma["t_stored"]
        with nc.Block() as block:
            col = lambda v: v.rearrange("(d o) -> d o", o=1)
            row = lambda v: v.rearrange("(o d) -> o d", o=1).broadcast_to([P, v.shape[0]])
            loads = [(w_q, prm["Wq"]), (w_k, prm["Wk"]), (w_v, prm["Wv"]), (w_o, prm["Wo"]), (b_q, col(prm["bq"])),
                     (b_k, col(prm["bk"])), (b_v, col(prm["bv"])), (b_o, row(prm["bo"])), (ln_g, row(prm["ln1_g"])),
                     (ln_b, row(prm["ln1_b"])), (gate_w, prm["gate_W"]), (gate_b, row(prm["gate_b"]))]

            @block.sync
            def _(sp):
                for dst, src in loads:
                    sp.dma_start(dst[:, :], src).then_inc(loaded, 16)
                sp.wait_ge(s_dve, 1)
                for h in range(H):
                    sp.dma_start(w_op[32 * (h % 4):32 * (h % 4) + HD, h // 4, :],
                                 prm["Wo"][HD * h:HD * (h + 1), :]).then_inc(loaded, 16)
                sp.wait_ge(s_pool, 1)
                sp.dma_start(table_dram.rearrange("(p n) o -> p (n o)", p=P), blank[:, :]).then_inc(table_in, 16)

            @block.gpsimd
            def _(pool):
                nc.gpsimd.memset(blank[:, :], NO_TOKEN).then_inc(s_pool, 1)
                nc.gpsimd.memset(head_mask[:, :], 1.0).then_inc(s_pool, 1)
                nc.gpsimd.memset(ones[:, :], 1.0).then_inc(s_pool, 1)
                nc.gpsimd.iota(p_int[:, :], pattern=[[0, 1]], base=0, channel_multiplier=1).then_inc(s_pool, 1)
                nc.gpsimd.iota(rev_int[:, :], pattern=[[-1, E]], base=E, channel_multiplier=0).then_inc(s_pool, 1)
                nc.gpsimd.iota(tile_int[:, :], pattern=[[1, TILES]], base=0, channel_multiplier=0).then_inc(s_pool, 1)
                pool.wait_ge(s_pool, 6)
                pool.affine_select(out=head_mask[:, :], in_=head_mask[:, :], compare_op=ALU.is_ge, fill=0.0, base=0,
                                   pattern=[[-HD, H]], channel_multiplier=1).then_inc(s_pool, 1)
                pool.wait_ge(s_pool, 7)
                pool.affine_select(out=head_mask[:, :], in_=head_mask[:, :], compare_op=ALU.is_ge, fill=0.0,
                                   base=HD - 1, pattern=[[HD, H]], channel_multiplier=-1).then_inc(s_pool, 1)
                pool.affine_select(out=below[:, :], in_=ones[:, :], compare_op=ALU.is_ge, fill=0.0, base=-1,
                                   pattern=[[1, P]], channel_multiplier=-1).then_inc(s_pool, 1)

            @block.vector
            def _(dve):
                nc.vector.memset(w_op[:, :, :], 0.0).then_inc(s_dve, 1)
                nc.vector.memset(eps[:, :], EPS)
                for t in hT + v_main + v_tail + p_tail:
                    flat = t[:, :] if len(t.shape) == 2 else (t[:, :, :] if len(t.shape) == 3 else t[:, :, :, :])
                    nc.vector.memset(flat, 0.0)
                nc.vector.memset(valid[:, :], 1.0)
                nc.vector.memset(skip[:, :], 0.0)
                for k in range(E):
                    nc.vector.memset(region[:, k:k + 1], float(k * CAP))
                    nc.vector.memset(base[:, k:k + 1], float(k * CAP))
                nc.vector.memset(b_vrep[:, :], 0.0).then_inc(s_dve, 1)
                dve.wait_ge(s_pool, 9)
                nc.vector.tensor_scalar(p_low[:, :], p_int[:, :], TP - 1, None, ALU.bitwise_and).then_inc(s_dve, 1)
                nc.vector.tensor_scalar(p_high[:, :], p_int[:, :], 5, None, ALU.logical_shift_right).then_inc(s_dve, 1)
                nc.vector.tensor_copy(p_f[:, :], p_int[:, :]).then_inc(s_dve, 1)
                nc.vector.tensor_copy(tile_no[:, :], tile_int[:, :])
                nc.vector.tensor_copy(rev[:, :], rev_int[:, :]).then_inc(s_dve, 1)
                dve.wait_ge(s_dve, 6)
                nc.vector.tensor_copy(low_f[:, :], p_low[:, :]).then_inc(s_dve, 1)
                nc.vector.tensor_copy(high_f[:, :], p_high[:, :]).then_inc(s_dve, 1)
                dve.wait_ge(s_dve, 8)
                nc.vector.tensor_scalar(valid[:, Q:SLOTS], low_f[:, :], float(TAIL), None, ALU.is_lt).then_inc(s_dve, 1)
                nc.vector.tensor_scalar(skip[:, Q:SLOTS], low_f[:, :], float(TAIL), float(1 << 20), ALU.is_ge,
                                        ALU.mult).then_inc(s_dve, 1)
                for k in range(Q):
                    nc.vector.tensor_scalar(token[:, k:k + 1], p_f[:, :], float(L * k), None, ALU.add)
                nc.vector.tensor_scalar(token[:, Q:SLOTS], high_f[:, :], float(L - TP), float(P), ALU.mult,
                                        ALU.add).then_inc(s_dve, 1)
                dve.wait_ge(s_dve, 11)
                nc.vector.tensor_tensor(token[:, Q:SLOTS], token[:, Q:SLOTS], p_f[:, :], ALU.add).then_inc(s_dve, 1)
                dve.wait_ge(loaded, 16 * (len(loads) + H))
                nc.vector.tensor_scalar(b_vrep[:, :], b_vrep[:, :], b_v[:, :], None, ALU.add).then_inc(s_dve, 1)
                nc.vector.tensor_scalar(b_q[:, :], b_q[:, :], HD ** -0.5, None, ALU.mult).then_inc(s_dve, 1)
                dve.wait_ge(s_pe, 1)
                nc.vector.tensor_tensor(b_o[:, :], b_o[:, :], m_ps[:, 0, 0:D], ALU.add).then_inc(s_dve, 1)

            @block.tensor
            def _(pe):
                pe.wait_ge(s_dve, 13)
                pe.matmul(m_ps[:, 0, 0:D], b_vrep[:, :], w_o[:, :], start=True, stop=True).then_inc(s_pe, 1)

        sems = lambda names: [sem("b_" + n) for n in names.split()]
        k_ready, s_mm, s_max, s_sub, e_exp, s_sum, s_rec, p_made, pv_half, pv_mm, oT_made = sems(
            "k_ready s_mm s_max s_sub e_exp s_sum s_rec p_made pv_half pv_mm oT_made")
        pt_mm, pT_copied = sems("pt_mm pT_copied")
        h_mm, h_tok_made, st0, agg0, lnv0, rstd0, x_made, x_bo_made, x_mm, xT_made = sems(
            "h_mm h_tok_made st0 agg0 lnv0 rstd0 x_made x_bo_made x_mm xT_made")
        q_mm, qT_made, k_mm, kT_made, v_mm, v_made = sems("q_mm qT_made k_mm kT_made v_mm v_made")
        wo_mm, r_made, st1, agg1, lnv1, rstd1, n_made, g_made, t_made, t_mm, tT_made = sems(
            "wo_mm r_made st1 agg1 lnv1 rstd1 n_made g_made t_made t_mm tT_made")
        logit_mm, logit_made, lmax_made, lsub_made, lexp_made, lsum_made, gw_made = sems(
            "logit_mm logit_made lmax_made lsub_made lexp_made lsum_made gw_made")
        eq_made, eqv_made, first_made, one_made, onehot_made, rank_mm, place_made, placed_one, region_made = sems(
            "eq_made eqv_made first_made one_made onehot_made rank_mm place_made placed_one region_made")
        where_made, where_skip, token_ready, token_next = sems(
            "where_made where_skip token_ready token_next")
        token_seen, tiles_step = sems("token_seen tiles_step")

        AHEAD = {"h": 2, "x": 2, "q": 1, "k": 1, "v": 1, "wo": -1, "t": -2, "logit": -2, "rank": -2}
        ORDER = []
        for i in range(Q):
            ORDER += [("pv", i, 0)] + [("pt", i, k) for k in range(4)]
            ORDER += {0: [("q", 0, 0), ("q", 0, 1), ("k", 0, 0), ("k", 0, 1), ("t", 0, 0), ("t", 0, 1)],
                      1: [("h", 0, 0), ("h", 0, 1), ("logit", 0, 0)],
                      2: [("wo", 0, 0), ("wo", 0, 1), ("rank", 0, 0)],
                      3: [("v", 0, 0), ("v", 0, 1), ("x", 0, 0), ("x", 0, 1)]}[i]
        assert len(ORDER) % 4 == 0
        TAKEN = {"pt": pT_copied, "pv": oT_made, "wo": r_made, "h": h_tok_made, "x": xT_made, "q": qT_made,
                 "k": kT_made, "v": v_made, "t": tT_made, "logit": logit_made, "rank": region_made}

        def runs(q, kind, i):
            if not isinstance(q, int):
                return True
            if kind in ("pt", "pv"):
                return 0 <= Q * q + i - LAG[kind] < Q * nquad
            return 0 <= q + AHEAD[kind] < nquad

        def count_of(q, kind, i, k):
            if kind == "pt":
                return 4 * (Q * q + i - LAG[kind]) + k + 1
            if kind == "pv":
                return Q * q + i - LAG[kind] + 1
            quad = q + AHEAD[kind]
            return 2 * quad + k + 1 if kind not in ("logit", "rank") else quad + 1

        def bank(kind, i, k=0):
            return ORDER.index((kind, i, k)) % 4

        def wait_bank(pe, q, kind, i, k=0):
            n = ORDER.index((kind, i, k)) - 4
            while True:
                quad = q if n >= 0 else q - 1
                before = ORDER[n]
                if runs(quad, before[0], before[1]):
                    pe.wait_ge(TAKEN[before[0]], count_of(quad, *before))
                    return
                n -= 4
                if n < -len(ORDER):
                    return

        def load_h(sp, r, par):
            at_least(sp, h_mm, 2 * (r - 1))
            sp.dma_start(hT[par][:, 0:Q * P].rearrange("d (i t) -> d i t", i=Q),
                         h1_dram[:, bass.ds(Q * r, Q), 0:P]).then_inc(h_in[par], 16)
            sp.dma_start(hT[par][:, Q * P:W5].rearrange("d (i t) -> d i t", i=Q)[:, :, 0:TAIL],
                         h1_dram[:, bass.ds(Q * r, Q), P:L]).then_inc(h_in[par], 16)

        def turn_h(pe, q, r, par):
            pe.wait_ge(h_in[par], 16 * (r - par) + 32)
            wait_bank(pe, q, "h", 0, 0)
            for s in range(Q):
                ins = pe.transpose(m_ps[:, bank("h", 0, 0), s * P:(s + 1) * P], hT[par][:, s * P:(s + 1) * P], ident[:, :])
            ins.then_inc(h_mm, 1)
            wait_bank(pe, q, "h", 0, 1)
            pe.transpose(m_ps[:, bank("h", 0, 1), 0:P], hT[par][:, Q * P:W5], ident[:, :]).then_inc(h_mm, 1)

        def copy_h(act, r, par):
            at_least(act, h_stored[par], 40 * (r - par))
            act.wait_ge(h_mm, 2 * r + 1)
            nc.scalar.activation(h_tok[par][:, 0:Q, :], m_ps[:, bank("h", 0, 0), :].rearrange("p (s d) -> p s d", s=Q),
                                 ACT.Copy).then_inc(h_tok_made, 1)
            act.wait_ge(h_mm, 2 * r + 2)
            nc.scalar.activation(h_tok[par][:, Q, :], m_ps[:, bank("h", 0, 1), 0:P], ACT.Copy).then_inc(h_tok_made, 1)

        def norm_stats(dve, src, par, n, st, agg):
            at_least(dve, agg, n)
            for s in range(SLOTS):
                ins = nc.vector.bn_stats(stats[par][:, s, :], src[:, s, :])
            ins.then_inc(st, 1)
            wait_apart(dve, st, n + 1, s_dve, 13)
            for s in range(SLOTS):
                ins = nc.vector.bn_aggr(mv[par][:, s, :], stats[par][:, s, :])
            ins.then_inc(agg, 1)

        def norm_rstd(act, par, n, agg, lnv_made, rstd_made, applied):
            act.wait_ge(agg, n + 1)
            at_least(act, rstd_made, n)
            nc.scalar.activation(lnv[par][:, :], mv[par][:, :, 1], ACT.Ln, bias=eps[:, :]).then_inc(lnv_made, 1)
            act.wait_ge(lnv_made, n + 1)
            at_least(act, applied, n)
            nc.scalar.activation(rstd[par][:, :], lnv[par][:, :], ACT.Exp, scale=-0.5).then_inc(rstd_made, 1)

        def norm_apply(dve, dst, src, par, n, rstd_made, applied):
            dve.wait_ge(rstd_made, n + 1)
            for s in range(SLOTS):
                ins = nc.vector.tensor_scalar(dst[:, s, :], src[:, s, :], mv[par][:, s, 0:1], rstd[par][:, s:s + 1],
                                              ALU.subtract, ALU.mult)
            ins.then_inc(applied, 1)

        def stats_x(dve, r, par):
            dve.wait_ge(h_tok_made, 2 * (r + 1))
            at_least(dve, x_made, r)
            norm_stats(dve, h_tok[par], 0, r, st0, agg0)

        def apply_x(dve, r, par):
            at_least(dve, x_mm, 2 * (r - 1))
            at_least(dve, x_bo_made, r - 1)
            norm_apply(dve, x_tok[par], h_tok[par], 0, r, rstd0, x_made)

        def add_bo(pool, r, par):
            pool.wait_ge(x_made, r + 1)
            at_least(pool, r_made, 2 * (r - 1))
            nc.gpsimd.tensor_tensor(x_bo[par][:, :, :], x_tok[par][:, :, :],
                                    b_o[:, :].rearrange("p (o d) -> p o d", o=1).broadcast_to([P, SLOTS, D]),
                                    ALU.add).then_inc(x_bo_made, 1)

        def turn(pe, q, kind, src, mm):
            wait_bank(pe, q, kind, 0, 0)
            for s in range(Q):
                ins = pe.transpose(m_ps[:, bank(kind, 0, 0), s * P:(s + 1) * P], src[:, s, 0:D], ident[:, :])
            ins.then_inc(mm, 1)
            wait_bank(pe, q, kind, 0, 1)
            pe.transpose(m_ps[:, bank(kind, 0, 1), 0:P], src[:, Q, 0:D], ident[:, :]).then_inc(mm, 1)

        def turn_x(pe, q, r, par):
            pe.wait_ge(x_made, r + 1)
            turn(pe, q, "x", x_tok[par], x_mm)

        def copy_turned(act, kind, dst, n, mm, copied):
            act.wait_ge(mm, 2 * n + 1)
            nc.scalar.activation(dst[:, 0:Q * P], m_ps[:, bank(kind, 0, 0), :], ACT.Copy).then_inc(copied, 1)
            act.wait_ge(mm, 2 * n + 2)
            nc.scalar.activation(dst[:, Q * P:W5], m_ps[:, bank(kind, 0, 1), 0:P], ACT.Copy).then_inc(copied, 1)

        def copy_x(act, r):
            at_least(act, v_mm, 2 * r)
            copy_turned(act, "x", xT, r, x_mm, xT_made)

        def project_qk(pe, q, r):
            pe.wait_ge(xT_made, 2 * (r + 1))
            for kind, w, mm in (("q", w_q, q_mm), ("k", w_k, k_mm)):
                wait_bank(pe, q, kind, 0, 0)
                pe.matmul(m_ps[:, bank(kind, 0, 0), :], w[:, :], xT[:, 0:Q * P], start=True, stop=True).then_inc(mm, 1)
                wait_bank(pe, q, kind, 0, 1)
                pe.matmul(m_ps[:, bank(kind, 0, 1), 0:P], w[:, :], xT[:, Q * P:W5], start=True, stop=True).then_inc(mm, 1)

        def project_v(pe, q, r):
            wait_bank(pe, q, "v", 0, 0)
            for i in range(Q):
                ins = pe.matmul(m_ps[:, bank("v", 0, 0), i * P:(i + 1) * P], xT[:, i * P:(i + 1) * P], w_v[:, :],
                                start=True, stop=True)
            ins.then_inc(v_mm, 1)
            wait_bank(pe, q, "v", 0, 1)
            for i in range(Q):
                for j in range(4):
                    ins = pe.matmul(m_ps[TP * j:TP * (j + 1), bank("v", 0, 1), i * P:(i + 1) * P],
                                    xT[:, Q * P + TP * i:Q * P + TP * (i + 1)], w_v[:, :], start=True, stop=True)
            ins.then_inc(v_mm, 1)

        def copy_qk(act, r, par):
            at_least(act, s_mm, Q * (r - 1))
            for k, (dst, src) in enumerate(((qT[par][:, 0:Q * P], m_ps[:, bank("q", 0, 0), :]),
                                            (qT[par][:, Q * P:W5], m_ps[:, bank("q", 0, 1), 0:P]))):
                act.wait_ge(q_mm, 2 * r + k + 1)
                nc.scalar.activation(dst, src, ACT.Identity, scale=HD ** -0.5, bias=b_q[:, :]).then_inc(qT_made, 1)
            at_least(act, k_ready, Q * (r - 1))
            act.wait_ge(k_mm, 2 * r + 1)
            nc.scalar.activation(kT[par][:, :, 0:P], m_ps[:, bank("k", 0, 0), :].rearrange("d (i t) -> d i t", i=Q),
                                 ACT.Identity, bias=b_k[:, :]).then_inc(kT_made, 1)
            act.wait_ge(k_mm, 2 * r + 2)
            nc.scalar.activation(kT[par][:, :, P:L],
                                 m_ps[:, bank("k", 0, 1), 0:P].rearrange("d (i t) -> d i t", i=Q)[:, :, 0:TAIL],
                                 ACT.Identity, bias=b_k[:, :]).then_inc(kT_made, 1)

        def copy_v(act, r, par):
            at_least(act, pv_mm, Q * (r - 1))
            for k, dst in enumerate((v_main[par], v_tail[par])):
                act.wait_ge(v_mm, 2 * r + k + 1)
                nc.scalar.activation(dst[:, :, :, 0:HD],
                                     m_ps[:, bank("v", 0, k), :].rearrange("p (i h c) -> p i h c", i=Q, c=HD),
                                     ACT.Copy).then_inc(v_made, 1)

        def heads_of_k(pool, m, i, par, r):
            pool.wait_ge(kT_made, 2 * (r + 1))
            at_least(pool, s_mm, m - 1)
            nc.gpsimd.tensor_tensor(k_heads[i % 2][:, :, :],
                                    kT[par][:, i:i + 1, :].broadcast_to([D, H, L]),
                                    head_mask[:, :].rearrange("d (h o) -> d h o", o=1).broadcast_to([D, H, L]),
                                    ALU.mult).then_inc(k_ready, 1)

        def scores(pe, m, i, par, r):
            pe.wait_ge(k_ready, m + 1)
            if i == 0:
                pe.wait_ge(qT_made, 2 * (r + 1))
            at_least(pe, s_sub, m)
            kh = k_heads[i % 2]
            for b, (h0, h1) in enumerate(((0, 3), (3, 6), (6, 8))):
                pe.matmul(s_ps[:, b, 0:(h1 - h0) * L], qT[par][:, i * P:(i + 1) * P],
                          kh[:, h0:h1, :].rearrange("d h k -> d (h k)"), start=True, stop=True)
            for j in range(4):
                ins = pe.matmul(s_ps[TP * j:TP * (j + 1), 3, 0:2 * L], qT[par][:, Q * P + TP * i:Q * P + TP * (i + 1)],
                                kh[:, 2 * j:2 * j + 2, :].rearrange("d h k -> d (h k)"), start=True, stop=True)
            ins.then_inc(s_mm, 1)

        S_PARTS = ((0, 2, 3), (2, 4, 2))

        def softmax(dve, m, i):
            dve.wait_ge(s_mm, m + 1)
            at_least(dve, s_rec, m - 3)
            c = 0
            for b0, b1, n in S_PARTS:
                w = (b1 - b0) * n
                ins = nc.vector.tensor_reduce(smax[:, i, c:c + w].rearrange("p (b h) -> p b h", b=b1 - b0),
                                              s_ps[:, b0:b1, 0:n * L].rearrange("p b (h k) -> p b h k", h=n), AX, ALU.max)
                c += w
            ins.then_inc(s_max, 1)
            dve.wait_ge(s_max, m + 1)
            at_least(dve, p_made, m - 3)
            c = 0
            for b0, b1, n in S_PARTS:
                w = (b1 - b0) * n
                ins = nc.vector.tensor_tensor(
                    e[i][:, c:c + w, :].rearrange("p (b h) k -> p b h k", b=b1 - b0),
                    s_ps[:, b0:b1, 0:n * L].rearrange("p b (h k) -> p b h k", h=n),
                    smax[:, i, c:c + w].rearrange("p (b h o) -> p b h o", b=b1 - b0, o=1).broadcast_to([P, b1 - b0, n, L]),
                    ALU.subtract)
                c += w
            ins.then_inc(s_sub, 1)

        def exponentials(act, m, i):
            act.wait_ge(s_sub, m + 1)
            nc.scalar.activation(e[i][:, :, :], e[i][:, :, :], ACT.Exp).then_inc(e_exp, 1)

        def denominators(dve, m, i):
            dve.wait_ge(e_exp, m + 1)
            nc.vector.tensor_reduce(ssum[:, i, :], e[i][:, :, :], AX, ALU.add).then_inc(s_sum, 1)
            dve.wait_ge(s_sum, m + 1)
            at_least(dve, p_made, m - 3)
            nc.vector.reciprocal(srec[:, i, :], ssum[:, i, :]).then_inc(s_rec, 1)

        def weights(pool, m, i):
            pool.wait_ge(s_rec, m + 1)
            at_least(pool, pt_mm, 4 * (m - 1))
            for dst, k0, k1 in ((p_main[i % 2], 0, P), (p_tail[i % 2], P, L)):
                ins = nc.gpsimd.tensor_tensor(dst[:, 0:HS, 0:k1 - k0], e[i][:, :, k0:k1],
                                              srec[:, i, :].rearrange("p (h o) -> p h o", o=1).broadcast_to([P, HS, k1 - k0]),
                                              ALU.mult)
            ins.then_inc(p_made, 1)

        def turn_p(pe, q, m, slot):
            i = (slot - LAG["pt"]) % Q
            pe.wait_ge(p_made, m + 1)
            main, tail = p_main[i % 2], p_tail[i % 2]
            for k in range(4):
                wait_bank(pe, q, "pt", slot, k)
                out = m_ps[:, bank("pt", slot, k), :]
                if k < 2:
                    for s in range(4):
                        ins = pe.transpose(out[:, s * P:(s + 1) * P], main[:, 4 * k + s, :], ident[:, :])
                elif k == 2:
                    for s in range(2):
                        pe.transpose(out[:, s * P:(s + 1) * P], main[:, H + s, :], ident[:, :])
                    for s in range(2):
                        ins = pe.transpose(out[:, (2 + s) * P:(3 + s) * P],
                                           tail[:, 4 * s:4 * s + 4, :].rearrange("p h k -> p (h k)"), ident[:, :])
                else:
                    ins = pe.transpose(out[:, 0:P], tail[:, H:HS + 2, :].rearrange("p h k -> p (h k)"), ident[:, :])
                ins.then_inc(pt_mm, 1)

        def copy_pT(act, m, slot):
            at_least(act, pv_mm, m)
            for k in range(4):
                act.wait_ge(pt_mm, 4 * m + k + 1)
                src = m_ps[:, bank("pt", slot, k), :]
                if k < 2:
                    nc.scalar.activation(pT_main[:, 4 * k:4 * k + 4, :], src.rearrange("p (s q) -> p s q", s=4),
                                         ACT.Copy).then_inc(pT_copied, 1)
                elif k == 2:
                    nc.scalar.activation(pT_main[:, H:HS, :], src[:, 0:2 * P].rearrange("p (s q) -> p s q", s=2), ACT.Copy)
                    nc.scalar.activation(pT_tail[:, 0:2, :], src[:, 2 * P:4 * P].rearrange("p (s q) -> p s q", s=2),
                                         ACT.Copy).then_inc(pT_copied, 1)
                else:
                    nc.scalar.activation(pT_tail[:, 2, :], src[:, 0:P], ACT.Copy).then_inc(pT_copied, 1)

        def with_v(pe, q, m, slot, par, r):
            i = (slot - LAG["pv"]) % Q
            pe.wait_ge(pT_copied, 4 * (m + 1))
            if i == 0:
                pe.wait_ge(v_made, 2 * (r + 1))
            wait_bank(pe, q, "pv", slot)
            out = m_ps[:, bank("pv", slot), 0:2 * (P + TP)].rearrange("p (a t) -> p a t", a=2)
            vm, vt = v_main[par], v_tail[par]
            for h in range(H):
                j, a = h % 4, h // 4
                pe.matmul(out[TP * j:TP * (j + 1), a, 0:P], vm[:, i, h, :], pT_main[:, h, :], start=(a == 0), stop=False,
                          skip_group_check=True)
            for h in range(H):
                j, a = h % 4, h // 4
                pe.matmul(out[TP * j:TP * (j + 1), a, P:P + TP], vm[:, i, h, :],
                          pT_main[:, H + h % 2, TP * (h // 2):TP * (h // 2 + 1)], start=False, stop=False,
                          skip_group_check=True)
            for h in range(H):
                j, a = h % 4, h // 4
                ins = pe.matmul(out[TP * j:TP * (j + 1), a, 0:P], vt[TP * j:TP * (j + 1), i, h, :],
                                pT_tail[TP * j:TP * (j + 1), a, :], start=False, stop=False, skip_group_check=True)
            ins.then_inc(pv_half, 1)
            wait_apart(pe, pv_half, m + 1, s_dve, 13)
            for h in range(H):
                j, a, g = h % 4, h // 4, h % 2
                ins = pe.matmul(out[TP * j:TP * (j + 1), a, P:P + TP], vt[TP * g:TP * (g + 1), i, h, :],
                                pT_tail[TP * g:TP * (g + 1), 2, TP * (h // 2):TP * (h // 2 + 1)], start=False,
                                stop=True, skip_group_check=True)
            ins.then_inc(pv_mm, 1)

        def copy_o(act, m, slot, par, r):
            i = (slot - LAG["pv"]) % Q
            act.wait_ge(pv_mm, m + 1)
            if i == 0:
                at_least(act, wo_mm, 2 * (r - 1))
            src = m_ps[:, bank("pv", slot), 0:2 * (P + TP)].rearrange("p (a t) -> p a t", a=2)
            nc.scalar.activation(oT[par][:, :, i * P:(i + 1) * P], src[:, :, 0:P], ACT.Copy)
            nc.scalar.activation(oT[par][:, :, Q * P + TP * i:Q * P + TP * (i + 1)], src[:, :, P:P + TP],
                                 ACT.Copy).then_inc(oT_made, 1)

        def output_of_heads(pe, q, r, par):
            pe.wait_ge(oT_made, Q * (r + 1))
            for k, slots in enumerate((range(Q), [Q])):
                wait_bank(pe, q, "wo", 0, k)
                for s in slots:
                    for a in range(2):
                        ins = pe.matmul(m_ps[:, bank("wo", 0, k), (s % Q) * P:(s % Q + 1) * P],
                                        oT[par][:, a, s * P:(s + 1) * P], w_op[:, a, :], start=(a == 0), stop=(a == 1))
                ins.then_inc(wo_mm, 1)

        def add_x(dve, r, par):
            dve.wait_ge(x_bo_made, r + 1)
            at_least(dve, n_made, r)
            for k, (s0, s1) in enumerate(((0, Q), (Q, SLOTS))):
                dve.wait_ge(wo_mm, 2 * r + k + 1)
                src = m_ps[:, bank("wo", 0, k), 0:(s1 - s0) * P].rearrange("p (s d) -> p s d", d=D)
                nc.vector.tensor_tensor(r_tok[:, s0:s1, :], src, x_bo[par][:, s0:s1, :], ALU.add).then_inc(r_made, 1)

        def stats_r(dve, r):
            dve.wait_ge(r_made, 2 * (r + 1))
            norm_stats(dve, r_tok, 1, r, st1, agg1)

        def apply_r(dve, r):
            at_least(dve, g_made, r)
            norm_apply(dve, n_tok, r_tok, 1, r, rstd1, n_made)

        def gain_and_bias(pool, r, par):
            pool.wait_ge(n_made, r + 1)
            at_least(pool, t_made, r)
            bc = lambda v: v[:, :].rearrange("p (o d) -> p o d", o=1).broadcast_to([P, SLOTS, D])
            nc.gpsimd.tensor_tensor(g_tok[:, :, :], n_tok[:, :, :], bc(ln_g), ALU.mult).then_inc(g_made, 1)
            pool.wait_ge(g_made, r + 1)
            at_least(pool, t_stored[par], 40 * (r - par))
            nc.gpsimd.tensor_tensor(t_tok[par][:, :, 0:D], g_tok[:, :, :], bc(ln_b), ALU.add).then_inc(t_made, 1)

        def turn_t(pe, q, r, par):
            pe.wait_ge(t_made, r + 1)
            turn(pe, q, "t", t_tok[par], t_mm)

        def copy_t(act, r):
            at_least(act, logit_mm, r)
            copy_turned(act, "t", tT, r, t_mm, tT_made)

        def gate(pe, q, r):
            pe.wait_ge(tT_made, 2 * (r + 1))
            wait_bank(pe, q, "logit", 0)
            for s in range(SLOTS):
                ins = pe.matmul(m_ps[:, bank("logit", 0), E * s:E * (s + 1)], tT[:, s * P:(s + 1) * P], gate_w[:, :],
                                start=True, stop=True)
            ins.then_inc(logit_mm, 1)

        bc_slot = lambda v: v.rearrange("p (s o) -> p s o", o=1).broadcast_to([P, SLOTS, E])
        bc_row = lambda v: v.rearrange("p (o x) -> p o x", o=1).broadcast_to([P, SLOTS, E])

        def choose(dve, r):
            dve.wait_ge(logit_mm, r + 1)
            at_least(dve, eq_made, r)
            nc.vector.tensor_tensor(logit[:, :, :], m_ps[:, bank("logit", 0), 0:SLOTS * E].rearrange("p (s x) -> p s x", x=E),
                                    bc_row(gate_b[:, :]), ALU.add).then_inc(logit_made, 1)
            dve.wait_ge(logit_made, r + 1)
            nc.vector.tensor_reduce(lmax[:, :], logit[:, :, :], AX, ALU.max).then_inc(lmax_made, 1)
            dve.wait_ge(lmax_made, r + 1)
            at_least(dve, lsum_made, r)
            nc.vector.tensor_tensor(lexp[:, :, :], logit[:, :, :], bc_slot(lmax[:, :]), ALU.subtract).then_inc(lsub_made, 1)
            at_least(dve, eqv_made, r)
            nc.vector.tensor_tensor(eq[:, :, :], logit[:, :, :], bc_slot(lmax[:, :]), ALU.is_equal).then_inc(eq_made, 1)
            dve.wait_ge(eq_made, r + 1)
            nc.vector.tensor_tensor(eq[:, :, :], eq[:, :, :], bc_row(rev[:, :]), ALU.mult).then_inc(eqv_made, 1)
            dve.wait_ge(eqv_made, r + 1)
            nc.vector.tensor_reduce(first[:, :], eq[:, :, :], AX, ALU.max).then_inc(first_made, 1)
            dve.wait_ge(first_made, r + 1)
            at_least(dve, rank_mm, r)
            at_least(dve, placed_one, r)
            nc.vector.tensor_tensor(onehot[:, :, :], bc_row(rev[:, :]), bc_slot(first[:, :]), ALU.is_equal).then_inc(one_made, 1)
            dve.wait_ge(one_made, r + 1)
            nc.vector.tensor_tensor(onehot[:, :, :], onehot[:, :, :], bc_slot(valid[:, :]), ALU.mult).then_inc(onehot_made, 1)

        def choice_exp(act, r):
            act.wait_ge(lsub_made, r + 1)
            nc.scalar.activation(lexp[:, :, :], lexp[:, :, :], ACT.Exp).then_inc(lexp_made, 1)

        def ranks(pe, q, r):
            pe.wait_ge(onehot_made, r + 1)
            wait_bank(pe, q, "rank", 0)
            out = m_ps[:, bank("rank", 0), :]
            flat = onehot[:, :, :].rearrange("p s x -> p (s x)")
            pe.matmul(out[:, 0:SLOTS * E], below[:, :], flat, start=True, stop=False, skip_group_check=True)
            for s in range(1, SLOTS):
                pe.matmul(out[:, E * s:E * SLOTS], ones[:, :], flat[:, 0:E * (SLOTS - s)], start=False, stop=True,
                          skip_group_check=True)
            for s in range(SLOTS):
                ins = pe.matmul(out[:, 64:64 + E], ones[:, :], flat[:, E * s:E * (s + 1)], start=False,
                                stop=(s == SLOTS - 1), skip_group_check=True)
            ins.then_inc(rank_mm, 1)

        def places(dve, r, par):
            dve.wait_ge(lexp_made, r + 1)
            nc.vector.tensor_reduce(lsum[:, :], lexp[:, :, :], AX, ALU.add).then_inc(lsum_made, 1)
            dve.wait_ge(lsum_made, r + 1)
            nc.vector.reciprocal(t_tok[par][:, :, D], lsum[:, :]).then_inc(gw_made, 1)
            dve.wait_ge(rank_mm, r + 1)
            out = m_ps[:, bank("rank", 0), :]
            at_least(dve, where_made, r)
            nc.vector.tensor_tensor(place[:, :, :], out[:, 0:SLOTS * E].rearrange("p (s x) -> p s x", x=E),
                                    bc_row(region[:, :]), ALU.add).then_inc(place_made, 1)
            dve.wait_ge(place_made, r + 1)
            nc.vector.tensor_tensor(region[:, :], region[:, :], out[:, 64:64 + E], ALU.add).then_inc(region_made, 1)
            nc.vector.tensor_tensor(place[:, :, :], place[:, :, :], onehot[:, :, :], ALU.mult).then_inc(placed_one, 1)
            dve.wait_ge(placed_one, r + 1)
            at_least(dve, where_skip, r)
            nc.vector.tensor_reduce(where[:, :], place[:, :, :], AX, ALU.add).then_inc(where_made, 1)
            dve.wait_ge(where_made, r + 1)
            at_least(dve, placed, 16 * SLOTS * r)
            nc.vector.tensor_tensor(where_int[:, :], where[:, :], skip[:, :], ALU.add).then_inc(where_skip, 1)
            at_least(dve, token_next, r)
            nc.vector.tensor_copy(token_int[:, :], token[:, :]).then_inc(token_ready, 1)
            dve.wait_ge(token_ready, r + 1)
            nc.vector.tensor_scalar(token[:, :], token[:, :], float(Q * L), None, ALU.add).then_inc(token_next, 1)

        def store_h(sp, r, par):
            rows = rows_dram.rearrange("(i t) c -> t i c", t=L)
            sp.wait_ge(h_tok_made, 2 * (r + 1))
            sp.dma_start(rows[0:P, bass.ds(Q * r, Q), D + 1:ROW], h_tok[par][:, 0:Q, :]).then_inc(h_stored[par], 16)
            for i in range(Q):
                sp.dma_start(rows[P:L, bass.ds(Q * r + i, 1), D + 1:ROW],
                             h_tok[par][TP * i:TP * i + TAIL, Q:SLOTS, :]).then_inc(h_stored[par], 16)

        def store_t(sp, r, par):
            rows = rows_dram.rearrange("(i t) c -> t i c", t=L)
            sp.wait_ge(t_made, r + 1)
            sp.wait_ge(gw_made, r + 1)
            sp.dma_start(rows[0:P, bass.ds(Q * r, Q), 0:D + 1], t_tok[par][:, 0:Q, :]).then_inc(t_stored[par], 16)
            for i in range(Q):
                sp.dma_start(rows[P:L, bass.ds(Q * r + i, 1), 0:D + 1],
                             t_tok[par][TP * i:TP * i + TAIL, Q:SLOTS, :]).then_inc(t_stored[par], 16)

        def put_tokens(pool, r):
            last = pool.to_reg(E * CAP - 1)
            pool.wait_ge(token_ready, r + 1)
            pool.sem_inc(token_seen, 1)
            for s in range(SLOTS):
                pool.indirect_dma_start(table_dram, bass.IndirectOffsetOnAxis(where_int[:, s:s + 1], 0),
                                        token_int[:, s:s + 1], None, bounds_check=last,
                                        oob_is_err=False).then_inc(placed, 16)

        def quads(eng, body):
            for q in range(-2, 4):
                body(q, q % 2)
            with eng.Fori(2, nquad // 2 - 2) as k:
                body(2 * k, 0)
                body(2 * k + 1, 1)
            for q in range(nquad - 4, nquad + 3):
                body(q, q % 2)

        def within(v, lo, hi):
            return not isinstance(v, int) or lo <= v < hi

        def tiles_of_experts(dve):
            num = [0]

            def step(ins):
                ins.then_inc(tiles_step, 1)
                num[0] += 1
                dve.wait_ge(tiles_step, num[0])

            over_e = lambda v: v.rearrange("p (o x) -> p o x", o=1).broadcast_to([1, TILES, E])
            over_j = lambda v: v.rearrange("p (j o) -> p j o", o=1).broadcast_to([1, TILES, E])
            dve.wait_ge(region_made, nquad)
            step(nc.vector.tensor_tensor(count[:, :], region[0:1, :], base[:, :], ALU.subtract))
            step(nc.vector.tensor_scalar(count[:, :], count[:, :], float(P - 1), None, ALU.add))
            step(nc.vector.tensor_copy(count_int[:, :], count[:, :]))
            step(nc.vector.tensor_scalar(count_int[:, :], count_int[:, :], 7, None, ALU.logical_shift_right))
            step(nc.vector.tensor_copy(count[:, :], count_int[:, :]))
            step(nc.vector.tensor_tensor_scan(upto[:, :], ones[0:1, 0:E], count[:, :], 0.0, ALU.mult, ALU.add))
            step(nc.vector.tensor_scalar(count[:, :], count[:, :], -float(P), float(CAP), ALU.mult, ALU.add))
            step(nc.vector.tensor_tensor(past[:, :, :], over_j(tile_no[:, :]), over_e(upto[:, :]), ALU.is_ge))
            step(nc.vector.tensor_reduce(of_tile[:, :], past[:, :, :], AX, ALU.add))
            step(nc.vector.tensor_scalar(of_tile[:, :], of_tile[:, :], float(E - 1), None, ALU.min))
            step(nc.vector.tensor_copy(tile_expert[:, :], of_tile[:, :]))
            step(nc.vector.tensor_tensor(past[:, :, :], past[:, :, :], over_e(count[:, :]), ALU.mult))
            step(nc.vector.tensor_reduce(of_tile[:, :], past[:, :, :], AX, ALU.add))
            step(nc.vector.tensor_scalar(tile_no[:, :], tile_no[:, :], float(P), None, ALU.mult))
            step(nc.vector.tensor_tensor(of_tile[:, :], of_tile[:, :], tile_no[:, :], ALU.add))
            step(nc.vector.tensor_copy(tile_start[:, :], of_tile[:, :]))

        ctx.callback(clear, nc, made)
        block = ctx.enter_context(nc.Block())

        @block.sync
        def _(sp):
            def body(q, par):
                if within(q + 3, 0, nquad):
                    load_h(sp, q + 3, 1 - par)
                if within(q - 2, 0, nquad):
                    store_t(sp, q - 2, par)
                if within(q + 2, 0, nquad):
                    store_h(sp, q + 2, par)

            sp.wait_ge(table_in, 16)
            load_h(sp, 0, 0)
            quads(sp, body)
            sp.wait_ge(h_stored[0], 40 * nquad)
            sp.wait_ge(h_stored[1], 40 * nquad)
            sp.wait_ge(t_stored[0], 40 * nquad)
            sp.wait_ge(t_stored[1], 40 * nquad)

        inside = lambda m: within(m, 0, Q * nquad)

        @block.tensor
        def _(pe):
            def body(q, par):
                there = lambda d: within(q + d, 0, nquad)
                for slot in range(Q):
                    m = Q * q + slot
                    if inside(m):
                        scores(pe, m, slot, par, q)
                    if inside(m - 3):
                        with_v(pe, q, m - 3, slot, *((1 - par, q - 1) if slot < 3 else (par, q)))
                    if inside(m - 2):
                        turn_p(pe, q, m - 2, slot)
                    if slot == 0 and there(1):
                        project_qk(pe, q, q + 1)
                    if slot == 0 and there(-2):
                        turn_t(pe, q, q - 2, par)
                    if slot == 1 and there(2):
                        turn_h(pe, q, q + 2, par)
                    if slot == 1 and there(-2):
                        gate(pe, q, q - 2)
                    if slot == 2 and there(-1):
                        output_of_heads(pe, q, q - 1, 1 - par)
                    if slot == 2 and there(-2):
                        ranks(pe, q, q - 2)
                    if slot == 3 and there(1):
                        project_v(pe, q, q + 1)
                    if slot == 3 and there(2):
                        turn_x(pe, q, q + 2, par)

            quads(pe, body)

        @block.scalar
        def _(act):
            def body(q, par):
                there = lambda d: within(q + d, 0, nquad)
                for slot in range(Q):
                    m = Q * q + slot
                    if inside(m - 3):
                        copy_o(act, m - 3, slot, *((1 - par, q - 1) if slot < 3 else (par, q)))
                    if inside(m - 2):
                        copy_pT(act, m - 2, slot)
                    if inside(m):
                        exponentials(act, m, slot)
                    if slot == 2 and there(-2):
                        choice_exp(act, q - 2)
                    if slot == 0 and there(1):
                        copy_qk(act, q + 1, 1 - par)
                    if slot == 0 and there(-2):
                        copy_t(act, q - 2)
                    if slot == 1 and there(2):
                        copy_h(act, q + 2, par)
                    if slot == 2 and there(2):
                        norm_rstd(act, 0, q + 2, agg0, lnv0, rstd0, x_made)
                    if slot == 3 and there(-1):
                        norm_rstd(act, 1, q - 1, agg1, lnv1, rstd1, n_made)
                    if slot == 3 and there(1):
                        copy_v(act, q + 1, 1 - par)
                    if slot == 3 and there(2):
                        copy_x(act, q + 2)

            act.preload_act_table_set(EXP_LN_SET)
            quads(act, body)

        @block.vector
        def _(dve):
            def body(q, par):
                there = lambda d: within(q + d, 0, nquad)
                for slot in range(Q):
                    m = Q * q + slot
                    if slot == 2 and there(-2):
                        choose(dve, q - 2)
                    if slot == 3 and there(-1):
                        add_x(dve, q - 1, 1 - par)
                    if slot == 3 and there(-2):
                        places(dve, q - 2, par)
                    if inside(m):
                        softmax(dve, m, slot)
                    if slot == 2 and there(2):
                        stats_x(dve, q + 2, par)
                    if slot == 3 and there(-1):
                        stats_r(dve, q - 1)
                    if inside(m - 1):
                        denominators(dve, m - 1, (slot - 1) % Q)
                    if slot == 2 and there(2):
                        apply_x(dve, q + 2, par)
                    if slot == 3 and there(-1):
                        apply_r(dve, q - 1)

            quads(dve, body)
            tiles_of_experts(dve)

        @block.gpsimd
        def _(pool):
            def body(q, par):
                there = lambda d: within(q + d, 0, nquad)
                for slot in range(Q):
                    m = Q * q + slot
                    if inside(m + 1):
                        heads_of_k(pool, m + 1, (slot + 1) % Q, *((1 - par, q + 1) if slot == 3 else (par, q)))
                    if slot == 0 and there(-2):
                        gain_and_bias(pool, q - 2, par)
                    if inside(m - 1):
                        weights(pool, m - 1, (slot - 1) % Q)
                    if slot == 0 and there(0):
                        add_bo(pool, q, par)
                    if slot == 1 and there(-3):
                        put_tokens(pool, q - 3)

            pool.wait_ge(table_in, 16)
            quads(pool, body)
            pool.wait_ge(placed, 16 * SLOTS * nquad)


FF = 4 * D
FC = FF // P
RINGT = 8


def dma_semaphores(nc, ctx):
    counts = dict(proj_stored=2, loaded=1, table_in=1, t_stored=2, placed=1, h_in=2, h_stored=2, weights_in=1,
                  place_in=RINGT, row_in=RINGT, out_put=2)
    return {name: [ctx.enter_context(nc.semaphore(f"{name}_{i}")) for i in range(n)] for name, n in counts.items()}


def chosen_experts(nc, prm, ident, rows_dram, table_dram, tile_start, tile_expert, out, dma, tiles=TILES):
    with ExitStack() as ctx:
        sb = lambda n, s, d=F32: ctx.enter_context(nc.sbuf_tensor(n, s, d))
        ps = lambda n, s, d=F32: ctx.enter_context(nc.psum_tensor(n, s, d))
        sems = lambda names: [ctx.enter_context(nc.semaphore("c_" + n)) for n in names.split()]

        w1, b1 = sb("w1", [D, E * FF]), sb("b1", [P, E * FF])
        w2, b2 = sb("w2", [P, E * FC * D]), sb("b2", [P, E * D])
        place = [sb(f"place_c{i}", [P, 1], I32) for i in range(RINGT)]
        target = [sb(f"target{i}", [P, 1], I32) for i in range(RINGT)]
        rows = [sb(f"rows_c{i}", [P, ROW]) for i in range(RINGT)]
        tT = [sb(f"tT_c{i}", [D, P]) for i in range(2)]
        pre = [sb(f"pre{i}", [P, FF]) for i in range(2)]
        hid = [sb(f"hid{i}", [P, FF]) for i in range(2)]
        hidT = [sb(f"hidT{i}", [P, FF]) for i in range(2)]
        ffn = [sb(f"ffn{i}", [P, D]) for i in range(2)]
        res = [sb(f"res_c{i}", [P, D]) for i in range(2)]
        t_ps = [ps(f"t_ps{i}", [P, 512]) for i in range(2)]
        h_ps = [ps(f"h_ps{i}", [P, FF]) for i in range(2)]
        hT_ps = [ps(f"hT_ps{i}", [P, FF]) for i in range(2)]
        o_ps = [ps(f"o_ps{i}", [P, 512]) for i in range(2)]

        weights_in = dma["weights_in"][0]
        cleared, t_turned, tT_made, h_mm, pre_made, hid_made, h_turned, hidT_made, o_mm, ffn_made, res_made, target_made, place_seen, res_seen = sems(
            "cleared t_turned tT_made h_mm pre_made hid_made h_turned hidT_made o_mm ffn_made res_made target_made place_seen res_seen")
        place_in, row_in, out_put = dma["place_in"], dma["row_in"], dma["out_put"]

        def steps(eng, parts):
            def body(s, r):
                for part, delay in parts:
                    j = s - delay
                    if not isinstance(j, int) or 0 <= j < tiles:
                        part(eng, j, (r - delay) % RINGT)
            for s in range(RINGT):
                body(s, s)
            with eng.Fori(1, tiles // RINGT - 1) as k:
                for r in range(RINGT):
                    body(RINGT * k + r, r)
            for s in range(tiles - RINGT, tiles + max(delay for _, delay in parts)):
                body(s, s % RINGT)

        turns = 16 // RINGT

        def load_place(sp, j, r):
            at_least(sp, res_made, j - RINGT + 1)
            at_least(sp, target_made, j - RINGT + 1)
            start = sp.value_load(tile_start[0:1, bass.ds(j, 1)], min_val=0, max_val=TABLE - P)
            sp.dma_start(place[r][:, :], table_dram[bass.ds(start, P), :]).then_inc(place_in[r], 16)

        def gather(pool, j, r):
            last = pool.to_reg(B * L - 1)
            pool.wait_ge(place_in[r], turns * (j - r) + 16)
            pool.sem_inc(place_seen, 1)
            pool.indirect_dma_start(rows[r][:, :], None, rows_dram, bass.IndirectOffsetOnAxis(place[r][:, 0:1], 0),
                                    bounds_check=last, oob_is_err=False).then_inc(row_in[r], 16)

        def keep_target(dve, j, r):
            dve.wait_ge(place_in[r], turns * (j - r) + 16)
            if not isinstance(j, int) or j >= RINGT:
                dve.wait_ge(out_put[r % 2], 8 * (j - RINGT - r % 2) + 16)
            nc.vector.tensor_copy(target[r][:, :], place[r][:, :]).then_inc(target_made, 1)

        def put(pool, j, r):
            last = pool.to_reg(B * L - 1)
            pool.wait_ge(res_made, j + 1)
            pool.sem_inc(res_seen, 1)
            pool.indirect_dma_start(out, bass.IndirectOffsetOnAxis(target[r][:, 0:1], 0), res[r % 2][:, :], None,
                                    bounds_check=last, oob_is_err=False).then_inc(out_put[r % 2], 16)

        def turn_t(pe, j, r):
            pe.wait_ge(row_in[r], turns * (j - r) + 16)
            at_least(pe, tT_made, j - 1)
            pe.transpose(t_ps[r % 2][:, 0:P], rows[r][:, 0:D], ident[:, :]).then_inc(t_turned, 1)

        def copy_t(act, j, r):
            act.wait_ge(t_turned, j + 1)
            at_least(act, h_mm, j - 1)
            nc.scalar.activation(tT[r % 2][:, :], t_ps[r % 2][:, 0:P], ACT.Copy).then_inc(tT_made, 1)

        expert = {}

        def load_expert(pe, j, r):
            expert[r] = pe.value_load(tile_expert[0:1, bass.ds(j, 1)], min_val=0, max_val=E - 1)

        def hidden(pe, j, r):
            e = expert[r]
            pe.wait_ge(tT_made, j + 1)
            at_least(pe, pre_made, j - 1)
            pe.matmul(h_ps[r % 2][:, :], tT[r % 2][:, :], w1[:, bass.ds(e * FF, FF)], start=True, stop=True).then_inc(h_mm, 1)

        def add_b1(dve, j, r):
            e = dve.value_load(tile_expert[0:1, bass.ds(j, 1)], min_val=0, max_val=E - 1)
            dve.wait_ge(h_mm, j + 1)
            at_least(dve, hid_made, j - 1)
            nc.vector.tensor_tensor(pre[r % 2][:, :], h_ps[r % 2][:, :], b1[:, bass.ds(e * FF, FF)], ALU.add).then_inc(pre_made, 1)

        def gelu(act, j, r):
            act.wait_ge(pre_made, j + 1)
            at_least(act, h_turned, j - 1)
            nc.scalar.activation(hid[r % 2][:, :], pre[r % 2][:, :], ACT.Gelu_apprx_tanh).then_inc(hid_made, 1)

        def turn_hidden(pe, j, r):
            pe.wait_ge(hid_made, j + 1)
            at_least(pe, hidT_made, j - 1)
            for c in range(FC):
                ins = pe.transpose(hT_ps[r % 2][:, c * P:(c + 1) * P], hid[r % 2][:, c * P:(c + 1) * P], ident[:, :])
            ins.then_inc(h_turned, 1)

        def copy_hidden(act, j, r):
            act.wait_ge(h_turned, j + 1)
            at_least(act, o_mm, j - 1)
            nc.scalar.activation(hidT[r % 2][:, :], hT_ps[r % 2][:, :], ACT.Copy).then_inc(hidT_made, 1)

        def output(pe, j, r):
            e = expert[r]
            pe.wait_ge(hidT_made, j + 1)
            at_least(pe, ffn_made, j - 1)
            for c in range(FC):
                ins = pe.matmul(o_ps[r % 2][:, 0:D], hidT[r % 2][:, c * P:(c + 1) * P],
                                w2[:, bass.ds(e * (FC * D) + c * D, D)], start=(c == 0), stop=(c == FC - 1))
            ins.then_inc(o_mm, 1)

        def add_b2(dve, j, r):
            e = dve.value_load(tile_expert[0:1, bass.ds(j, 1)], min_val=0, max_val=E - 1)
            dve.wait_ge(o_mm, j + 1)
            at_least(dve, res_made, j - 1)
            nc.vector.tensor_tensor(ffn[r % 2][:, :], o_ps[r % 2][:, 0:D], b2[:, bass.ds(e * D, D)], ALU.add).then_inc(ffn_made, 1)
            dve.wait_ge(ffn_made, j + 1)
            if not isinstance(j, int) or j >= 2:
                dve.wait_ge(out_put[r % 2], 8 * (j - r % 2))
            nc.vector.scalar_tensor_tensor(out=res[r % 2][:, :], in0=ffn[r % 2][:, :], scalar=rows[r][:, D:D + 1],
                                           in1=rows[r][:, D + 1:ROW], op0=ALU.mult, op1=ALU.add).then_inc(res_made, 1)

        block = ctx.enter_context(nc.Block())

        @block.sync
        def _(sp):
            sp.dma_start(w1[:, :].rearrange("d (e f) -> d e f", e=E), prm["W1"].rearrange("e d f -> d e f")).then_inc(weights_in, 16)
            steps(sp, [(load_place, 0)])

        @block.scalar
        def _(act):
            bc = lambda v, n: v.rearrange("e f -> (e f)").rearrange("(o n) -> o n", o=1).broadcast_to([P, n])
            act.dma_start(b1[:, :], bc(prm["b1"], E * FF)).then_inc(weights_in, 16)
            act.dma_start(b2[:, :], bc(prm["b2"], E * D)).then_inc(weights_in, 16)
            act.dma_start(w2[:, :].rearrange("p (e c d) -> p e c d", e=E, c=FC),
                          prm["W2"].rearrange("e (c p) d -> p e c d", p=P)).then_inc(weights_in, 16)
            steps(act, [(copy_t, 3), (gelu, 4), (copy_hidden, 5)])

        @block.gpsimd
        def _(pool):
            pool.wait_ge(cleared, 1)
            steps(pool, [(gather, 1), (put, 7)])
            for i in range(2):
                pool.wait_ge(out_put[i], 8 * tiles)

        @block.tensor
        def _(pe):
            pe.wait_ge(weights_in, 64)
            steps(pe, [(load_expert, 4), (hidden, 4), (load_expert, 6), (turn_hidden, 5), (turn_t, 3), (output, 6)])

        @block.vector
        def _(dve):
            for r in rows:
                ins = nc.vector.memset(r[:, :], 0.0)
            ins.then_inc(cleared, 1)
            dve.wait_ge(weights_in, 64)
            steps(dve, [(keep_target, 2), (add_b1, 4), (add_b2, 6)])


def vit_tower(nc, x, cls_tok, tok_W, tok_b, tok_cls_token, tok_pos_emb, A_log, W_B, b_B, W_C, b_C, W_dt, b_dt, D_skip,
              W_mix, b_mix, ln_g, ln_b, W_dec, b_dec, ln1_g, ln1_b, Wq, bq, Wk, bk, Wv, bv, Wo, bo, gate_W, gate_b,
              W1, b1, W2, b2, out):
    proj_dram = nc.dram_tensor("proj", [D, PW, B, PH], F32).ap()
    h1_dram = nc.dram_tensor("h1", [D, B, L], F32).ap()
    rows_dram = nc.dram_tensor("rows", [B * L, ROW], F32).ap()
    table_dram = nc.dram_tensor("table", [TABLE, 1], I32).ap()
    with ExitStack() as ctx:
        ident = ctx.enter_context(nc.sbuf_tensor("ident", [P, P], F32))
        tile_start = ctx.enter_context(nc.sbuf_tensor("tile_start", [1, TILES], I32))
        tile_expert = ctx.enter_context(nc.sbuf_tensor("tile_expert", [1, TILES], I32))
        identity_ready = ctx.enter_context(nc.semaphore("identity_ready"))
        dma = dma_semaphores(nc, ctx)


        with nc.Block() as block:
            @block.gpsimd
            def _(pool):
                nc.gpsimd.memset(ident[:, :], 0.0).then_inc(identity_ready, 1)
                pool.wait_ge(identity_ready, 1)
                pool.affine_select(out=ident[:, :], in_=ident[:, :], compare_op=ALU.not_equal, fill=1.0, base=0,
                                   pattern=[[-1, P]], channel_multiplier=1).then_inc(identity_ready, 1)

        embed_patches(nc, x, tok_W, identity_ready, ident, proj_dram, dma["proj_stored"])
        ssm_layers(nc, dict(W_B=W_B, W_C=W_C, b_B=b_B, b_C=b_C, A_log=A_log, W_dt=W_dt, W_mix=W_mix, W_dec=W_dec,
                            pos=tok_pos_emb, b_tok=tok_b, b_dec=b_dec, cls0=cls_tok, cls1=tok_cls_token, b_dt=b_dt,
                            b_mix=b_mix, D_skip=D_skip, ln_g=ln_g, ln_b=ln_b), ident, proj_dram, h1_dram)
        attention_and_routing(nc, dict(ln1_g=ln1_g, ln1_b=ln1_b, Wq=Wq, bq=bq, Wk=Wk, bk=bk, Wv=Wv, bv=bv, Wo=Wo, bo=bo,
                                       gate_W=gate_W, gate_b=gate_b), ident, h1_dram, rows_dram, table_dram,
                              tile_start, tile_expert, dma)
        chosen_experts(nc, dict(W1=W1, b1=b1, W2=W2, b2=b2), ident, rows_dram, table_dram, tile_start, tile_expert,
                       out.rearrange("b t d -> (b t) d"), dma)


_INS = ['x', 'cls_tok', 'L0_tok_W', 'L0_tok_b', 'L0_tok_cls_token', 'L0_tok_pos_emb', 'L0_attn_A_log', 'L0_attn_W_B',
        'L0_attn_b_B', 'L0_attn_W_C', 'L0_attn_b_C', 'L0_attn_W_dt', 'L0_attn_b_dt', 'L0_attn_D_skip', 'L0_attn_W_mix',
        'L0_attn_b_mix', 'L0_attn_ln_g', 'L0_attn_ln_b', 'L0_attn_W_dec', 'L0_attn_b_dec', 'L0_ffn_ln1_g', 'L0_ffn_ln1_b',
        'L0_ffn_Wq', 'L0_ffn_bq', 'L0_ffn_Wk', 'L0_ffn_bk', 'L0_ffn_Wv', 'L0_ffn_bv', 'L0_ffn_Wo', 'L0_ffn_bo',
        'L0_ffn_gate_W', 'L0_ffn_gate_b', 'L0_ffn_W1', 'L0_ffn_b1', 'L0_ffn_W2', 'L0_ffn_b2']
_OUTS = [((128, 145, 128), 'float32')]


def kernel(**inputs):
    import numpy as _np
    import concourse.bacc as _bacc
    from concourse import mybir as _mybir
    from concourse.bass_utils import run_bass_kernel_spmd as _run

    nc = _bacc.Bacc("TRN2", target_bir_lowering=False, num_devices=1)
    arrays, args = {}, []
    for name in _INS:
        a = _np.ascontiguousarray(inputs[name])
        arrays[f"in_{name}_dram"] = a
        args.append(nc.dram_tensor(f"in_{name}_dram", a.shape, _mybir.dt.from_np(a.dtype), kind="ExternalInput").ap())
    for i, (shape, dtype) in enumerate(_OUTS):
        dt = _mybir.dt.from_np(_np.dtype(dtype))
        args.append(nc.dram_tensor(f"out_{i}_dram", shape, dt, kind="ExternalOutput").ap())
    vit_tower(nc, *args)
    r = _run(nc, [arrays], core_ids=[0])
    got = tuple(r.results[0][f"out_{i}_dram"] for i in range(len(_OUTS)))
    return got[0]
```
